# Optimizing a Trainium2 kernel written in Bass

```python
import numpy as np
import jax
import jax.numpy as jnp

def _softmax(x, axis=-1):
    return jax.nn.softmax(x, axis=axis)

def _gelu(x):
    return jax.nn.gelu(x, approximate=True)

def _silu(x):
    return jax.nn.silu(x)

def _sigmoid(x):
    return jax.nn.sigmoid(x)

def _layernorm(x, axis=-1, eps=1e-05):
    m = jnp.mean(x, axis=axis, keepdims=True)
    v = jnp.var(x, axis=axis, keepdims=True)
    return (x - m) / jnp.sqrt(v + eps)

def _scatter_add(tgt, idx, src, axis=0):
    return tgt.at[idx].add(src)

def _segment_sum(src, seg, n):
    return jax.ops.segment_sum(src, seg, n)
kernel_name = 'mk_gps_d1_gnn_r8_18a735'

def setup_inputs(seed: int=0):
    np.random.seed(seed)
    _w = jnp.asarray

    def _rec_inputs():
        import jax
        import jax.numpy as jnp
        _gk = jax.random.key(seed)
        x = -0.0003713 + 1 * jax.random.normal(jax.random.fold_in(_gk, 1), (6250, 256), jnp.float32)
        src = jax.random.randint(jax.random.fold_in(_gk, 2), (100000,), 0, 6250, jnp.int32)
        dst = jnp.minimum((6250 * jax.random.uniform(jax.random.fold_in(_gk, 3), (100000,)) ** 2.0).astype(jnp.int32), 49999)
        _o = jnp.argsort(dst, stable=True)
        src = src[_o]
        dst = dst[_o]
        return (x, src, dst)
    x, src, dst = _rec_inputs()

    def _L0_gnn_setup():
        import jax, jax.numpy as jnp
        import numpy as np
        N = 6250
        E = 50000
        IN_DIM = 256
        H = 8
        D = 32
        LN_EPS = 1e-05
        key = jax.random.key(seed)
        k_x, k_e, k_w, k_a = jax.random.split(key, 4)
        x = jax.random.normal(k_x, (N, IN_DIM), dtype=jnp.float32)
        edge_index = jax.random.randint(k_e, (2, E), 0, N, dtype=jnp.int32)
        w_lim = np.sqrt(6.0 / (IN_DIM + H * D)) * np.sqrt(2.0)
        W = jax.random.uniform(k_w, (IN_DIM, H * D), minval=-w_lim, maxval=w_lim, dtype=jnp.float32)
        a_lim = np.sqrt(6.0 / (2 * D + 1))
        k_as, k_ad = jax.random.split(k_a)
        a_src = jnp.broadcast_to(jax.random.uniform(k_as, (1, D), minval=-a_lim, maxval=a_lim, dtype=jnp.float32), (H, D)).copy()
        a_dst = jnp.broadcast_to(jax.random.uniform(k_ad, (1, D), minval=-a_lim, maxval=a_lim, dtype=jnp.float32), (H, D)).copy()
        gamma = jnp.ones((H * D,), dtype=jnp.float32)
        beta = jnp.zeros((H * D,), dtype=jnp.float32)
        return {'x': x, 'edge_index': edge_index, 'W': W, 'a_src': a_src, 'a_dst': a_dst, 'gamma': gamma, 'beta': beta}
    _L0_gnn_all = _L0_gnn_setup()
    _L0_gnn_in = {k: v for k, v in _L0_gnn_all.items() if k in ('W', 'a_src', 'a_dst', 'gamma', 'beta')}
    del _L0_gnn_all

    def _L0_mix_setup():
        import jax, jax.numpy as jnp
        import numpy as np
        C_CURV = 1.0
        MIN_NORM = 1e-15
        BALL_EPS = 1e-05
        ATT_EPS = 1e-15
        DIM = 32

        def _norm(x):
            return jnp.clip(jnp.linalg.norm(x, axis=-1, keepdims=True), MIN_NORM)

        def proj(x, c):
            maxnorm = (1.0 - BALL_EPS) / jnp.sqrt(c)
            n = _norm(x)
            return jnp.where(n > maxnorm, x / n * maxnorm, x)

        def expmap0(u, c):
            sc = jnp.sqrt(c)
            n = _norm(u)
            return jnp.tanh(sc * n) * u / (sc * n)

        def logmap0(p, c):
            sc = jnp.sqrt(c)
            n = _norm(p)
            return jnp.arctanh(jnp.clip(sc * n, -1.0 + 1e-07, 1.0 - 1e-07)) * p / (sc * n)

        def mobius_add(x, y, c):
            x2 = jnp.sum(x * x, -1, keepdims=True)
            y2 = jnp.sum(y * y, -1, keepdims=True)
            xy = jnp.sum(x * y, -1, keepdims=True)
            num = (1 + 2 * c * xy + c * y2) * x + (1 - c * x2) * y
            den = 1 + 2 * c * xy + c * c * x2 * y2
            return num / jnp.clip(den, MIN_NORM)

        def conv1d(x, w, pad, groups=1):
            return jax.lax.conv_general_dilated(x, w, (1,), [(pad, pad)], dimension_numbers=('NCH', 'OIH', 'NCH'), feature_group_count=groups)

        def batchnorm(x, gamma, beta):
            mean = jnp.mean(x, axis=(0, 2), keepdims=True)
            var = jnp.var(x, axis=(0, 2), keepdims=True)
            xn = (x - mean) * jax.lax.rsqrt(var + 1e-05)
            return gamma[None, :, None] * xn + beta[None, :, None]

        def _reference_tuple_inner(x, w_qkv, bn_gamma, bn_beta, w_dw, w_pw, w_res, b_res):
            c = C_CURV
            h = logmap0(proj(x, c), c)
            h = jnp.transpose(h, (1, 2, 0))
            h = conv1d(h, w_qkv, pad=2)
            h = batchnorm(h, bn_gamma, bn_beta)
            h = jax.nn.relu(jnp.transpose(h, (2, 0, 1)))
            qkv = proj(expmap0(h, c), c)
            t = jnp.transpose(logmap0(proj(qkv, c), c), (1, 2, 0))
            s = conv1d(t, w_dw, pad=2, groups=t.shape[1])
            s = conv1d(s, w_pw, pad=0, groups=t.shape[1] // DIM)
            cat = jnp.concatenate([t, s], axis=1)
            ai = proj(expmap0(jnp.transpose(cat, (2, 0, 1)), c), c)
            t2 = logmap0(proj(ai, c), c)
            L, N, C2 = t2.shape
            g = C2 // (3 * DIM)
            qkv3 = jnp.transpose(t2, (1, 2, 0)).reshape(N, g, 3 * DIM, L)
            q, k, v = jnp.split(qkv3, 3, axis=2)
            q = jax.nn.relu(q)
            k = jax.nn.relu(k)
            vk = jnp.einsum('ngdl,ngel->ngde', v, k)
            out = jnp.einsum('ngde,ngdl->ngdl', vk, q)
            out = out / (jnp.sum(v, -1, keepdims=True) + ATT_EPS)
            out = jnp.transpose(out.reshape(N, g * DIM, L), (2, 0, 1))
            fx_h = proj(expmap0(out, c), c)
            ft = jnp.transpose(logmap0(proj(fx_h, c), c), (1, 2, 0))
            ft = conv1d(ft, w_res, pad=0) + b_res[None, :, None]
            fx = proj(expmap0(jnp.transpose(ft, (2, 0, 1)), c), c)
            residual = mobius_add(fx, x, c)
            return (fx, residual)
        key = jax.random.key(seed)
        ks = jax.random.split(key, 6)
        L, N, C, TD = (256, 16, 256, 256)
        x = jax.random.normal(ks[0], (L, N, C), jnp.float32) * 0.05
        w_qkv = jax.random.normal(ks[1], (3 * TD, C, 5), jnp.float32) / np.sqrt(C * 5)
        bn_gamma = jnp.ones((3 * TD,), jnp.float32)
        bn_beta = jnp.zeros((3 * TD,), jnp.float32)
        w_dw = jax.random.normal(ks[2], (3 * TD, 1, 5), jnp.float32) / np.sqrt(5.0)
        w_pw = jax.random.normal(ks[3], (3 * TD, DIM, 1), jnp.float32) / np.sqrt(DIM)
        w_res = jax.random.normal(ks[4], (C, 2 * TD, 1), jnp.float32) / np.sqrt(2 * TD)
        b_res = jnp.zeros((C,), jnp.float32)
        return {'x': x, 'w_qkv': w_qkv, 'bn_gamma': bn_gamma, 'bn_beta': bn_beta, 'w_dw': w_dw, 'w_pw': w_pw, 'w_res': w_res, 'b_res': b_res}
    _L0_mix_all = _L0_mix_setup()
    _L0_mix_in = {k: v for k, v in _L0_mix_all.items() if k in ('w_qkv', 'bn_gamma', 'bn_beta', 'w_dw', 'w_pw', 'w_res', 'b_res')}
    del _L0_mix_all

    def _L0_ffn_setup():
        import jax, jax.numpy as jnp
        import numpy as np
        B, S, D = (8, 512, 256)
        H = 4 * D
        CAPACITY = 0.5
        key = jax.random.key(seed)
        ks = jax.random.split(key, 6)
        x = jax.random.normal(ks[0], (B, S, D), dtype=jnp.float32)
        attention_mask = jnp.zeros((B, 1, 1, S), dtype=jnp.float32)
        wr = jax.random.normal(ks[1], (D, 1), dtype=jnp.float32) * 0.02
        br = jnp.zeros((1,), dtype=jnp.float32)
        w1 = jax.random.normal(ks[2], (D, H), dtype=jnp.float32) * 0.02
        b1 = jnp.zeros((H,), dtype=jnp.float32)
        w2 = jax.random.normal(ks[3], (H, D), dtype=jnp.float32) * 0.02
        b2 = jnp.zeros((D,), dtype=jnp.float32)
        return {'x': x, 'attention_mask': attention_mask, 'wr': wr, 'br': br, 'w1': w1, 'b1': b1, 'w2': w2, 'b2': b2}
    _L0_ffn_all = _L0_ffn_setup()
    _L0_ffn_in = {k: v for k, v in _L0_ffn_all.items() if k in ('attention_mask', 'wr', 'br', 'w1', 'b1', 'w2', 'b2')}
    del _L0_ffn_all
    return {'x': x, 'src': src, 'dst': dst, 'L0_gnn_W': _L0_gnn_in['W'], 'L0_gnn_a_src': _L0_gnn_in['a_src'], 'L0_gnn_a_dst': _L0_gnn_in['a_dst'], 'L0_gnn_gamma': _L0_gnn_in['gamma'], 'L0_gnn_beta': _L0_gnn_in['beta'], 'L0_mix_w_qkv': _L0_mix_in['w_qkv'], 'L0_mix_bn_gamma': _L0_mix_in['bn_gamma'], 'L0_mix_bn_beta': _L0_mix_in['bn_beta'], 'L0_mix_w_dw': _L0_mix_in['w_dw'], 'L0_mix_w_pw': _L0_mix_in['w_pw'], 'L0_mix_w_res': _L0_mix_in['w_res'], 'L0_mix_b_res': _L0_mix_in['b_res'], 'L0_ffn_attention_mask': _L0_ffn_in['attention_mask'], 'L0_ffn_wr': _L0_ffn_in['wr'], 'L0_ffn_br': _L0_ffn_in['br'], 'L0_ffn_w1': _L0_ffn_in['w1'], 'L0_ffn_b1': _L0_ffn_in['b1'], 'L0_ffn_w2': _L0_ffn_in['w2'], 'L0_ffn_b2': _L0_ffn_in['b2']}

def reference(x, src, dst, L0_gnn_W, L0_gnn_a_src, L0_gnn_a_dst, L0_gnn_gamma, L0_gnn_beta, L0_mix_w_qkv, L0_mix_bn_gamma, L0_mix_bn_beta, L0_mix_w_dw, L0_mix_w_pw, L0_mix_w_res, L0_mix_b_res, L0_ffn_attention_mask, L0_ffn_wr, L0_ffn_br, L0_ffn_w1, L0_ffn_b1, L0_ffn_w2, L0_ffn_b2):
    import jax
    import jax.numpy as jnp

    def _L0_gnn_ref(x, edge_index, W, a_src, a_dst, gamma, beta):
        import jax, jax.numpy as jnp
        import numpy as np
        N = 6250
        E = 50000
        IN_DIM = 256
        H = 8
        D = 32
        LN_EPS = 1e-05
        n = x.shape[0]
        src, dst = (edge_index[0], edge_index[1])
        hh = (x @ W).reshape(n, H, D)
        s_src = jnp.einsum('nhd,hd->nh', hh, a_src)
        s_dst = jnp.einsum('nhd,hd->nh', hh, a_dst)
        scores = jax.nn.leaky_relu(s_src[src] + s_dst[dst], negative_slope=0.2)
        m = jax.ops.segment_max(scores, dst, num_segments=n)
        e = jnp.exp(scores - m[dst])
        denom = jax.ops.segment_sum(e, dst, num_segments=n)
        alpha = e / denom[dst]
        msgs = hh[src] * alpha[:, :, None]
        out = jax.ops.segment_sum(msgs, dst, num_segments=n).reshape(n, H * D)
        out = out + x
        mu = jnp.mean(out, axis=-1, keepdims=True)
        var = jnp.mean(jnp.square(out - mu), axis=-1, keepdims=True)
        out = (out - mu) / jnp.sqrt(var + LN_EPS) * gamma + beta
        return jax.nn.elu(out)

    def _L0_mix_ref(x, w_qkv, bn_gamma, bn_beta, w_dw, w_pw, w_res, b_res):
        import jax, jax.numpy as jnp
        import numpy as np
        C_CURV = 1.0
        MIN_NORM = 1e-15
        BALL_EPS = 1e-05
        ATT_EPS = 1e-15
        DIM = 32

        def _norm(x):
            return jnp.clip(jnp.linalg.norm(x, axis=-1, keepdims=True), MIN_NORM)

        def proj(x, c):
            maxnorm = (1.0 - BALL_EPS) / jnp.sqrt(c)
            n = _norm(x)
            return jnp.where(n > maxnorm, x / n * maxnorm, x)

        def expmap0(u, c):
            sc = jnp.sqrt(c)
            n = _norm(u)
            return jnp.tanh(sc * n) * u / (sc * n)

        def logmap0(p, c):
            sc = jnp.sqrt(c)
            n = _norm(p)
            return jnp.arctanh(jnp.clip(sc * n, -1.0 + 1e-07, 1.0 - 1e-07)) * p / (sc * n)

        def mobius_add(x, y, c):
            x2 = jnp.sum(x * x, -1, keepdims=True)
            y2 = jnp.sum(y * y, -1, keepdims=True)
            xy = jnp.sum(x * y, -1, keepdims=True)
            num = (1 + 2 * c * xy + c * y2) * x + (1 - c * x2) * y
            den = 1 + 2 * c * xy + c * c * x2 * y2
            return num / jnp.clip(den, MIN_NORM)

        def conv1d(x, w, pad, groups=1):
            return jax.lax.conv_general_dilated(x, w, (1,), [(pad, pad)], dimension_numbers=('NCH', 'OIH', 'NCH'), feature_group_count=groups)

        def batchnorm(x, gamma, beta):
            mean = jnp.mean(x, axis=(0, 2), keepdims=True)
            var = jnp.var(x, axis=(0, 2), keepdims=True)
            xn = (x - mean) * jax.lax.rsqrt(var + 1e-05)
            return gamma[None, :, None] * xn + beta[None, :, None]

        def _reference_tuple_inner(x, w_qkv, bn_gamma, bn_beta, w_dw, w_pw, w_res, b_res):
            c = C_CURV
            h = logmap0(proj(x, c), c)
            h = jnp.transpose(h, (1, 2, 0))
            h = conv1d(h, w_qkv, pad=2)
            h = batchnorm(h, bn_gamma, bn_beta)
            h = jax.nn.relu(jnp.transpose(h, (2, 0, 1)))
            qkv = proj(expmap0(h, c), c)
            t = jnp.transpose(logmap0(proj(qkv, c), c), (1, 2, 0))
            s = conv1d(t, w_dw, pad=2, groups=t.shape[1])
            s = conv1d(s, w_pw, pad=0, groups=t.shape[1] // DIM)
            cat = jnp.concatenate([t, s], axis=1)
            ai = proj(expmap0(jnp.transpose(cat, (2, 0, 1)), c), c)
            t2 = logmap0(proj(ai, c), c)
            L, N, C2 = t2.shape
            g = C2 // (3 * DIM)
            qkv3 = jnp.transpose(t2, (1, 2, 0)).reshape(N, g, 3 * DIM, L)
            q, k, v = jnp.split(qkv3, 3, axis=2)
            q = jax.nn.relu(q)
            k = jax.nn.relu(k)
            vk = jnp.einsum('ngdl,ngel->ngde', v, k)
            out = jnp.einsum('ngde,ngdl->ngdl', vk, q)
            out = out / (jnp.sum(v, -1, keepdims=True) + ATT_EPS)
            out = jnp.transpose(out.reshape(N, g * DIM, L), (2, 0, 1))
            fx_h = proj(expmap0(out, c), c)
            ft = jnp.transpose(logmap0(proj(fx_h, c), c), (1, 2, 0))
            ft = conv1d(ft, w_res, pad=0) + b_res[None, :, None]
            fx = proj(expmap0(jnp.transpose(ft, (2, 0, 1)), c), c)
            residual = mobius_add(fx, x, c)
            return (fx, residual)
        return _reference_tuple_inner(x, w_qkv, bn_gamma, bn_beta, w_dw, w_pw, w_res, b_res)[0]

    def _L0_ffn_ref(x, attention_mask, wr, br, w1, b1, w2, b2):
        import jax, jax.numpy as jnp
        import numpy as np
        B, S, D = (8, 512, 256)
        H = 4 * D
        CAPACITY = 0.5
        b, s, d = x.shape
        weights = (jnp.einsum('bsd,do->bso', x, wr) + br)[..., 0]
        k = max(1, int(CAPACITY * s))
        kk = k - 1 if k > 1 else 1
        _, idx = jax.lax.top_k(weights, k)
        sel_idx = idx[:, :kk]
        sel = jnp.take_along_axis(x, sel_idx[:, :, None], axis=1)
        h = jax.nn.gelu(jnp.einsum('bkd,dh->bkh', sel, w1) + b1)
        y = jnp.einsum('bkh,hd->bkd', h, w2) + b2
        w_sel = jnp.take_along_axis(weights, sel_idx, axis=1)
        y = y * w_sel[..., None]
        batch_idx = jnp.arange(b)[:, None]
        processed = jnp.zeros_like(x).at[batch_idx, sel_idx].set(y)
        return processed + x
    edge_index = jnp.stack([src, dst])
    xn = _layernorm(x, axis=-1)
    x = x + _L0_gnn_ref(xn, edge_index, L0_gnn_W, L0_gnn_a_src, L0_gnn_a_dst, L0_gnn_gamma, L0_gnn_beta) + _L0_mix_ref(xn[None], L0_mix_w_qkv, L0_mix_bn_gamma, L0_mix_bn_beta, L0_mix_w_dw, L0_mix_w_pw, L0_mix_w_res, L0_mix_b_res)[0]
    x = x + _L0_ffn_ref(_layernorm(x, axis=-1)[None], L0_ffn_attention_mask, L0_ffn_wr, L0_ffn_br, L0_ffn_w1, L0_ffn_b1, L0_ffn_w2, L0_ffn_b2)[0]
    return x

_drawn_inputs = setup_inputs


def setup_inputs(seed=0):
    import zlib

    import numpy as np

    out = dict(_drawn_inputs(seed))
    spreads = {'L0_gnn_gamma': (1.0, 0.2),
     'L0_gnn_beta': (0.0, 0.1),
     'L0_mix_bn_gamma': (1.0, 0.6),
     'L0_mix_bn_beta': (0.0, 2.0),
     'L0_mix_b_res': (0.0, 0.626),
     'L0_ffn_b1': (0.0, 0.8),
     'L0_ffn_b2': (0.0, 0.8)}
    factors = {'L0_mix_w_dw': 29.187,
     'L0_mix_w_pw': 27.59,
     'L0_ffn_wr': 5.096,
     'L0_ffn_w1': 6.542,
     'L0_ffn_w2': 6.113,
     'L0_mix_w_qkv': 4.035,
     'L0_mix_w_res': 3.267}
    for name, (base, spread) in spreads.items():
        noise = np.random.default_rng([zlib.crc32(name.encode()), seed]).standard_normal(out[name].shape)
        drawn = base * np.exp(spread * noise) if base else spread * noise
        out[name] = jnp.asarray(drawn.astype(out[name].dtype))
    for name, factor in factors.items():
        out[name] = (out[name] * factor).astype(out[name].dtype)
    return out
```

```python
from contextlib import ExitStack

import numpy as np

import concourse.bass as bass
from concourse import mybir

F32 = mybir.dt.float32
I32 = mybir.dt.int32
ALU = mybir.AluOpType
ACT = mybir.ActivationFunctionType

P = 128
N = 6250
D = 256
KD = D // P
E = 100000
H = 8
HD = D // H
ROW = HD + 1
TAB = H * ROW
NT = -(-N // P)
BLK = 4
NB = -(-NT // BLK)
NTP = NB * BLK
ET = -(-E // (16 * P)) * 16
EG = 16
NG = ET // EG
VT = ET + NT - 1
VG = VT // EG
CH = VT * P // 16
NQ = 3 * D
QC = NQ // P
HF = 4 * D
HC = HF // P
PAD_DST = 1000000
BIG = 1.0e30
MAXN = float(np.float32(1.0 - 1e-5))
CAP = float(np.arctanh(np.float64(MAXN)))
MINN = 1e-15
KSEL = N // 2 - 1

assert VT % EG == 0 and VT == 832 and NTP * P == 512 * NB


class Count:

    def __init__(self, sem, per, by=1):
        self.sem, self.per, self.by = sem, per, by

    def wait(self, eng, i, c):
        eng.wait_ge(self.sem, (i * self.per + c) * self.by)

    def wait_before(self, eng, i, c):
        if not (isinstance(i, int) and i == 0):
            eng.wait_ge(self.sem, ((i - 1) * self.per + c) * self.by)


class Chain:

    def __init__(self, eng, sem):
        self.eng, self.sem, self.base, self.k = eng, sem, 0, 0

    def turn(self, i, per):
        self.base, self.k = self.start + i * per, 0

    def loop(self):
        self.start, self.base, self.k = self.base + self.k, self.base + self.k, 0

    def end(self, turns, per):
        assert self.k == per, (self.k, per)
        self.base, self.k = self.start + turns * per, 0

    def step(self, ins):
        ins.then_inc(self.sem, 1)
        self.k += 1

    def done(self):
        self.eng.wait_ge(self.sem, self.base + self.k)

    def do(self, ins):
        self.step(ins)
        self.done()


def turns(eng, n, body):
    body(0)
    if n > 1:
        with eng.Fori(1, n) as i:
            body(i)


def build(nc, A, out):
    with ExitStack() as ctx:
        def sb(name, shape, dt=F32):
            return ctx.enter_context(nc.sbuf_tensor(name, shape, dt))

        def sem(name):
            return ctx.enter_context(nc.semaphore(name))

        def dram(name, shape, dt=F32):
            return nc.dram_tensor(name, shape, dt).ap()

        table_d = dram("table_d", [NTP * P, TAB])
        ssrc_d = dram("ssrc_d", [NTP * P, H])
        xn_d = dram("xn_d", [NTP, P, D])
        fx_d = dram("fx_d", [NTP, P, D])
        sat_d = dram("sat_d", [H, VT, P])
        et_d = dram("et_d", [H, VT, P])

        pb = [ctx.enter_context(nc.psum_tensor(f"bank{i}", [P, 512], F32)) for i in range(8)]

        ident = sb("ident", [P, P])
        ones = sb("ones", [P, P])
        iota_f = sb("iota_f", [P, P])
        pcol = sb("pcol", [P, 2])
        src_sb = sb("src_sb", [P, VT + 2 * EG], I32)
        dst_f = sb("dst_f", [P, VT])
        nt_f = sb("nt_f", [P, VT])
        nodecol = sb("nodecol", [P, VT])
        nt_pack = sb("nt_pack", [1, VT // 4], I32)
        tau_i = sb("tau_i", [1, NT - 1], I32)
        never = sb("never", [P, NT - 1])
        sc = sb("sc", [P, 12, NTP])
        sd_nodes = sb("sd_nodes", [P, NTP, H])
        E_all = sb("E_all", [P, VT, H])
        idx = sb("idx", [P, 4, EG], I32)
        grab = sb("grab", [P, 4, EG, H])

        r1 = sb("r1", [P, NTP * D + 8])
        r2 = sb("r2", [P, CH + 8])
        r3 = sb("r3", [P, 14100])
        r4 = sb("r4", [P, 4640])
        xn = r1[:, 0:NTP * D].rearrange("p (t d) -> p t d", d=D)
        sde = r2[:, 0:CH].rearrange("p (t h) -> p t h", h=H)

        class Area:
            def __init__(self, region):
                self.region, self.at = region, 0

            def take(self, *shape, dt=F32):
                n = int(np.prod(shape))
                v = self.region[:, self.at:self.at + n]
                self.at += n
                if dt != F32:
                    v = v.bitcast(dt)
                if len(shape) == 2:
                    v = v.rearrange("p (a b) -> p a b", b=shape[1])
                elif len(shape) == 3:
                    v = v.rearrange("p (a b c) -> p a b c", b=shape[1], c=shape[2])
                return v

        prologue(nc, ctx, sem, locals())
        edges_and_mix(nc, ctx, sem, locals())
        combine_and_ffn(nc, ctx, sem, locals(), out)


def prologue(nc, ctx, sem, L):
    A, pb, ident, ones, xn, sc = L["A"], L["pb"], L["ident"], L["ones"], L["xn"], L["sc"]
    iota_f, pcol, dst_f, nt_f, nodecol = (L[k] for k in ("iota_f", "pcol", "dst_f", "nt_f", "nodecol"))
    area = L["Area"](L["r3"])
    W_sb = area.take(KD, D + 2 * H)
    a_sb = area.take(2, D)
    wa_tmp = area.take(D)
    xr = area.take(2, D)
    xnT = area.take(2, D)
    trow = area.take(2, TAB)
    srow = area.take(2, H)
    junk = area.take(2, D)
    stats = area.take(NTP, 6)
    first_i = area.take(ET, dt=I32)
    cmp = area.take(ET)
    dst_i = area.take(VT, dt=I32)
    iota_i = area.take(P, dt=I32)
    pcol_i = area.take(1, dt=I32)
    cnt = area.take(1)
    cntd = area.take(NT - 1)
    pack_f = area.take(VT // 4)
    tau_f = area.take(NT - 1)

    x_in = [sem(f"x_in{j}") for j in range(4)]
    w_in, edge_in = sem("w_in"), sem("edge_in")
    const_set, iota_set = sem("const_set"), sem("iota_set")
    dve_pro = sem("dve_pro")
    var_ready, std_ready = sem("var_ready"), sem("std_ready")
    xn_ready = sem("xn_ready")
    wa_ready = sem("wa_ready")
    xT_ready, xT_out = Count(sem("xT_ready"), 2), Count(sem("xT_out"), 2)
    proj_ready, proj_out = Count(sem("proj_ready"), 2), Count(sem("proj_out"), 2)
    stored = [Count(sem(f"row_stored{u}"), 2, 16) for u in range(2)]
    xn_stored = sem("xn_stored")
    squares, xr_ready = Count(sem("squares"), 2), Count(sem("xr_ready"), 2)
    cnt_ready, cnt_bc = sem("cnt_ready"), sem("cnt_bc")
    TURNS = NTP // 2
    XT = NTP // 4

    with nc.Block() as block:
        @block.sync
        def _(sp):
            for j in range(4):
                sp.dma_start(xn[:, j * XT:(j + 1) * XT, :],
                             A["x"].rearrange("(t p) d -> p t d", p=P)[:, j * XT:(j + 1) * XT, :]).then_inc(x_in[j], 16)
            sp.dma_start(W_sb[:, :, 0:D], A["W"].rearrange("(k p) n -> p k n", p=P)).then_inc(w_in, 16)
            for j, name in enumerate(("a_src", "a_dst")):
                sp.dma_start(a_sb[:, j, :], A[name].to_broadcast([P, D])).then_inc(w_in, 16)
            sp.dma_start(first_i, A["first"].to_broadcast([P, ET])).then_inc(edge_in, 16)
            sp.dma_start(dst_i, A["dst_cols"]).then_inc(edge_in, 16)
            sp.dma_start(L["src_sb"][:, :], A["src_cols"]).then_inc(edge_in, 16)

            def body(i):
                for u in range(2):
                    t = 2 * i + u
                    proj_out.wait(sp, i, u + 1)
                    sp.dma_start(L["table_d"][bass.ds(t * P, P), :], trow[:, u, :]).then_inc(stored[u].sem, 16)
                    sp.dma_start(L["ssrc_d"][bass.ds(t * P, P), :], srow[:, u, :]).then_inc(stored[u].sem, 16)
            turns(sp, TURNS, body)
            sp.wait_ge(xn_ready, NTP)
            sp.dma_start(L["xn_d"].rearrange("t p d -> p t d"), xn).then_inc(xn_stored, 16)
            sp.wait_ge(xn_stored, 16)
            for u in range(2):
                sp.wait_ge(stored[u].sem, TURNS * 32)

        @block.gpsimd
        def _(g):
            nc.gpsimd.memset(ones[:, :], 1.0).then_inc(const_set, 1)
            nc.gpsimd.memset(ident[:, :], 0.0).then_inc(const_set, 1)
            g.wait_ge(const_set, 2)
            nc.gpsimd.affine_select(out=ident[:, :], in_=ident[:, :], compare_op=ALU.not_equal, fill=1.0, base=0,
                                    pattern=[[-1, P]], channel_multiplier=1).then_inc(const_set, 1)
            nc.gpsimd.iota(iota_i, pattern=[[1, P]], base=0, channel_multiplier=0).then_inc(iota_set, 1)
            nc.gpsimd.iota(pcol_i, pattern=[[0, 1]], base=0, channel_multiplier=1).then_inc(iota_set, 1)

        @block.vector
        def _(v):
            ch = Chain(v, dve_pro)
            v.wait_ge(w_in, 48)
            for k in range(KD):
                for j in range(2):
                    ch.do(nc.vector.tensor_tensor(wa_tmp, W_sb[:, k, 0:D], a_sb[:, j, :], ALU.mult))
                    ins = nc.vector.reduce_sum(W_sb[:, k, D + H * j:D + H * (j + 1)],
                                               wa_tmp.rearrange("p (h d) -> p h d", h=H), mybir.AxisListType.X)
                    ch.do(ins)
            nc.vector.memset(trow[:, :, :], 1.0).then_inc(wa_ready, 1)
            for j in range(4):
                v.wait_ge(x_in[j], 16)
            ch.loop()
            with v.Fori(0, NTP // 4) as i:
                ch.turn(i, 4)
                for u in range(4):
                    t = 4 * i + u
                    ch.step(nc.vector.bn_stats(stats[:, bass.ds(t, 1), :], xn[:, bass.ds(t, 1), :]))
            ch.end(NTP // 4, 4)
            ch.done()
            row_moments(nc, ch, stats, sc)
            nc.vector.tensor_scalar(sc[:, 3, :], sc[:, 3, :], 1e-5, None, ALU.add).then_inc(var_ready, 1)
            v.wait_ge(std_ready, 1)
            ch.do(nc.vector.reciprocal(sc[:, 3, :], sc[:, 4, :]))
            with v.Fori(0, NTP // 4) as i:
                for u in range(4):
                    t = 4 * i + u
                    nc.vector.tensor_scalar(xn[:, bass.ds(t, 1), :], xn[:, bass.ds(t, 1), :], sc[:, 2, bass.ds(t, 1)],
                                            sc[:, 3, bass.ds(t, 1)], ALU.subtract, ALU.mult).then_inc(xn_ready, 1)

            def body(i):
                for u in range(2):
                    t = 2 * i + u
                    proj_ready.wait(v, i, u + 1)
                    stored[u].wait_before(v, i, 2)
                    q = pb[2 + u]
                    nc.vector.tensor_copy(trow[:, u, :].rearrange("p (h r) -> p h r", r=ROW)[:, :, 0:HD],
                                          q[:, 0:D].rearrange("p (h d) -> p h d", h=H))
                    nc.vector.tensor_copy(L["sd_nodes"][:, bass.ds(t, 1), :],
                                          q[:, D + H:D + 2 * H].rearrange("p (o h) -> p o h", o=1))
                    nc.vector.tensor_copy(srow[:, u, :], q[:, D:D + H]).then_inc(proj_out.sem, 1)
            turns(v, TURNS, body)

            v.wait_ge(edge_in, 48)
            v.wait_ge(iota_set, 2)
            v.wait_ge(const_set, 3)
            ch.do(nc.vector.tensor_single_scalar(first_i, first_i, 7, op=ALU.arith_shift_right))
            ch.step(nc.vector.tensor_copy(iota_f[:, :], iota_i))
            ch.step(nc.vector.tensor_copy(pcol[:, 0:1], pcol_i))
            ch.do(nc.vector.tensor_scalar(nt_f[:, 0:ET], first_i, float(NT - 1), None, ALU.min))
            ch.step(nc.vector.tensor_copy(nt_f[:, ET:VT], iota_f[:, 1:NT]))
            ch.step(nc.vector.tensor_copy(dst_f[:, :], dst_i))
            ch.do(nc.vector.tensor_scalar(pcol[:, 1:2], pcol[:, 0:1], 1.0, None, ALU.add))
            ch.do(nc.vector.tensor_scalar(cmp, nt_f[:, 0:ET], pcol[:, 1:2], None, ALU.is_lt))
            ch.do(nc.vector.reduce_sum(cnt, cmp, mybir.AxisListType.X))
            nc.vector.tensor_scalar(cntd, ident[:, 0:NT - 1], cnt, None, ALU.mult).then_inc(cnt_ready, 1)
            v.wait_ge(cnt_bc, 1)
            ch.do(nc.vector.tensor_scalar(L["never"][:, :], pb[4][:, 0:NT - 1], 0.5, 1.0e7,
                                          ALU.is_lt, ALU.mult))
            ch.do(nc.vector.tensor_scalar(tau_f, pb[4][:, 0:NT - 1], -1.0, 0.0, ALU.add, ALU.max))
            ch.step(nc.vector.tensor_copy(L["tau_i"][0:1, :], tau_f[0:1, :]))
            ch.do(nc.vector.tensor_scalar(nodecol[:, :], nt_f[:, :], float(P), pcol[:, 0:1], ALU.mult, ALU.add))
            ch.do(nc.vector.tensor_tensor(nodecol[:, ET:VT], nodecol[:, ET:VT], L["never"][:, :], ALU.add))
            four = nt_f[0:1, :].rearrange("p (k j) -> p k j", j=4)
            ch.do(nc.vector.tensor_scalar(pack_f[0:1, :], four[:, :, 3], float(NT), None, ALU.mult))
            for j in (2, 1):
                ch.do(nc.vector.tensor_tensor(pack_f[0:1, :], pack_f[0:1, :], four[:, :, j], ALU.add))
                ch.do(nc.vector.tensor_scalar(pack_f[0:1, :], pack_f[0:1, :], float(NT), None, ALU.mult))
            ch.do(nc.vector.tensor_tensor(pack_f[0:1, :], pack_f[0:1, :], four[:, :, 0], ALU.add))
            ch.do(nc.vector.tensor_copy(L["nt_pack"][0:1, :], pack_f[0:1, :]))
            v.wait_ge(squares.sem, NTP)

        @block.scalar
        def _(s):
            s.wait_ge(var_ready, 1)
            nc.scalar.activation(sc[:, 4, :], sc[:, 3, :], ACT.Sqrt).then_inc(std_ready, 1)

            def body(i):
                for u in range(2):
                    t = 2 * i + u
                    s.wait_ge(xn_ready, t + 1)
                    xT_ready.wait_before(s, i, u + 1)
                    squares.wait_before(s, i, u + 1)
                    nc.scalar.activation(xr[:, u, :], xn[:, bass.ds(t, 1), :].rearrange("p o d -> p (o d)"),
                                         ACT.Copy).then_inc(xr_ready.sem, 1)
                for u in range(2):
                    t = 2 * i + u
                    xr_ready.wait(s, i, u + 1)
                    nc.scalar.activation(junk[:, u, :], xr[:, u, :], ACT.Square,
                                         accum_out=sc[:, 0, bass.ds(t, 1)]).then_inc(squares.sem, 1)
                for u in range(2):
                    xT_ready.wait(s, i, u + 1)
                    proj_ready.wait_before(s, i, u + 1)
                    nc.scalar.activation(xnT[:, u, :], pb[u][:, 0:D], ACT.Copy).then_inc(xT_out.sem, 1)
            turns(s, TURNS, body)

        @block.tensor
        def _(pe):
            pe.wait_ge(const_set, 3)
            pe.wait_ge(wa_ready, 1)

            def body(i):
                for u in range(2):
                    xr_ready.wait(pe, i, u + 1)
                    xT_out.wait_before(pe, i, u + 1)
                    for k in range(KD):
                        ins = nc.tensor.transpose(pb[u][:, k * P:(k + 1) * P],
                                                  xr[:, u, k * P:(k + 1) * P], ident[:, :])
                    ins.then_inc(xT_ready.sem, 1)
                for u in range(2):
                    xT_out.wait(pe, i, u + 1)
                    proj_out.wait_before(pe, i, u + 1)
                    for k in range(KD):
                        ins = nc.tensor.matmul(pb[2 + u][:, 0:D + 2 * H], xnT[:, u, k * P:(k + 1) * P], W_sb[:, k, :],
                                               start=k == 0, stop=k == KD - 1)
                    ins.then_inc(proj_ready.sem, 1)
            turns(pe, TURNS, body)
            pe.wait_ge(cnt_ready, 1)
            nc.tensor.matmul(pb[4][:, 0:NT - 1], ones[:, :], cntd, start=True, stop=True).then_inc(cnt_bc, 1)


def row_moments(nc, ch, stats, sc, T=NTP):
    v = nc.vector
    mean, var, d = sc[:, 2, 0:T], sc[:, 3, 0:T], sc[:, 4, 0:T]
    ch.step(v.tensor_tensor(mean, stats[:, :, 1], stats[:, :, 4], ALU.add))
    ch.step(v.tensor_tensor(d, stats[:, :, 1], stats[:, :, 4], ALU.subtract))
    ch.do(v.tensor_tensor(var, stats[:, :, 2], stats[:, :, 5], ALU.add))
    ch.step(v.tensor_scalar(mean, mean, 0.5, None, ALU.mult))
    ch.step(v.tensor_scalar(var, var, 1.0 / D, None, ALU.mult))
    ch.do(v.tensor_tensor(d, d, d, ALU.mult))
    ch.do(v.scalar_tensor_tensor(var, d, 0.25, var, ALU.mult, ALU.add))


class Mix:

    DVE_STEPS = 32

    def __init__(self, nc, sem, L):
        self.nc, self.L = nc, L
        self.pb, self.sc, self.xn = L["pb"], L["sc"], L["xn"]
        self.ident, self.ones = L["ident"][:, :], L["ones"][:, :]
        area = L["Area"](L["r3"])
        self.wq = area.take(KD, NQ)
        self.pwbd = area.take(QC, P)
        self.wres = area.take(4, D)
        self.blk = area.take(P)
        self.brow = area.take(D)
        self.bn = area.take(8, QC)
        self.fcol = area.take(BLK)
        self.hrow = area.take(BLK, D)
        self.hT = area.take(KD, 512)
        self.hp = area.take(QC, 512)
        self.sp = area.take(4, 512)
        self.rt = area.take(4, 512)
        self.sq = area.take(2, 512)
        hpf = L["r3"][:, self.off(self.hp):]
        self.mu = hpf[:, 0:D]
        self.cov = hpf[:, D:3 * D].rearrange("p (k d) -> p k d", k=KD)
        self.prod = hpf[:, 3 * D:3 * D + 2 * NQ].rearrange("p (k c) -> p k c", k=KD)
        self.mucol = hpf[:, 3 * D + 2 * NQ:3 * D + 2 * NQ + 2]
        self.mask = hpf[:, 3 * D + 2 * NQ + 2:3 * D + 2 * NQ + 3]
        c = lambda name, per, by=1: Count(sem(name), per, by)
        self.w_in = sem("mix_w_in")
        self.pw_zero, self.pw_set = sem("pw_zero"), sem("pw_set")
        self.pw_in = sem("pw_in")
        self.norm_root, self.ratio, self.logged = sem("norm_root"), sem("ratio"), sem("logged")
        self.h_ready, self.h_used = c("h_ready", 2), c("h_used", 2)
        self.hc_ready, self.hc_used = c("hc_ready", 2), c("hc_used", 2)
        self.mu_ready, self.muT, self.mucol_ready = sem("mu_ready"), sem("muT"), sem("mucol_ready")
        self.cov_ready, self.cw, self.prod_ready, self.bn_sums = sem("cov_ready"), sem("cw"), sem("prod_ready"), sem("bn_sums")
        self.var_set, self.std_set, self.bn_set = sem("var_set"), sem("std_set"), sem("bn_set")
        self.hrow_ready = c("hrow_ready", 1)
        self.hT_ready, self.hT_out = c("hT_ready", 2), c("hT_out", 2)
        self.mm_ready, self.mm_out = c("mm_ready", 12), c("mm_out", 12)
        self.sq_ready, self.sq_used = c("sq_ready", 16), c("sq_used", 16)
        self.ksum, self.o1 = c("ksum", 4), c("o1", 4)
        self.root = c("root", 4)
        self.m2, self.o_ready = c("m2", 1), c("o_ready", 4)
        self.f_ready, self.fT, self.fT_out = c("f_ready", 1), c("fT", 1), c("fT_out", 1)
        self.res, self.res_out = c("res", 4), c("res_out", 4)
        self.fx_sq, self.fx_stored = c("fx_sq", 4), c("fx_stored", 1, 16)
        self.order = (2, 3, 0, 1, 4, 5)

    def off(self, ap):
        return 2 * 0 + self._at(ap)

    def _at(self, ap):
        return KD * NQ + QC * P + 4 * D + P + D + 8 * QC + BLK + BLK * D + KD * 512

    def loads(self, sp):
        A = self.L["A"]
        sp.dma_start(self.wq, A["w_qkv"].rearrange("(k p) c -> p k c", p=P)).then_inc(self.w_in, 16)
        sp.dma_start(self.wres, A["w_res"].rearrange("(k p) c -> p k c", p=P)).then_inc(self.w_in, 16)
        sp.dma_start(self.brow, A["b_res"].to_broadcast([P, D])).then_inc(self.w_in, 16)
        for j, name in enumerate(("bn_gamma", "bn_beta", "w_dw")):
            sp.dma_start(self.bn[:, j, :], A[name]).then_inc(self.w_in, 16)
        sp.wait_ge(self.pw_zero, 2)
        for b in range(4):
            sp.dma_start(self.pwbd[32 * b:32 * b + 32, :, 32 * b:32 * b + 32],
                         A["w_pw"][32 * b:32 * b + 32]).then_inc(self.pw_in, 16)

    def pool_start(self):
        self.nc.gpsimd.memset(self.pwbd, 0.0).then_inc(self.pw_zero, 1)
        self.nc.gpsimd.memset(self.blk, 0.0).then_inc(self.pw_zero, 1)

    def dve_start(self, ch):
        nc, sc, v, pb = self.nc, self.sc, self.nc.vector, self.pb
        v.wait_ge(self.pw_zero, 2)
        for b in range(4):
            ch.step(v.memset(self.blk[32 * b:32 * b + 32, 32 * b:32 * b + 32], 1.0))
        v.wait_ge(self.norm_root, 1)
        n, p, a, b, c, d = (sc[:, j, :] for j in (5, 6, 7, 8, 10, 11))
        ch.do(v.tensor_scalar(n, n, MINN, None, ALU.max))
        ch.do(v.tensor_scalar(p, n, MAXN, None, ALU.min))
        ch.step(v.tensor_scalar(a, p, -1.0, 1.0, ALU.mult, ALU.add))
        ch.do(v.tensor_scalar(b, p, 1.0, None, ALU.add))
        ch.do(v.reciprocal(a, a))
        v.tensor_tensor(a, a, b, ALU.mult).then_inc(self.ratio, 1)
        ch.do(v.tensor_tensor(c, p, p, ALU.mult))
        ch.do(v.tensor_scalar(d, c, 1.0 / 9.0, 1.0 / 7.0, ALU.mult, ALU.add))
        for k in (5.0, 3.0, 1.0):
            ch.do(v.tensor_tensor(d, d, c, ALU.mult))
            ch.do(v.tensor_scalar(d, d, 1.0 / k, None, ALU.add))
        ch.do(v.tensor_tensor(d, d, p, ALU.mult))
        v.wait_ge(self.logged, 1)
        ch.do(v.tensor_scalar(b, b, 0.5, None, ALU.mult))
        ch.do(v.tensor_tensor(d, d, b, ALU.subtract))
        ch.do(v.tensor_scalar(p, p, 0.2, None, ALU.is_lt))
        ch.do(v.tensor_tensor(d, d, p, ALU.mult))
        ch.do(v.tensor_tensor(b, b, d, ALU.add))
        ch.do(v.reciprocal(n, n))
        ch.do(v.tensor_tensor(sc[:, 1, :], b, n, ALU.mult))
        ch.do(v.tensor_scalar(self.mask, self.L["pcol"][:, 0:1], float(N - (NT - 1) * P), None, ALU.is_lt))

        def tile(t):
            return self.xn[:, bass.ds(t, 1), :].rearrange("p o d -> p (o d)")

        def h(i, us=(0, 1)):
            for u in us:
                t = 2 * i + u
                self.h_used.wait_before(v, i, u + 1)
                v.tensor_scalar(self.hrow[:, u, :], tile(t), sc[:, 1, bass.ds(t, 1)], None, ALU.mult)\
                    .then_inc(self.h_ready.sem, 1)
        turns(v, NT // 2, h)
        h(NT // 2, (0,))
        v.wait_ge(self.h_used.sem, NT)
        v.tensor_scalar(self.mu, pb[0][:, 0:D], 1.0 / N, None, ALU.mult).then_inc(self.mu_ready, 1)
        v.wait_ge(self.mu_ready, 1)

        def hc(i, us=(0, 1)):
            for u in us:
                t = 2 * i + u
                self.hc_used.wait_before(v, i, u + 1)
                ins = v.scalar_tensor_tensor(self.hrow[:, u, :], tile(t), sc[:, 1, bass.ds(t, 1)], self.mu, ALU.mult,
                                             ALU.subtract)
                if len(us) == 1:
                    ch.do(ins)
                    ins = v.tensor_scalar(self.hrow[:, u, :], self.hrow[:, u, :], self.mask, None, ALU.mult)
                ins.then_inc(self.hc_ready.sem, 1)
        turns(v, NT // 2, hc)
        hc(NT // 2, (0,))
        v.wait_ge(self.muT, 1)
        for k in range(KD):
            v.tensor_copy(self.mucol[:, k:k + 1], pb[5][:, k * P:k * P + 1]).then_inc(self.mucol_ready, 1)
        v.wait_ge(self.hc_used.sem, NT)
        for k in range(KD):
            v.tensor_scalar(self.cov[:, k, :], pb[1 + k][:, 0:D], 1.0 / N, None, ALU.mult).then_inc(self.cov_ready, 1)
        v.wait_ge(self.w_in, 6 * 16)
        for k in range(KD):
            v.wait_ge(self.cw, 2 * k + 2)
            for j in range(2):
                c = slice(j * NQ // 2, (j + 1) * NQ // 2)
                v.tensor_tensor(self.prod[:, k, c], pb[3 + j][:, 0:NQ // 2], self.wq[:, k, c], ALU.mult)\
                    .then_inc(self.prod_ready, 1)
        v.wait_ge(self.bn_sums, 1)
        bn = self.bn
        v.tensor_scalar(bn[:, 4, :], pb[5][:, 0:QC], 1e-5, None, ALU.add).then_inc(self.var_set, 1)
        v.wait_ge(self.std_set, 1)
        ch.do(v.reciprocal(bn[:, 4, :], bn[:, 4, :]))
        ch.do(v.tensor_tensor(bn[:, 5, :], bn[:, 0, :], bn[:, 4, :], ALU.mult))
        ch.do(v.tensor_tensor(bn[:, 6, :], pb[5][:, 8:8 + QC], bn[:, 5, :], ALU.mult))
        ch.do(v.tensor_tensor(bn[:, 6, :], bn[:, 1, :], bn[:, 6, :], ALU.subtract))
        v.wait_ge(self.pw_in, 64)
        for c in range(QC):
            ch.step(v.tensor_scalar(self.pwbd[:, c, :], self.pwbd[:, c, :], bn[:, 2, c:c + 1], None, ALU.mult))
        ch.done()
        v.sem_inc(self.bn_set, 1)

    def act_start(self, s):
        sc, act = self.sc, self.nc.scalar
        act.activation(sc[:, 5, :], sc[:, 0, :], ACT.Sqrt).then_inc(self.norm_root, 1)
        s.wait_ge(self.ratio, 1)
        act.activation(sc[:, 8, :], sc[:, 7, :], ACT.Ln).then_inc(self.logged, 1)
        s.wait_ge(self.var_set, 1)
        act.activation(self.bn[:, 4, :], self.bn[:, 4, :], ACT.Sqrt).then_inc(self.std_set, 1)
        s.wait_ge(self.bn_set, 1)

    def pe_start(self, pe):
        mm, pb, ones = self.nc.tensor.matmul, self.pb, self.ones

        def colsum(i, us=(0, 1)):
            for u in us:
                self.h_ready.wait(pe, i, u + 1)
                first = isinstance(i, int) and i == 0 and u == 0
                mm(pb[0][:, 0:D], ones, self.hrow[:, u, :], start=first, stop=len(us) == 1)\
                    .then_inc(self.h_used.sem, 1)
        turns(pe, NT // 2, colsum)
        colsum(NT // 2, (0,))
        pe.wait_ge(self.mu_ready, 1)
        for k in range(KD):
            ins = self.nc.tensor.transpose(pb[5][:, k * P:(k + 1) * P], self.mu[:, k * P:(k + 1) * P], self.ident)
        ins.then_inc(self.muT, 1)

        def gram(i, us=(0, 1)):
            for u in us:
                self.hc_ready.wait(pe, i, u + 1)
                first = isinstance(i, int) and i == 0 and u == 0
                for k in range(KD):
                    ins = mm(pb[1 + k][:, 0:D], self.hrow[:, u, k * P:(k + 1) * P], self.hrow[:, u, :], start=first,
                             stop=len(us) == 1)
                ins.then_inc(self.hc_used.sem, 1)
        turns(pe, NT // 2, gram)
        gram(NT // 2, (0,))
        pe.wait_ge(self.cov_ready, 2)
        pe.wait_ge(self.w_in, 6 * 16)
        for m in range(KD):
            for j in range(2):
                if m:
                    pe.wait_ge(self.prod_ready, j + 1)
                for k in range(KD):
                    ins = mm(pb[3 + j][:, 0:NQ // 2], self.cov[:, k, m * P:(m + 1) * P],
                             self.wq[:, k, j * NQ // 2:(j + 1) * NQ // 2], start=k == 0, stop=k == KD - 1)
                ins.then_inc(self.cw, 1)
        pe.wait_ge(self.prod_ready, 4)
        pe.wait_ge(self.mucol_ready, 2)
        for c in range(QC):
            for k in range(KD):
                mm(pb[5][:, c:c + 1], self.prod[:, k, c * P:(c + 1) * P], ones[:, 0:1], start=k == 0, stop=k == KD - 1)
            for k in range(KD):
                ins = mm(pb[5][:, 8 + c:9 + c], self.wq[:, k, c * P:(c + 1) * P], self.mucol[:, k:k + 1], start=k == 0,
                         stop=k == KD - 1)
        ins.then_inc(self.bn_sums, 1)
        pe.wait_ge(self.bn_set, 1)

    def bank(self, n):
        return self.pb[2 + n % 2][:, :]

    def sq_free(self, s, i, k):
        if k >= 2:
            self.sq_used.wait(s, i, k - 1)
        else:
            self.sq_used.wait_before(s, i, 15 + k)

    def pe(self, pe, i, q):
        mm, tr, pb = self.nc.tensor.matmul, self.nc.tensor.transpose, self.pb

        def norm(k):
            bank = pb[5] if 6 <= k < 12 else pb[4]
            self.sq_ready.wait(pe, i, k + 1)
            if k == 0:
                self.root.wait_before(pe, i, 4)
            if k == 6:
                self.fT_out.wait_before(pe, i, 1)
            if k == 12:
                self.root.wait(pe, i, 1)
                self.m2.wait(pe, i, 1)
            mm(bank[:, :], self.ones, self.sq[:, k % 2, :], start=k in (0, 6, 12), stop=k in (5, 11, 15))\
                .then_inc(self.sq_used.sem, 1)

        if q == 0:
            self.hrow_ready.wait(pe, i, 1)
            self.o1.wait_before(pe, i, 4)
            for k in range(KD):
                for j in range(BLK):
                    ins = tr(pb[k][:, j * P:(j + 1) * P], self.hrow[:, j, k * P:(k + 1) * P], self.ident)
                ins.then_inc(self.hT_ready.sem, 1)
            self.hT_out.wait(pe, i, 2)
            self.res_out.wait_before(pe, i, 4)
            for n in range(QC):
                if n >= 2:
                    self.mm_out.wait(pe, i, n - 1)
                c = self.order[n]
                for k in range(KD):
                    ins = mm(self.bank(n), self.wq[:, k, c * P:(c + 1) * P], self.hT[:, k, :], start=k == 0, stop=k == 1)
                ins.then_inc(self.mm_ready.sem, 1)
                if n:
                    norm(n - 1)
            norm(QC - 1)
        if q == 1:
            def key_sum(j, count):
                self.mm_out.wait(pe, i, count)
                mm(pb[j % 2][:, :], self.blk, self.hp[:, 2 + j % 2, :], start=True, stop=True).then_inc(self.ksum.sem, 1)
            key_sum(0, 2)
            key_sum(1, 2)
            for n in range(QC, 2 * QC):
                self.mm_out.wait(pe, i, n - 1)
                c = self.order[n - QC]
                mm(self.bank(n), self.pwbd[:, c, :], self.hp[:, c, :], start=True, stop=True).then_inc(self.mm_ready.sem, 1)
                if n > QC:
                    norm(n - 1)
                if n - QC == 3:
                    for j in range(2):
                        self.o1.wait(pe, i, j + 1)
                        key_sum(2 + j, QC + 1 + j)
            norm(11)
        if q == 2:
            for k in range(12, 16):
                norm(k)
        if q == 3:
            self.mm_out.wait(pe, i, 12)
            self.o_ready.wait(pe, i, 4)
            for j in range(BLK):
                for m in range(4):
                    o = self.hp[:, m, :] if m < 2 else self.sp[:, m - 2, :]
                    ins = mm(pb[2 + j // 2][:, (j % 2) * D:(j % 2 + 1) * D], o[:, j * P:(j + 1) * P], self.wres[:, m, :],
                             start=m == 0, stop=m == 3)
                ins.then_inc(self.res.sem, 1)
            self.f_ready.wait(pe, i, 1)
            self.root.wait(pe, i, 2)
            for j in range(BLK):
                ins = tr(pb[5][:, j * P:(j + 1) * P], self.rt[:, 3, j * P:(j + 1) * P], self.ident)
            ins.then_inc(self.fT.sem, 1)

    def act(self, s, i, q):
        act, pb = self.nc.scalar.activation, self.pb
        if q == 0:
            self.mm_ready.wait_before(s, i, 6)
            for k in range(KD):
                self.hT_ready.wait(s, i, k + 1)
                act(self.hT[:, k, :], pb[k][:, :], ACT.Copy).then_inc(self.hT_out.sem, 1)
            self.res.wait_before(s, i, 4)
            for n in range(QC):
                c = self.order[n]
                self.mm_ready.wait(s, i, n + 1)
                act(self.hp[:, c, :], self.bank(n), ACT.Relu, bias=self.bn[:, 6, c:c + 1], scale=self.bn[:, 5, c:c + 1])\
                    .then_inc(self.mm_out.sem, 1)
                self.mm_out.wait(s, i, n + 1)
                self.sq_free(s, i, n)
                act(self.sq[:, n % 2, :], self.hp[:, c, :], ACT.Square).then_inc(self.sq_ready.sem, 1)
        if q == 1:
            for n in range(QC, 2 * QC):
                c = self.order[n - QC]
                self.mm_ready.wait(s, i, n + 1)
                self.sq_free(s, i, n)
                act(self.sq[:, n % 2, :], self.bank(n), ACT.Square).then_inc(self.sq_ready.sem, 1)
                dst = self.hp[:, c, :] if c in (2, 3) else self.sp[:, {0: 0, 1: 1, 4: 2, 5: 3}[c], :]
                act(dst, self.bank(n), ACT.Copy if c >= 4 else ACT.Relu).then_inc(self.mm_out.sem, 1)
        if q == 2:
            self.sq_used.wait(s, i, 6)
            act(self.rt[:, 0, :], pb[4][:, :], ACT.Sqrt).then_inc(self.root.sem, 1)
            self.sq_used.wait(s, i, 12)
            act(self.rt[:, 2, :], pb[5][:, :], ACT.Copy).then_inc(self.root.sem, 1)
            self.m2.wait(s, i, 1)
            act(self.rt[:, 2, :], self.rt[:, 2, :], ACT.Sqrt).then_inc(self.root.sem, 1)
            for k in range(12, 16):
                m = k - 12
                self.o_ready.wait(s, i, m + 1)
                self.sq_free(s, i, k)
                o = self.hp[:, m, :] if m < 2 else self.sp[:, m - 2, :]
                act(self.sq[:, k % 2, :], o, ACT.Square).then_inc(self.sq_ready.sem, 1)
            self.sq_used.wait(s, i, 16)
            act(self.rt[:, 2, :], pb[4][:, :], ACT.Sqrt).then_inc(self.root.sem, 1)
        if q == 3:
            for j in range(BLK):
                self.res_out.wait(s, i, j + 1)
                if j:
                    self.fx_sq.wait(s, i, j)
                act(self.sq[:, 0, 0:D], self.hrow[:, j, :], ACT.Square, accum_out=self.sc[:, 9, bass.ds(4 * i + j, 1)])\
                    .then_inc(self.fx_sq.sem, 1)
            s.dma_start(self.L["fx_d"][bass.ds(4 * i, BLK), :, :].rearrange("t p d -> p t d"), self.hrow)\
                .then_inc(self.fx_stored.sem, 16)

    def dve(self, ch, i, q):
        v, pb, rt = self.nc.vector, self.pb, self.rt
        rs = self.sc[:, 1, :]
        if q == 0:
            self.fx_stored.wait_before(v, i, 1)
            self.fx_sq.wait_before(v, i, 4)
            v.tensor_tensor(self.hrow, self.xn[:, bass.ds(4 * i, BLK), :],
                            rs[:, bass.ds(4 * i, BLK)].unsqueeze(2).to_broadcast([P, BLK, D]), ALU.mult)\
                .then_inc(self.hrow_ready.sem, 1)
        if q == 1:
            for j in range(4):
                x = self.hp[:, j, :] if j < 2 else self.sp[:, j - 2, :]
                self.ksum.wait(v, i, j + 1)
                if j < 2:
                    self.mm_ready.wait(v, i, 9 + j)
                    self.sq_used.wait(v, i, 3 + j)
                else:
                    self.mm_out.wait(v, i, 7 + j)
                v.tensor_tensor(x, x, pb[j % 2][:, :], ALU.mult).then_inc(self.o1.sem, 1)
        if q == 2:
            r0, r1, r2, r3 = (rt[:, j, :] for j in range(4))
            self.root.wait(v, i, 1)
            ch.do(v.tensor_scalar(r0, r0, MINN, None, ALU.max))
            ch.step(v.tensor_scalar(r1, r0, CAP, None, ALU.min))
            ch.do(v.reciprocal(r0, r0))
            self.root.wait(v, i, 2)
            v.tensor_tensor(r2, r2, pb[4][:, :], ALU.add).then_inc(self.m2.sem, 1)
            ch.do(v.tensor_tensor(r0, r0, r1, ALU.mult))
            self.root.wait(v, i, 3)
            ch.do(v.tensor_tensor(r2, r2, r0, ALU.mult))
            ch.do(v.tensor_scalar(r2, r2, MINN, None, ALU.max))
            ch.step(v.tensor_scalar(r1, r2, CAP, None, ALU.min))
            ch.do(v.reciprocal(r2, r2))
            ch.do(v.tensor_tensor(r1, r1, r2, ALU.mult))
            ch.do(v.tensor_tensor(r0, r0, r1, ALU.mult))
            for m in range(4):
                val = self.hp[:, 4 + m, :] if m < 2 else self.sp[:, m, :]
                o = self.hp[:, m, :] if m < 2 else self.sp[:, m - 2, :]
                w = r1 if m % 2 == 0 else r3
                self.mm_out.wait(v, i, 12)
                ch.do(v.tensor_tensor(val, val, r0, ALU.mult))
                ch.do(v.tensor_scalar(w, val, MINN, None, ALU.add))
                ch.do(v.reciprocal(w, w))
                ch.do(v.tensor_tensor(val, val, w, ALU.mult))
                v.tensor_tensor(o, o, val, ALU.mult).then_inc(self.o_ready.sem, 1)
            ch.do(v.tensor_tensor(r0, r0, r0, ALU.mult))
        if q == 3:
            r0, r1, r2, r3 = (rt[:, j, :] for j in range(4))
            self.root.wait(v, i, 4)
            ch.do(v.tensor_tensor(r2, r2, r0, ALU.mult))
            ch.do(v.tensor_scalar(r2, r2, MINN, None, ALU.max))
            ch.step(v.tensor_scalar(r3, r2, CAP, None, ALU.min))
            ch.do(v.reciprocal(r2, r2))
            ch.do(v.tensor_tensor(r3, r3, r2, ALU.mult))
            v.tensor_tensor(r3, r3, r0, ALU.mult).then_inc(self.f_ready.sem, 1)
            self.fT.wait(v, i, 1)
            v.tensor_copy(self.fcol, pb[5][:, ::P]).then_inc(self.fT_out.sem, 1)
            self.fT_out.wait(v, i, 1)
            for j in range(BLK):
                self.res.wait(v, i, 2 * (j // 2) + 2)
                v.scalar_tensor_tensor(self.hrow[:, j, :], pb[2 + j // 2][:, (j % 2) * D:(j % 2 + 1) * D],
                                       self.fcol[:, j:j + 1], self.brow, ALU.mult, ALU.add).then_inc(self.res_out.sem, 1)

    def rest(self, fn, eng, i, groups):
        for q in range(len(groups), 4):
            fn(eng, i, q)


def edges_and_mix(nc, ctx, sem, L):
    A, pb, ident, ones, xn, sc = L["A"], L["pb"], L["ident"], L["ones"], L["xn"], L["sc"]
    iota_f, dst_f, nt_f, nodecol, E_all = (L[k] for k in ("iota_f", "dst_f", "nt_f", "nodecol", "E_all"))
    src_sb, idx, grab, sde, r1, r2, r3 = (L[k] for k in ("src_sb", "idx", "grab", "sde", "r1", "r2", "r3"))
    sat_d, et_d, tau_i = L["sat_d"], L["et_d"], L["tau_i"]
    TA = NB
    NX = NT - 1

    small = L["Area"](L["r4"])
    dstb = small.take(EG * P, dt=I32)
    st = small.take(EG, P)
    edge_pre = small.take(2, EG * H)
    satb = small.take(2, EG * H)
    cols = small.take(16)

    same = r1[:, 0:CH + 1]
    tmp = r1[:, CH + 8:2 * CH + 8]
    dstx = r2[:, 0:CH + 2].bitcast(I32)
    pre = r2[:, 0:CH]
    score = r3[:, 0:CH]
    PR = 4
    TB = VT // (4 * PR)
    rows = r3[:, CH:CH + 4 * PR * TAB].rearrange("p (q e d) -> p q e d", q=4, e=PR)
    acc = r1[:, 0:NT * TAB].rearrange("p (t d) -> p t d", d=TAB)
    S = st[:, 0:4, :]
    msg = L["r4"][:, EG * P + 4 * P:EG * P + 4 * P + 4 * TAB].rearrange("p (u d) -> p u d", u=4)
    etb = L["r4"][:, 0:1024].rearrange("p (u t e) -> p u t e", u=2, t=4)
    carry = L["r4"][:, 1024:2048].rearrange("p (j e) -> p j e", e=P)

    idx_in = [Count(sem(f"idx_in{q}"), 1, 16) for q in range(4)]
    grabbed = [Count(sem(f"grabbed{q}"), EG, 16) for q in range(4)]
    copied = [Count(sem(f"copied{q}"), 1, 16) for q in range(4)]
    gate = sem("gate")
    dst_in = Count(sem("dst_in"), 4, 16)
    st_built = Count(sem("st_built"), 4)
    sde_ready = Count(sem("sde_ready"), 4)
    sde_used = Count(sem("sde_used"), 4)
    score_ready = Count(sem("score_ready"), 4)
    scT_ready = Count(sem("scT_ready"), 4)
    scT_out = Count(sem("scT_out"), 4)
    sat_stored = [Count(sem(f"sat_stored{u}"), 2, 16) for u in range(2)]
    x_dst_in, x_cols_in = [sem(f"x_dst_in{j}") for j in range(3)], sem("x_cols_in")
    x_built, x_sde, x_used = sem("x_built"), sem("x_sde"), sem("x_used")
    dve2 = sem("dve2")
    dst_chunks_in, sat_in = sem("dst_chunks_in"), sem("sat_in")
    r2_free = sem("r2_free")
    diag_ready, diag_sum = sem("diag_ready"), sem("diag_sum")
    shifted, weighed, et_out = sem("shifted"), sem("weighed"), sem("et_out")
    et_in = [Count(sem(f"et_in{u}"), 1, 64) for u in range(2)]
    etT_ready, etT_out = Count(sem("etT_ready"), 2), Count(sem("etT_out"), 2)
    e_extra = sem("e_extra")
    bidx_in = [Count(sem(f"bidx_in{q}"), 1, 16) for q in range(4)]
    row_in = [Count(sem(f"row_in{q}"), PR, 16) for q in range(4)]
    msg_ready = Count(sem("msg_ready"), 4 * PR)
    summed = Count(sem("summed"), 4 * PR)
    added = Count(sem("added"), 4 * PR)
    acc_zero = sem("acc_zero")
    mixed = sem("mixed")

    MIX = Mix(nc, sem, L)
    PER_TURN = MIX.DVE_STEPS + 4

    def groups(i):
        return range(4) if not isinstance(i, int) or i < TA - 1 else range(NG - 4 * (TA - 1))

    def all_turns(eng, body):
        body(0)
        with eng.Fori(1, TA - 1) as i:
            body(i)
        body(TA - 1)

    with nc.Block() as block:
        @block.sync
        def _(sp):
            def extra(j):
                sp.dma_start(idx[:, j, :], src_sb[:, j * EG:(j + 1) * EG]).then_inc(idx_in[j].sem, 16)
            MIX.loads(sp)
            for q in range(4):
                extra(q)
            for j in range(3):
                if j:
                    sp.wait_ge(x_built, j)
                for e in range(EG):
                    n = j * EG + e
                    t = sp.value_load(tau_i[0:1, n:n + 1], min_val=0, max_val=ET - 1)
                    sp.dma_start(dstb[:, e * P:(e + 1) * P],
                                 A["dst_flat"][:, bass.ds(t * P, P)].to_broadcast([P, P])).then_inc(x_dst_in[j], 16)
                    sp.dma_start(src_sb[:, ET + n:ET + n + 1], src_sb[:, bass.ds(t, 1)]).then_inc(x_cols_in, 16)
                    sp.dma_start(dst_f[:, ET + n:ET + n + 1], dst_f[:, bass.ds(t, 1)]).then_inc(x_cols_in, 16)
            sp.wait_ge(x_built, 3)
            sp.dma_start(dstb, A["dst_flat"][:, 0:EG * P].to_broadcast([P, EG * P])).then_inc(dst_in.sem, 16)
            sp.wait_ge(x_cols_in, 2 * 16 * NX)

            def body(i):
                for q in groups(i):
                    g = 4 * i + q
                    if not (isinstance(g, int) and g == NG - 1):
                        st_built.wait(sp, i, q + 1)
                        sp.dma_start(dstb, A["dst_flat"][:, bass.ds((g + 1) * EG * P, EG * P)]
                                     .to_broadcast([P, EG * P])).then_inc(dst_in.sem, 16)
                    grabbed[q].wait(sp, i, EG)
                    sp.dma_start(E_all[:, bass.ds(g * EG, EG), :], grab[:, q, :, :]).then_inc(copied[q].sem, 16)
                    copied[q].wait(sp, i, 1)
                    sp.dma_start(idx[:, q, :], src_sb[:, bass.ds((g + 4) * EG, EG)]).then_inc(idx_in[q].sem, 16)
            all_turns(sp, body)
            for q in range(4):
                idx_in[q].wait(sp, TA if q < 1 else TA - 1, 1)
            for q in range(4):
                sp.dma_start(idx[:, q, 0:PR], src_sb[:, q * PR:(q + 1) * PR]).then_inc(bidx_in[q].sem, 16)
            sp.wait_ge(r2_free, 1)
            for h in range(H):
                sp.dma_start(dstx[16 * h:16 * (h + 1), :], A["dst_chunks"]).then_inc(dst_chunks_in, 16)
            for u in range(2):
                sp.wait_ge(sat_stored[u].sem, 16 * (NG + 1) // 2)
            sp.wait_ge(mixed, 1)
            sp.dma_start(score, sat_d.rearrange("h t e -> (h t e)").rearrange("(p f) -> p f", p=P)).then_inc(sat_in, 16)
            W4 = CH // 4
            for k in range(4):
                sp.wait_ge(weighed, k + 1)
                sp.dma_start(et_d.rearrange("h t e -> (h t e)").rearrange("(p f) -> p f", p=P)[:, k * W4:(k + 1) * W4],
                             score[:, k * W4:(k + 1) * W4]).then_inc(et_out, 16)
            sp.wait_ge(et_out, 64)
            for i in range(TA):
                u = i % 2
                if i > 1:
                    sp.wait_ge(etT_ready.sem, i - 1)
                for k in groups(i):
                    g = 4 * i + k
                    sp.dma_start(etb[:, u, k, :], et_d[:, g * EG:(g + 1) * EG, :].rearrange("h t e -> t h e"))\
                        .then_inc(et_in[u].sem, 16)
            sp.wait_ge(etT_out.sem, TA)
            for n in range(NX):
                t = sp.value_load(tau_i[0:1, n:n + 1], min_val=0, max_val=ET - 1)
                sp.dma_start(E_all[:, ET + n:ET + n + 1, :], E_all[:, bass.ds(t, 1), :]).then_inc(e_extra, 16)

            def second(i):
                for q in range(4):
                    msg_ready.wait(sp, i, (q + 1) * PR)
                    if not (isinstance(i, int) and i == TB - 1):
                        sp.dma_start(idx[:, q, 0:PR], src_sb[:, bass.ds(((i + 1) * 4 + q) * PR, PR)])\
                            .then_inc(bidx_in[q].sem, 16)
            second(0)
            with sp.Fori(1, TB - 1) as i:
                second(i)

        @block.gpsimd
        def _(g_):
            MIX.pool_start()

            def body(i):
                for q in groups(i):
                    idx_in[q].wait(g_, i, 1)
                    g_.sem_inc(gate, 1)
                    for e in range(EG):
                        g_.indirect_dma_start(out=grab[:, q, e, :], out_offset=None, in_=L["ssrc_d"],
                                              in_offset=bass.IndirectOffsetOnAxis(ap=idx[:, q, e:e + 1], axis=0))\
                            .then_inc(grabbed[q].sem, 16)
            all_turns(g_, body)
            g_.wait_ge(mixed, 1)

            def second(i):
                for q in range(4):
                    bidx_in[q].wait(g_, i, 1)
                    g_.sem_inc(gate, 1)
                    for e in range(PR):
                        g_.indirect_dma_start(out=rows[:, q, e, :], out_offset=None, in_=L["table_d"],
                                              in_offset=bass.IndirectOffsetOnAxis(ap=idx[:, q, e:e + 1], axis=0))\
                            .then_inc(row_in[q].sem, 16)
            turns(g_, TB, second)

        @block.vector
        def _(v):
            ch = Chain(v, dve2)
            ch.do(nc.vector.memset(r2[:, :], 0.0))
            for j in range(3):
                v.wait_ge(x_dst_in[j], 16 * EG)
                nc.vector.tensor_tensor(st[:, :, :], dstb.rearrange("p (t e) -> p t e", e=P),
                                        nodecol[:, ET + j * EG:ET + (j + 1) * EG].unsqueeze(2).to_broadcast([P, EG, P]),
                                        ALU.is_equal).then_inc(x_built, 1)
                v.wait_ge(x_sde, j + 1)
                for e in range(EG):
                    n = j * EG + e
                    t = v.value_load(tau_i[0:1, n:n + 1], min_val=0, max_val=ET - 1)
                    ch.do(nc.vector.tensor_tensor(sde[:, bass.ds(t, 1), :], sde[:, bass.ds(t, 1), :],
                                                  pb[6][:, e * H:(e + 1) * H].rearrange("p (o h) -> p o h", o=1), ALU.add))
                v.sem_inc(x_used, 1)
            v.wait_ge(x_cols_in, 2 * 16 * NX)
            ch.do(nc.vector.scalar_tensor_tensor(dst_f[:, :], nt_f[:, :], -float(P), dst_f[:, :], ALU.mult, ALU.add))
            ch.do(nc.vector.tensor_tensor(dst_f[:, ET:VT], dst_f[:, ET:VT], L["never"][:, :], ALU.subtract))
            MIX.dve_start(ch)
            ch.loop()

            def body(i):
                ch.turn(i, PER_TURN)
                for q in groups(i):
                    u, g = q % 2, 4 * i + q
                    dst_in.wait(v, i, q + 1)
                    nc.vector.tensor_tensor(st[:, :, :], dstb.rearrange("p (t e) -> p t e", e=P),
                                            nodecol[:, bass.ds(g * EG, EG)].unsqueeze(2).to_broadcast([P, EG, P]),
                                            ALU.is_equal).then_inc(st_built.sem, 1)
                    MIX.dve(ch, i, q)
                    sde_ready.wait(v, i, q + 1)
                    copied[q].wait(v, i, 1)
                    if q >= 2:
                        scT_ready.wait(v, i, q - 1)
                    else:
                        scT_ready.wait_before(v, i, q + 3)
                    ep = edge_pre[:, u, :]
                    nc.vector.tensor_tensor(ep, E_all[:, bass.ds(g * EG, EG), :].rearrange("p t h -> p (t h)"),
                                            pb[6][:, u * P:(u + 1) * P], ALU.add).then_inc(sde_used.sem, 1)
                    sde_used.wait(v, i, q + 1)
                    ch.do(nc.vector.tensor_tensor(ep, ep, sde[:, bass.ds(g * EG, EG), :].rearrange("p t h -> p (t h)"),
                                                  ALU.add))
                    nc.vector.scalar_tensor_tensor(ep, ep, 0.2, ep, ALU.mult, ALU.max).then_inc(score_ready.sem, 1)
            body(0)
            assert ch.k == PER_TURN, ch.k
            with v.Fori(1, TA - 1) as i:
                body(i)
            body(TA - 1)
            v.wait_ge(score_ready.sem, NG)
            v.sem_inc(r2_free, 1)
            MIX.rest(MIX.dve, ch, TA - 1, groups(TA - 1))
            v.wait_ge(mixed, 1)
            v.wait_ge(dst_chunks_in, 16 * H)
            ch.do(nc.vector.tensor_tensor(same, dstx[:, 1:CH + 2], dstx[:, 0:CH + 1], ALU.not_equal))
            ch.do(nc.vector.tensor_scalar(same, same, -BIG, None, ALU.mult))
            col = lambda j: cols[:, j:j + 1]
            ch.step(nc.vector.tensor_tensor(col(0), dstx[:, CH:CH + 1], dstx[:, 0:1], ALU.not_equal))
            ch.do(nc.vector.tensor_tensor(col(1), dstx[:, CH + 1:CH + 2], dstx[:, 1:2], ALU.not_equal))
            ch.do(nc.vector.tensor_scalar(cols[:, 0:2], cols[:, 0:2], -BIG, None, ALU.mult))
            v.wait_ge(sat_in, 16)
            fwd_neg, bwd_neg = same[:, 0:CH], same[:, 1:CH + 1]

            def across(k, own, chain, edge, back):
                for j, c in enumerate((own, chain, edge)):
                    ch.step(nc.vector.tensor_scalar(carry[:, j, :], ident[:, :], c, None, ALU.mult))
                ch.done()
                v.sem_inc(diag_ready, 1)
                v.wait_ge(diag_sum, k + 1)
                ch.do(nc.vector.tensor_copy(carry[:, 0:3, :], pb[5][:, 0:3 * P].rearrange("p (j e) -> p j e", e=P)))
                o, c, d, w, r = (carry[:, j, :] for j in range(5))
                ch.do(nc.vector.memset(r, -BIG))
                if back:
                    ch.do(nc.vector.tensor_tensor_scan(w[:, ::-1], c[:, ::-1], o[:, ::-1], -BIG, ALU.add, ALU.max))
                    ch.do(nc.vector.tensor_tensor(r[:, 0:P - 1], w[:, 1:P], d[:, 0:P - 1], ALU.add))
                else:
                    ch.do(nc.vector.tensor_tensor_scan(w, c, o, -BIG, ALU.add, ALU.max))
                    ch.do(nc.vector.tensor_tensor(r[:, 1:P], w[:, 0:P - 1], d[:, 1:P], ALU.add))
                ch.do(nc.vector.tensor_tensor(r, r, ident[:, :], ALU.mult))
                ch.do(nc.vector.reduce_sum(col(4 + k), r, mybir.AxisListType.X))
                ch.do(nc.vector.tensor_scalar(col(4 + k), col(4 + k), -BIG, None, ALU.max))

            ch.do(nc.vector.tensor_tensor_scan(pre, fwd_neg, score, -BIG, ALU.add, ALU.max))
            across(0, pre[:, CH - 1:CH], col(0), same[:, 0:1], False)
            ch.do(nc.vector.tensor_tensor_scan(pre, fwd_neg, score, col(4), ALU.add, ALU.max))
            ch.do(nc.vector.tensor_tensor_scan(tmp[:, ::-1], bwd_neg[:, ::-1], pre[:, ::-1], -BIG, ALU.add, ALU.max))
            across(1, tmp[:, 0:1], col(1), same[:, CH:CH + 1], True)
            ch.do(nc.vector.tensor_tensor_scan(tmp[:, ::-1], bwd_neg[:, ::-1], pre[:, ::-1], col(5), ALU.add, ALU.max))
            W4 = CH // 4
            for k in range(4):
                c = slice(k * W4, (k + 1) * W4)
                nc.vector.tensor_tensor(score[:, c], score[:, c], tmp[:, c], ALU.subtract).then_inc(shifted, 1)
            v.wait_ge(shifted, 4)
            nc.vector.memset(r1[:, 0:T2 * TAB], 0.0).then_inc(acc_zero, 1)
            for i in range(TA):
                u = i % 2
                v.wait_ge(etT_ready.sem, i + 1)
                w = 512 if i < TA - 1 else P * len(groups(i))
                nc.vector.tensor_copy(E_all[:, i * 64:i * 64 + w // H, :].rearrange("p t h -> p (t h)"),
                                      pb[6 + u][:, 0:w]).then_inc(etT_out.sem, 1)
            v.wait_ge(etT_out.sem, TA)
            v.wait_ge(acc_zero, 1)
            v.wait_ge(e_extra, 16 * NX)

            def second(i):
                for q in range(4):
                    nts = []
                    for k in range(PR // 4):
                        t4 = v.value_load(L["nt_pack"][0:1, bass.ds((i * 4 + q) * (PR // 4) + k, 1)], min_val=0, max_val=NT ** 4 - 1)
                        for e in range(4):
                            nts.append(v.snap(t4 % NT))
                            if e < 3:
                                t4 = v.snap(t4 // NT)

                    def add(e):
                        c = q * PR + e
                        summed.wait(v, i, c + 1)
                        if c:
                            added.wait(v, i, c)
                        else:
                            added.wait_before(v, i, 4 * PR)
                        a = acc[:, bass.ds(nts[e], 1), :]
                        nc.vector.tensor_tensor(a, a, pb[c % 4][:, 0:TAB].rearrange("p (o d) -> p o d", o=1),
                                                ALU.add).then_inc(added.sem, 1)
                    row_in[q].wait(v, i, PR)
                    for e in range(PR):
                        c, u = q * PR + e, e % 4
                        t = i * 4 * PR + c
                        if c >= 4:
                            summed.wait(v, i, c - 3)
                        else:
                            summed.wait_before(v, i, 4 * PR + c - 3)
                        nc.vector.tensor_scalar(S[:, u, :], iota_f[:, :], dst_f[:, bass.ds(t, 1)], None, ALU.is_equal)
                        nc.vector.tensor_tensor(msg[:, u, :].rearrange("p (h r) -> p h r", r=ROW),
                                                rows[:, q, e, :].rearrange("p (h r) -> p h r", r=ROW),
                                                E_all[:, bass.ds(t, 1), :].rearrange("p o h -> p (o h)").unsqueeze(2)
                                                .to_broadcast([P, H, ROW]), ALU.mult).then_inc(msg_ready.sem, 1)
                        if e >= 2:
                            add(e - 2)
                    add(PR - 2)
                    add(PR - 1)
            turns(v, TB, second)

        @block.scalar
        def _(s):
            MIX.act_start(s)

            def body(i):
                for q in groups(i):
                    u, g = q % 2, 4 * i + q
                    MIX.act(s, i, q)
                    scT_ready.wait(s, i, q + 1)
                    if q < 2:
                        sat_stored[u].wait_before(s, i, 2)
                    else:
                        sat_stored[u].wait(s, i, 1)
                    nc.scalar.activation(satb[:, u, :], pb[7][:, u * P:(u + 1) * P], ACT.Copy).then_inc(scT_out.sem, 1)
                    scT_out.wait(s, i, q + 1)
                    s.dma_start(sat_d[:, bass.ds(g * EG, EG), :].rearrange("h t e -> t h e"),
                                satb[:, u, :]).then_inc(sat_stored[u].sem, 16)
            all_turns(s, body)
            s.dma_start(sat_d[:, ET:VT, :], A["zeros"]).then_inc(sat_stored[1].sem, 16)
            MIX.rest(MIX.act, s, TA - 1, groups(TA - 1))
            s.wait_ge(MIX.fx_stored.sem, 16 * NB)
            s.wait_ge(MIX.fx_sq.sem, 4 * NB)
            s.sem_inc(mixed, 1)
            for k in range(4):
                W4 = CH // 4
                s.wait_ge(shifted, k + 1)
                nc.scalar.activation(score[:, k * W4:(k + 1) * W4], score[:, k * W4:(k + 1) * W4], ACT.Exp)\
                    .then_inc(weighed, 1)

        @block.tensor
        def _(pe):
            for j in range(3):
                pe.wait_ge(x_built, j + 1)
                if j:
                    pe.wait_ge(x_used, j)
                for e in range(EG):
                    ins = nc.tensor.matmul(pb[6][:, e * H:(e + 1) * H], st[:, e, :], L["sd_nodes"][:, j * EG + e + 1, :],
                                           start=True, stop=True)
                ins.then_inc(x_sde, 1)
            pe.wait_ge(x_used, 3)
            MIX.pe_start(pe)

            def body(i):
                for q in groups(i):
                    u, g = q % 2, 4 * i + q
                    nts = []
                    for k in range(4):
                        t4 = pe.value_load(L["nt_pack"][0:1, bass.ds(g * 4 + k, 1)], min_val=0, max_val=NT ** 4 - 1)
                        for e in range(4):
                            nts.append(pe.snap(t4 % NT))
                            if e < 3:
                                t4 = pe.snap(t4 // NT)
                    st_built.wait(pe, i, q + 1)
                    if q:
                        sde_used.wait(pe, i, q)
                    else:
                        sde_used.wait_before(pe, i, 4)
                    for e in range(EG):
                        ins = nc.tensor.matmul(pb[6][:, u * P + e * H:u * P + (e + 1) * H], st[:, e, :],
                                               L["sd_nodes"][:, bass.ds(nts[e], 1), :], start=True, stop=True)
                    ins.then_inc(sde_ready.sem, 1)
                    MIX.pe(pe, i, q)
                    score_ready.wait(pe, i, q + 1)
                    if q:
                        scT_out.wait(pe, i, q)
                    else:
                        scT_out.wait_before(pe, i, 4)
                    nc.tensor.transpose(pb[7][:, u * P:(u + 1) * P], edge_pre[:, u, :], ident[:, :])\
                        .then_inc(scT_ready.sem, 1)
            all_turns(pe, body)
            MIX.rest(MIX.pe, pe, TA - 1, groups(TA - 1))
            for k in range(2):
                pe.wait_ge(diag_ready, k + 1)
                for j in range(3):
                    ins = nc.tensor.matmul(pb[5][:, j * P:(j + 1) * P], ones[:, :], carry[:, j, :], start=True, stop=True)
                ins.then_inc(diag_sum, 1)
            for i in range(TA):
                u = i % 2
                pe.wait_ge(et_in[u].sem, 64 * (i // 2) + 16 * len(groups(i)))
                if i > 1:
                    pe.wait_ge(etT_out.sem, i - 1)
                for k in groups(i):
                    ins = nc.tensor.transpose(pb[6 + u][:, k * P:(k + 1) * P], etb[:, u, k, :], ident[:, :])
                ins.then_inc(etT_ready.sem, 1)

            def second(i):
                for c in range(4 * PR):
                    u = c % 4
                    msg_ready.wait(pe, i, c + 1)
                    if c >= 4:
                        added.wait(pe, i, c - 3)
                    else:
                        added.wait_before(pe, i, 4 * PR + c - 3)
                    nc.tensor.matmul(pb[u][:, 0:TAB], S[:, u, :], msg[:, u, :], start=True, stop=True)\
                        .then_inc(summed.sem, 1)
            turns(pe, TB, second)


T2 = NT + 1
PAIRS = T2 // 2
FT = PAIRS // 2
CTRL_TIES = 6


def combine_and_ffn(nc, ctx, sem, L, out):
    A, pb, ident, ones, sc = L["A"], L["pb"], L["ident"], L["ones"], L["sc"]
    acc = L["r1"][:, 0:T2 * TAB].rearrange("p (t d) -> p t d", d=TAB)
    area = L["Area"](L["r2"])
    h1 = area.take(HC, 512)
    xT = area.take(KD, 512)
    tri = area.take(P)
    xs = area.take(BLK, D)
    area = L["Area"](L["r3"])
    xn2 = area.take(NTP, D)
    cmp = area.take(15, T2)
    area = L["Area"](L["r4"])
    xb, fb = area.take(2, 2 * D), area.take(2, 2 * D)
    wk, ek = area.take(2, 2 * D), area.take(2, 2 * D)
    digits = area.take(15)
    area = L["Area"](L["E_all"][:, :, :].rearrange("p t h -> p (t h)"))
    w1 = area.take(KD, HF)
    w2 = area.take(HC, D)
    grow, brow, wrow, b2row = (area.take(D) for _ in range(4))
    b1 = area.take(HC)
    br = area.take(1)
    rec = area.take(T2, H)
    stats = area.take(T2, 6)
    wts, key_hi, key_lo, sel, wsel, t0, t1 = (area.take(T2) for _ in range(7))
    ki, km = area.take(T2, dt=I32), area.take(T2, dt=I32)
    cand, cnt, tot = area.take(15), area.take(15), area.take(15)
    base, need, top = area.take(1), area.take(1), area.take(1)

    c = lambda name, per, by=1: Count(sem(name), per, by)
    w_in = sem("ffn_w_in")
    dve3 = sem("dve3")
    tri_set = sem("tri_set")
    xn_in = [c(f"xn_in{u}", 1, 16) for u in range(2)]
    xf_in = [c(f"xf_in{u}", 2, 16) for u in range(2)]
    c1_used, c2_min, c2_exp, c2_used = c("c1_used", 2), c("c2_min", 2), c("c2_exp", 2), c("c2_used", 2)
    fx_root, fx_tanh, fx_n = sem("fx_root"), sem("fx_tanh"), sem("fx_n")
    var1, std1, var2, std2 = sem("var1"), sem("std1"), sem("var2"), sem("std2")
    x2_ready = sem("x2_ready")
    xT2_ready, xT2_out = c("xT2_ready", 2), c("xT2_out", 2)
    xs_ready, c3_done = c("xs_ready", 1), c("c3_done", 2)
    h_mm, h_gelu = c("h_mm", HC), c("h_gelu", HC)
    y_mm, y_out = c("y_mm", BLK), c("y_out", BLK)
    counted, count_all = sem("counted"), sem("count_all")
    ties_ready, ties = sem("ties_ready"), sem("ties")
    final, out_stored = c("final", BLK), sem("out_stored")
    NFB = (T2 + BLK - 1) // BLK

    def pairs(i):
        return (0, 1) if not isinstance(i, int) or i < FT else (0,)

    def all_pairs(eng, body):
        body(0)
        with eng.Fori(1, FT) as i:
            body(i)
        body(FT)

    def tiles(i):
        return range(BLK) if not isinstance(i, int) or i < NFB - 1 else range(T2 - BLK * (NFB - 1))

    def all_blocks(eng, body, between=None):
        body(0)
        if between:
            with eng.Fori(1, CTRL_TIES) as i:
                body(i)
            between()
            with eng.Fori(CTRL_TIES, NFB - 1) as i:
                body(i)
        else:
            with eng.Fori(1, NFB - 1) as i:
                body(i)
        body(NFB - 1)

    with nc.Block() as block:
        @block.sync
        def _(sp):
            def c1(i):
                for u in pairs(i):
                    c1_used.wait_before(sp, i, u + 1)
                    sp.dma_start(xb[:, u, :], L["xn_d"][bass.ds(4 * i + 2 * u, 2), :, :].rearrange("t p d -> p t d"))\
                        .then_inc(xn_in[u].sem, 16)
            all_pairs(sp, c1)
            sp.dma_start(w1, A["w1"].rearrange("(k p) n -> p k n", p=P)).then_inc(w_in, 16)
            sp.dma_start(w2, A["w2"].rearrange("(k p) n -> p k n", p=P)).then_inc(w_in, 16)
            for dst, name, n in ((grow, "gamma", D), (brow, "beta", D), (wrow, "wr", D), (b2row, "b2", D), (br, "br", 1)):
                sp.dma_start(dst, A[name].to_broadcast([P, n])).then_inc(w_in, 16)
            sp.dma_start(b1, A["b1"]).then_inc(w_in, 16)
            sp.wait_ge(c1_used.sem, PAIRS)

            def c2(i):
                for u in pairs(i):
                    c2_used.wait_before(sp, i, u + 1)
                    sp.dma_start(xb[:, u, :], A["x"].rearrange("(t p) d -> p t d", p=P)[:, bass.ds(4 * i + 2 * u, 2), :])\
                        .then_inc(xf_in[u].sem, 16)
                    sp.dma_start(fb[:, u, :], L["fx_d"][bass.ds(4 * i + 2 * u, 2), :, :].rearrange("t p d -> p t d"))\
                        .then_inc(xf_in[u].sem, 16)
            all_pairs(sp, c2)

            def store(i):
                n = len(tiles(i))
                final.wait(sp, i, n)
                sp.dma_start(out.rearrange("(t p) d -> p t d", p=P)[:, bass.ds(BLK * i, n), :],
                             acc[:, bass.ds(BLK * i, n), 0:D]).then_inc(out_stored, 16)
            all_blocks(sp, store)
            sp.wait_ge(out_stored, 16 * NFB)

        @block.gpsimd
        def _(g):
            g.memset(tri, 1.0).then_inc(tri_set, 1)
            g.wait_ge(tri_set, 1)
            g.affine_select(out=tri, in_=tri, compare_op=ALU.is_gt, fill=0.0, base=0, pattern=[[1, P]],
                            channel_multiplier=-1).then_inc(tri_set, 1)
            for k in range(9):
                g.wait_ge(counted, k + 1)
                g.partition_all_reduce(tot, cnt, P, bass.bass_isa.ReduceOp.add).then_inc(count_all, 1)

        @block.vector
        def _(v_):
            v = nc.vector
            ch = Chain(v_, dve3)
            n, f = sc[:, 5, :], sc[:, 6, :]
            v.wait_ge(fx_root, 1)
            v.tensor_scalar(n, n, MINN, None, ALU.max).then_inc(fx_n, 1)
            ch.do(v.tensor_scalar(rec, acc[:, :, HD::ROW], 1e-30, None, ALU.max))
            ch.do(v.reciprocal(rec, rec))
            v.wait_ge(fx_tanh, 1)
            ch.do(v.tensor_scalar(f, f, MAXN, None, ALU.min))
            ch.do(v.reciprocal(n, n))
            ch.do(v.tensor_tensor(f, f, n, ALU.mult))

            def t4(i, u):
                return bass.ds(4 * i + 2 * u, 2)

            def two(ap):
                return ap.rearrange("p (t d) -> p t d", d=D)

            def c1(i):
                ch.turn(i, 4)
                for u in pairs(i):
                    a = acc[:, t4(i, u), :]
                    ch.do(v.tensor_tensor(wk[:, u, :].rearrange("p (t h d) -> p t h d", h=H, d=HD),
                                          a.rearrange("p t (h r) -> p t h r", r=ROW)[:, :, :, 0:HD],
                                          rec[:, t4(i, u), :].unsqueeze(3).to_broadcast([P, 2, H, HD]), ALU.mult))
                    xn_in[u].wait(v_, i, 1)
                    ch.do(v.tensor_tensor(a[:, :, 0:D], two(wk[:, u, :]), two(xb[:, u, :]), ALU.add))
                    for k in range(2):
                        t = bass.ds(4 * i + 2 * u + k, 1)
                        ins = v.bn_stats(stats[:, t, :], acc[:, t, 0:D])
                        if k:
                            ins.then_inc(c1_used.sem, 1)
            ch.loop()
            all_pairs(v_, c1)
            v_.wait_ge(c1_used.sem, PAIRS)
            row_moments(nc, ch, stats, sc, T2)
            v.tensor_scalar(sc[:, 3, 0:T2], sc[:, 3, 0:T2], 1e-5, None, ALU.add).then_inc(var1, 1)
            v_.wait_ge(std1, 1)
            ch.do(v.reciprocal(sc[:, 3, 0:T2], sc[:, 4, 0:T2]))
            v_.wait_ge(w_in, 8 * 16)

            def c2(i):
                ch.turn(i, 16)
                for u in pairs(i):
                    for k in range(2):
                        t = bass.ds(4 * i + 2 * u + k, 1)
                        ch.step(v.tensor_scalar(wk[:, u, k * D:(k + 1) * D], acc[:, t, 0:D].rearrange("p o d -> p (o d)"),
                                                sc[:, 2, t], sc[:, 3, t], ALU.subtract, ALU.mult))
                    ch.done()
                    w = two(wk[:, u, :])
                    ch.do(v.tensor_tensor(w, w, grow.unsqueeze(1).to_broadcast([P, 2, D]), ALU.mult))
                    ch.do(v.tensor_tensor(w, w, brow.unsqueeze(1).to_broadcast([P, 2, D]), ALU.add))
                    v.tensor_scalar(ek[:, u, :], wk[:, u, :], 0.0, None, ALU.min).then_inc(c2_min.sem, 1)
                for u in pairs(i):
                    w = wk[:, u, :]
                    c2_exp.wait(v_, i, u + 1)
                    ch.do(v.scalar_tensor_tensor(w, w, 0.0, ek[:, u, :], ALU.max, ALU.add))
                    xf_in[u].wait(v_, i, 2)
                    ch.do(v.scalar_tensor_tensor(w, w, -1.0, xb[:, u, :], ALU.add, ALU.add))
                    for k in range(2):
                        t = bass.ds(4 * i + 2 * u + k, 1)
                        cs = slice(k * D, (k + 1) * D)
                        ch.step(v.scalar_tensor_tensor(acc[:, t, 0:D].rearrange("p o d -> p (o d)"), fb[:, u, cs],
                                                       sc[:, 6, t], wk[:, u, cs], ALU.mult, ALU.add))
                    ch.done()
                    for k in range(2):
                        t = bass.ds(4 * i + 2 * u + k, 1)
                        ins = v.bn_stats(stats[:, t, :], acc[:, t, 0:D])
                        if k:
                            ins.then_inc(c2_used.sem, 1)
            ch.loop()
            all_pairs(v_, c2)
            v_.wait_ge(c2_used.sem, PAIRS)
            row_moments(nc, ch, stats, sc, T2)
            v.tensor_scalar(sc[:, 3, 0:T2], sc[:, 3, 0:T2], 1e-5, None, ALU.add).then_inc(var2, 1)
            v_.wait_ge(std2, 1)
            ch.do(v.reciprocal(sc[:, 3, 0:T2], sc[:, 4, 0:T2]))

            def c3(i):
                ch.turn(i, 4)
                for u in pairs(i):
                    for k in range(2):
                        t = bass.ds(4 * i + 2 * u + k, 1)
                        v.tensor_scalar(xn2[:, t, :], acc[:, t, 0:D], sc[:, 2, t], sc[:, 3, t], ALU.subtract, ALU.mult)\
                            .then_inc(x2_ready, 1)
                    v_.wait_ge(x2_ready, 4 * i + 2 * u + 2)
                    tt = t4(i, u)
                    ch.do(v.tensor_tensor(two(wk[:, u, :]), xn2[:, tt, :], wrow.unsqueeze(1).to_broadcast([P, 2, D]), ALU.mult))
                    ch.step(v.reduce_sum(wts[:, tt], two(wk[:, u, :]), mybir.AxisListType.X))
                    v.tensor_tensor(acc[:, tt, 0:D], acc[:, tt, 0:D], xn2[:, tt, :], ALU.add).then_inc(c3_done.sem, 1)
            ch.do(v.memset(xn2[:, T2:NTP, :], 0.0))
            ch.loop()
            all_pairs(v_, c3)
            ch.done()
            v_.wait_ge(c3_done.sem, PAIRS)
            v_.sem_inc(c3_done.sem, 1)
            ch.do(v.tensor_scalar(wts, wts, br, None, ALU.add))
            wbits = wts.bitcast(I32)
            ch.do(v.tensor_single_scalar(km, wbits, 31, op=ALU.arith_shift_right))
            ch.do(v.tensor_single_scalar(km, km, 0x7FFFFFFF, op=ALU.bitwise_and))
            ch.do(v.tensor_tensor(ki, wbits, km, ALU.bitwise_xor))
            ch.do(v.tensor_single_scalar(km, ki, 16, op=ALU.arith_shift_right))
            ch.do(v.tensor_copy(key_hi, km))
            ch.do(v.tensor_single_scalar(km, ki, 0xFFFF, op=ALU.bitwise_and))
            ch.do(v.tensor_copy(key_lo, km))
            ch.do(v.tensor_scalar(key_hi, key_hi, 32768.0, None, ALU.add))
            ch.do(v.memset(key_hi[:, NT:T2], -1.0))
            last = key_hi[:, NT - 1:NT]
            ch.do(v.tensor_scalar(t0[:, 0:1], L["pcol"][:, 0:1], float(N - (NT - 1) * P), None, ALU.is_lt))
            ch.do(v.tensor_scalar(last, last, 1.0, t0[:, 0:1], ALU.add, ALU.mult))
            ch.do(v.tensor_scalar(last, last, -1.0, None, ALU.add))
            ch.do(v.tensor_scalar(digits, L["iota_f"][:, 1:16], 1.0, None, ALU.mult))
            rounds = [0]

            def count(k):
                ch.done()
                v_.sem_inc(counted, 1)
                v_.wait_ge(count_all, k + 1)

            def search(keys, half):
                ch.do(v.memset(base, 0.0))
                for r in range(4):
                    step = float(16 ** (3 - r))
                    ch.do(v.tensor_scalar(cand, digits, step, base, ALU.mult, ALU.add))
                    ch.do(v.tensor_tensor(cmp, keys.unsqueeze(1).to_broadcast([P, 15, T2]),
                                          cand.unsqueeze(2).to_broadcast([P, 15, T2]), ALU.is_ge))
                    ch.do(v.reduce_sum(cnt, cmp, mybir.AxisListType.X))
                    count(4 * half + r)
                    ch.do(v.tensor_scalar(cand, tot, float(KSEL), None, ALU.is_ge))
                    ch.do(v.reduce_sum(need, cand, mybir.AxisListType.X))
                    ch.do(v.scalar_tensor_tensor(base, need, step, base, ALU.mult, ALU.add))
            search(key_hi, 0)
            ch.step(v.tensor_scalar(t0, key_hi, base, None, ALU.is_equal))
            ch.do(v.tensor_scalar(t1, key_hi, base, 1.0e6, ALU.is_gt, ALU.mult))
            ch.do(v.tensor_scalar(key_lo, key_lo, 1.0, None, ALU.add))
            ch.do(v.tensor_tensor(key_lo, key_lo, t0, ALU.mult))
            ch.do(v.tensor_tensor(key_lo, key_lo, t1, ALU.add))
            ch.do(v.tensor_scalar(key_lo, key_lo, -1.0, None, ALU.add))
            search(key_lo, 1)
            ch.step(v.tensor_scalar(sel, key_lo, base, None, ALU.is_gt))
            ch.step(v.tensor_scalar(t0, key_lo, base, None, ALU.is_equal))
            ch.step(v.memset(cnt, 0.0))
            ch.done()
            ch.do(v.reduce_sum(cnt[:, 0:1], sel, mybir.AxisListType.X))
            count(8)
            ch.do(v.tensor_scalar(need, tot[:, 0:1], -1.0, float(KSEL), ALU.mult, ALU.add))
            v_.sem_inc(ties_ready, 1)
            v_.wait_ge(ties, 1)
            ch.do(v.tensor_copy(t1, pb[7][:, 0:T2]))
            ch.do(v.tensor_tensor_scan(key_hi, t1, t1, 0.0, ALU.add, ALU.max))
            ch.do(v.tensor_tensor(key_hi, key_hi, t1, ALU.subtract))
            ch.do(v.tensor_tensor(key_hi, key_hi, pb[6][:, 0:T2], ALU.add))
            ch.do(v.tensor_scalar(key_hi, key_hi, need, None, ALU.is_lt))
            ch.do(v.tensor_tensor(key_hi, key_hi, t0, ALU.mult))
            ch.do(v.tensor_tensor(sel, sel, key_hi, ALU.add))
            ch.do(v.tensor_tensor(wsel, sel, wts, ALU.mult))

            def last_sum(i):
                for j in tiles(i):
                    t = bass.ds(BLK * i + j, 1)
                    a = acc[:, t, 0:D].rearrange("p o d -> p (o d)")
                    ch.turn(i, BLK)
                    ch.k = j
                    ch.do(v.scalar_tensor_tensor(a, b2row, wsel[:, t], a, ALU.mult, ALU.add))
                    y_out.wait(v_, i, j + 1)
                    v.scalar_tensor_tensor(a, xn2[:, t, :].rearrange("p o d -> p (o d)"), wsel[:, t], a, ALU.mult, ALU.add)\
                        .then_inc(final.sem, 1)
            ch.loop()
            all_blocks(v_, last_sum)

        @block.scalar
        def _(s):
            act = nc.scalar.activation
            act(sc[:, 5, :], sc[:, 9, :], ACT.Sqrt).then_inc(fx_root, 1)
            s.wait_ge(fx_n, 1)
            act(sc[:, 6, :], sc[:, 5, :], ACT.Tanh).then_inc(fx_tanh, 1)
            s.wait_ge(var1, 1)
            act(sc[:, 4, 0:T2], sc[:, 3, 0:T2], ACT.Sqrt).then_inc(std1, 1)

            def c2(i):
                for u in pairs(i):
                    c2_min.wait(s, i, u + 1)
                    act(ek[:, u, :], ek[:, u, :], ACT.Exp).then_inc(c2_exp.sem, 1)
            all_pairs(s, c2)
            s.wait_ge(var2, 1)
            act(sc[:, 4, 0:T2], sc[:, 3, 0:T2], ACT.Sqrt).then_inc(std2, 1)
            s.wait_ge(w_in, 8 * 16)

            def fetch(b):
                c3_done.wait(s, b, 2)
                act(xs, xn2[:, bass.ds(BLK * b, BLK), :], ACT.Copy).then_inc(xs_ready.sem, 1)

            def transposed(b):
                for k in range(KD):
                    xT2_ready.wait(s, b, k + 1)
                    act(xT[:, k, :], pb[k][:, :], ACT.Copy).then_inc(xT2_out.sem, 1)

            def ffn(i):
                w = P * len(tiles(i))
                y_mm.wait_before(s, i, BLK)
                for m in range(HC):
                    h_mm.wait(s, i, m + 1)
                    act(h1[:, m, 0:w], pb[2 + m % 2][:, 0:w], ACT.Gelu_apprx_tanh, bias=b1[:, m:m + 1])\
                        .then_inc(h_gelu.sem, 1)
                if not (isinstance(i, int) and i == NFB - 1):
                    xT2_ready.wait(s, i, KD)
                    fetch(i + 1)
                    transposed(i + 1)
                for j in tiles(i):
                    y_mm.wait(s, i, j + 1)
                    act(xn2[:, bass.ds(BLK * i + j, 1), :].rearrange("p o d -> p (o d)"), pb[4 + j % 2][:, 0:D], ACT.Copy)\
                        .then_inc(y_out.sem, 1)
            fetch(0)
            transposed(0)
            all_blocks(s, ffn)

        @block.tensor
        def _(pe):
            mm = nc.tensor.matmul
            pe.wait_ge(w_in, 8 * 16)

            def transposes(b):
                xs_ready.wait(pe, b, 1)
                for k in range(KD):
                    for j in range(BLK):
                        ins = nc.tensor.transpose(pb[k][:, j * P:(j + 1) * P], xs[:, j, k * P:(k + 1) * P], ident[:, :])
                    ins.then_inc(xT2_ready.sem, 1)

            def ffn(i):
                w = P * len(tiles(i))
                for m in range(HC):
                    xT2_out.wait(pe, i, 2)
                    if m >= 2:
                        h_gelu.wait(pe, i, m - 1)
                    else:
                        h_gelu.wait_before(pe, i, HC + m - 1)
                    for k in range(KD):
                        ins = mm(pb[2 + m % 2][:, 0:w], w1[:, k, m * P:(m + 1) * P], xT[:, k, 0:w], start=k == 0, stop=k == 1)
                    ins.then_inc(h_mm.sem, 1)
                if not (isinstance(i, int) and i == NFB - 1):
                    transposes(i + 1)
                h_gelu.wait(pe, i, HC)
                for j in tiles(i):
                    if j >= 2:
                        y_out.wait(pe, i, j - 1)
                    else:
                        y_out.wait_before(pe, i, BLK + j - 1)
                    for m in range(HC):
                        ins = mm(pb[4 + j % 2][:, 0:D], h1[:, m, j * P:(j + 1) * P], w2[:, m, :], start=m == 0,
                                 stop=m == HC - 1)
                    ins.then_inc(y_mm.sem, 1)

            def count_ties():
                pe.wait_ge(tri_set, 2)
                pe.wait_ge(ties_ready, 1)
                mm(pb[6][:, 0:T2], tri, t0, start=True, stop=True)
                mm(pb[7][:, 0:T2], ones[:, :], t0, start=True, stop=True).then_inc(ties, 1)
            transposes(0)
            all_blocks(pe, ffn, count_ties)


def kernel(x, src, dst, L0_gnn_W, L0_gnn_a_src, L0_gnn_a_dst, L0_gnn_gamma, L0_gnn_beta, L0_mix_w_qkv,
           L0_mix_bn_gamma, L0_mix_bn_beta, L0_mix_w_dw, L0_mix_w_pw, L0_mix_w_res, L0_mix_b_res,
           L0_ffn_attention_mask, L0_ffn_wr, L0_ffn_br, L0_ffn_w1, L0_ffn_b1, L0_ffn_w2, L0_ffn_b2):
    import concourse.bacc as bacc
    from concourse.bass_utils import run_bass_kernel_spmd

    def arr(a):
        return np.ascontiguousarray(a)

    x_pad = np.zeros((NTP * P, D), np.float32)
    x_pad[:N] = x
    src_pad = np.zeros((VT + 2 * EG) * P, np.int32)
    src_pad[:E] = src
    dst_pad = np.full(VT * P + 2, PAD_DST, np.int32)
    dst_pad[0] = -1
    dst_pad[-1] = -2
    dst_pad[1:E + 1] = dst
    dst_main = dst_pad[1:-1]
    chunks = np.lib.stride_tricks.as_strided(dst_pad, (16, CH + 2), (CH * 4, 4))

    def by_role(w):
        return arr(np.asarray(w).reshape((8, 3, 32) + w.shape[1:]).swapaxes(0, 1).reshape((NQ,) + w.shape[1:]))

    pw = by_role(np.asarray(L0_mix_w_pw)[:, :, 0]).reshape(QC, 4, 32, 32)
    arrays = {
        "x": x_pad,
        "src_cols": arr(src_pad.reshape(-1, P).T),
        "dst_cols": arr(dst_main.reshape(VT, P).T),
        "dst_flat": arr(dst_main.reshape(1, VT * P)),
        "dst_chunks": arr(chunks),
        "first": arr(dst_main.reshape(VT, P)[:ET, 0].reshape(1, ET)),
        "W": arr(L0_gnn_W),
        "a_src": arr(L0_gnn_a_src).reshape(1, D),
        "a_dst": arr(L0_gnn_a_dst).reshape(1, D),
        "gamma": arr(L0_gnn_gamma).reshape(1, D),
        "beta": arr(L0_gnn_beta).reshape(1, D),
        "w_qkv": arr(by_role(np.asarray(L0_mix_w_qkv)[:, :, 2]).T),
        "bn_gamma": arr(by_role(L0_mix_bn_gamma).reshape(QC, P).T),
        "bn_beta": arr(by_role(L0_mix_bn_beta).reshape(QC, P).T),
        "w_dw": arr(by_role(np.asarray(L0_mix_w_dw)[:, 0, 2]).reshape(QC, P).T),
        "w_pw": arr(pw.transpose(1, 3, 0, 2).reshape(P, QC, 32)),
        "w_res": arr(np.asarray(L0_mix_w_res)[:, :, 0].T),
        "b_res": arr(L0_mix_b_res).reshape(1, D),
        "wr": arr(L0_ffn_wr).reshape(1, D),
        "br": arr(L0_ffn_br).reshape(1, 1),
        "w1": arr(L0_ffn_w1),
        "b1": arr(np.asarray(L0_ffn_b1).reshape(HC, P).T),
        "w2": arr(L0_ffn_w2),
        "b2": arr(L0_ffn_b2).reshape(1, D),
        "zeros": np.zeros((H, VT - ET, P), np.float32),
    }
    nc = bacc.Bacc("TRN2", target_bir_lowering=False, num_devices=1)
    A = {}
    for name, a in arrays.items():
        A[name] = nc.dram_tensor(name, a.shape, mybir.dt.from_np(a.dtype), kind="ExternalInput").ap()
    out = nc.dram_tensor("out", [T2 * P, D], F32, kind="ExternalOutput").ap()
    build(nc, A, out)
    r = run_bass_kernel_spmd(nc, [arrays], core_ids=[0])
    return np.asarray(r.results[0]["out"])[:N]
```

```python
from contextlib import ExitStack

import numpy as np

import concourse.bass as bass
from concourse import mybir

F32 = mybir.dt.float32
I32 = mybir.dt.int32
BF16 = mybir.dt.bfloat16
ALU = mybir.AluOpType
ACT = mybir.ActivationFunctionType

P = 128
N = 6250
D = 256
KD = D // P
E = 100000
H = 8
HD = D // H
ROW = HD + 1
TAB = H * ROW
NT = -(-N // P)
BLK = 4
NB = -(-NT // BLK)
NTP = NB * BLK
ET = -(-E // (16 * P)) * 16
EG = 16
NG = ET // EG
VT = ET + NT - 1
VG = VT // EG
CH = VT * P // 16
NQ = 3 * D
QC = NQ // P
HF = 4 * D
HC = HF // P
PAD_DST = 1000000
BIG = 1.0e30
MAXN = float(np.float32(1.0 - 1e-5))
CAP = float(np.arctanh(np.float64(MAXN)))
MINN = 1e-15
KSEL = N // 2 - 1

assert VT % EG == 0 and VT == 832 and NTP * P == 512 * NB


class Count:

    def __init__(self, sem, per, by=1):
        self.sem, self.per, self.by = sem, per, by

    def wait(self, eng, i, c):
        eng.wait_ge(self.sem, (i * self.per + c) * self.by)

    def wait_before(self, eng, i, c):
        if not (isinstance(i, int) and i == 0):
            eng.wait_ge(self.sem, ((i - 1) * self.per + c) * self.by)


class Chain:

    def __init__(self, eng, sem):
        self.eng, self.sem, self.base, self.k = eng, sem, 0, 0

    def turn(self, i, per):
        self.base, self.k = self.start + i * per, 0

    def loop(self):
        self.start, self.base, self.k = self.base + self.k, self.base + self.k, 0

    def end(self, turns, per):
        assert self.k == per, (self.k, per)
        self.base, self.k = self.start + turns * per, 0

    def step(self, ins):
        ins.then_inc(self.sem, 1)
        self.k += 1

    def done(self):
        self.eng.wait_ge(self.sem, self.base + self.k)

    def do(self, ins):
        self.step(ins)
        self.done()


def turns(eng, n, body):
    body(0)
    if n > 1:
        with eng.Fori(1, n) as i:
            body(i)


def build(nc, A, out):
    with ExitStack() as ctx:
        def sb(name, shape, dt=F32):
            return ctx.enter_context(nc.sbuf_tensor(name, shape, dt))

        def sem(name):
            return ctx.enter_context(nc.semaphore(name))

        def dram(name, shape, dt=F32):
            return nc.dram_tensor(name, shape, dt).ap()

        table_d = dram("table_d", [NTP * P, TAB])
        ssrc_d = dram("ssrc_d", [NTP * P, H])
        xn_d = dram("xn_d", [NTP, P, D])
        fx_d = dram("fx_d", [NTP, P, D])
        sat_d = dram("sat_d", [H, VT, P])
        et_d = dram("et_d", [H, VT, P])

        pb = [ctx.enter_context(nc.psum_tensor(f"bank{i}", [P, 512], F32)) for i in range(8)]

        ident = sb("ident", [P, P])
        ones = sb("ones", [P, P])
        iota_f = sb("iota_f", [P, P])
        pcol = sb("pcol", [P, 2])
        src_sb = sb("src_sb", [P, VT + 2 * EG], I32)
        dst_f = sb("dst_f", [P, VT])
        nt_f = sb("nt_f", [P, VT])
        nodecol = sb("nodecol", [P, VT])
        nt_pack = sb("nt_pack", [1, VT // 4], I32)
        tau_i = sb("tau_i", [1, NT - 1], I32)
        never = sb("never", [P, NT - 1])
        sc = sb("sc", [P, 12, NTP])
        sd_nodes = sb("sd_nodes", [P, NTP, 3 * H], BF16)
        E_all = sb("E_all", [P, VT, H])
        idx = sb("idx", [P, 4, EG], I32)
        grab = sb("grab", [P, 4, EG, H])

        r1 = sb("r1", [P, NTP * D + 8])
        r2 = sb("r2", [P, CH + 8])
        r3 = sb("r3", [P, 13700])
        r4 = sb("r4", [P, 4640])
        xn = r1[:, 0:NTP * D].rearrange("p (t d) -> p t d", d=D)
        sde = r2[:, 0:CH].rearrange("p (t h) -> p t h", h=H)

        class Area:
            def __init__(self, region):
                self.region, self.at = region, 0

            def take(self, *shape, dt=F32):
                n = int(np.prod(shape))
                v = self.region[:, self.at:self.at + n]
                self.at += n
                if dt != F32:
                    v = v.bitcast(dt)
                if len(shape) == 2:
                    v = v.rearrange("p (a b) -> p a b", b=shape[1])
                elif len(shape) == 3:
                    v = v.rearrange("p (a b c) -> p a b c", b=shape[1], c=shape[2])
                return v

        prologue(nc, ctx, sem, locals())
        edges_and_mix(nc, ctx, sem, locals())
        combine_and_ffn(nc, ctx, sem, locals(), out)


def prologue(nc, ctx, sem, L):
    A, pb, ident, ones, xn, sc = L["A"], L["pb"], L["ident"], L["ones"], L["xn"], L["sc"]
    iota_f, pcol, dst_f, nt_f, nodecol = (L[k] for k in ("iota_f", "pcol", "dst_f", "nt_f", "nodecol"))
    area = L["Area"](L["r3"])
    W_sb = area.take(KD, D + 2 * H)
    a_sb = area.take(2, D)
    wa_tmp = area.take(D)
    xr = area.take(2, D)
    xnT = area.take(2, D)
    trow = area.take(2, TAB)
    srow = area.take(2, H)
    sd = area.take(NTP, H)
    junk = area.take(2, D)
    stats = area.take(NTP, 6)
    first_i = area.take(ET, dt=I32)
    cmp = area.take(ET)
    dst_i = area.take(VT, dt=I32)
    iota_i = area.take(P, dt=I32)
    pcol_i = area.take(1, dt=I32)
    cnt = area.take(1)
    cntd = area.take(NT - 1)
    pack_f = area.take(VT // 4)
    tau_f = area.take(NT - 1)

    x_in = [sem(f"x_in{j}") for j in range(4)]
    w_in, edge_in = sem("w_in"), sem("edge_in")
    const_set, iota_set = sem("const_set"), sem("iota_set")
    dve_pro = sem("dve_pro")
    var_ready, std_ready = sem("var_ready"), sem("std_ready")
    xn_ready = sem("xn_ready")
    wa_ready = sem("wa_ready")
    xT_ready, xT_out = Count(sem("xT_ready"), 2), Count(sem("xT_out"), 2)
    proj_ready, proj_out = Count(sem("proj_ready"), 2), Count(sem("proj_out"), 2)
    stored = [Count(sem(f"row_stored{u}"), 2, 16) for u in range(2)]
    xn_stored = sem("xn_stored")
    squares, xr_ready = Count(sem("squares"), 2), Count(sem("xr_ready"), 2)
    cnt_ready, cnt_bc = sem("cnt_ready"), sem("cnt_bc")
    TURNS = NTP // 2
    XT = NTP // 4

    with nc.Block() as block:
        @block.sync
        def _(sp):
            for j in range(4):
                sp.dma_start(xn[:, j * XT:(j + 1) * XT, :],
                             A["x"].rearrange("(t p) d -> p t d", p=P)[:, j * XT:(j + 1) * XT, :]).then_inc(x_in[j], 16)
            sp.dma_start(W_sb[:, :, 0:D], A["W"].rearrange("(k p) n -> p k n", p=P)).then_inc(w_in, 16)
            for j, name in enumerate(("a_src", "a_dst")):
                sp.dma_start(a_sb[:, j, :], A[name].to_broadcast([P, D])).then_inc(w_in, 16)
            sp.dma_start(first_i, A["first"].to_broadcast([P, ET])).then_inc(edge_in, 16)
            sp.dma_start(dst_i, A["dst_cols"]).then_inc(edge_in, 16)
            sp.dma_start(L["src_sb"][:, :], A["src_cols"]).then_inc(edge_in, 16)

            def body(i):
                for u in range(2):
                    t = 2 * i + u
                    proj_out.wait(sp, i, u + 1)
                    sp.dma_start(L["table_d"][bass.ds(t * P, P), :], trow[:, u, :]).then_inc(stored[u].sem, 16)
                    sp.dma_start(L["ssrc_d"][bass.ds(t * P, P), :], srow[:, u, :]).then_inc(stored[u].sem, 16)
            turns(sp, TURNS, body)
            sp.wait_ge(xn_ready, NTP)
            sp.dma_start(L["xn_d"].rearrange("t p d -> p t d"), xn).then_inc(xn_stored, 16)
            sp.wait_ge(xn_stored, 16)
            for u in range(2):
                sp.wait_ge(stored[u].sem, TURNS * 32)

        @block.gpsimd
        def _(g):
            nc.gpsimd.memset(ones[:, :], 1.0).then_inc(const_set, 1)
            nc.gpsimd.memset(ident[:, :], 0.0).then_inc(const_set, 1)
            g.wait_ge(const_set, 2)
            nc.gpsimd.affine_select(out=ident[:, :], in_=ident[:, :], compare_op=ALU.not_equal, fill=1.0, base=0,
                                    pattern=[[-1, P]], channel_multiplier=1).then_inc(const_set, 1)
            nc.gpsimd.iota(iota_i, pattern=[[1, P]], base=0, channel_multiplier=0).then_inc(iota_set, 1)
            nc.gpsimd.iota(pcol_i, pattern=[[0, 1]], base=0, channel_multiplier=1).then_inc(iota_set, 1)

        @block.vector
        def _(v):
            ch = Chain(v, dve_pro)
            v.wait_ge(w_in, 48)
            for k in range(KD):
                for j in range(2):
                    ch.do(nc.vector.tensor_tensor(wa_tmp, W_sb[:, k, 0:D], a_sb[:, j, :], ALU.mult))
                    ins = nc.vector.reduce_sum(W_sb[:, k, D + H * j:D + H * (j + 1)],
                                               wa_tmp.rearrange("p (h d) -> p h d", h=H), mybir.AxisListType.X)
                    ch.do(ins)
            nc.vector.memset(trow[:, :, :], 1.0).then_inc(wa_ready, 1)
            for j in range(4):
                v.wait_ge(x_in[j], 16)
            ch.loop()
            with v.Fori(0, NTP // 4) as i:
                ch.turn(i, 4)
                for u in range(4):
                    t = 4 * i + u
                    ch.step(nc.vector.bn_stats(stats[:, bass.ds(t, 1), :], xn[:, bass.ds(t, 1), :]))
            ch.end(NTP // 4, 4)
            ch.done()
            row_moments(nc, ch, stats, sc)
            nc.vector.tensor_scalar(sc[:, 3, :], sc[:, 3, :], 1e-5, None, ALU.add).then_inc(var_ready, 1)
            v.wait_ge(std_ready, 1)
            ch.do(nc.vector.reciprocal(sc[:, 3, :], sc[:, 4, :]))
            with v.Fori(0, NTP // 4) as i:
                for u in range(4):
                    t = 4 * i + u
                    nc.vector.tensor_scalar(xn[:, bass.ds(t, 1), :], xn[:, bass.ds(t, 1), :], sc[:, 2, bass.ds(t, 1)],
                                            sc[:, 3, bass.ds(t, 1)], ALU.subtract, ALU.mult).then_inc(xn_ready, 1)

            def body(i):
                for u in range(2):
                    t = 2 * i + u
                    proj_ready.wait(v, i, u + 1)
                    stored[u].wait_before(v, i, 2)
                    q = pb[2 + u]
                    nc.vector.tensor_copy(trow[:, u, :].rearrange("p (h r) -> p h r", r=ROW)[:, :, 0:HD],
                                          q[:, 0:D].rearrange("p (h d) -> p h d", h=H))
                    nc.vector.tensor_copy(sd[:, bass.ds(t, 1), :],
                                          q[:, D + H:D + 2 * H].rearrange("p (o h) -> p o h", o=1))
                    nc.vector.tensor_copy(srow[:, u, :], q[:, D:D + H]).then_inc(proj_out.sem, 1)
            turns(v, TURNS, body)

            part = L["sd_nodes"][:, :, :].rearrange("p t (k h) -> p t k h", k=3)
            v.wait_ge(proj_out.sem, NTP)
            for k in range(3):
                ch.do(nc.vector.tensor_copy(part[:, :, k, :], sd))
                if k < 2:
                    ch.do(nc.vector.tensor_tensor(sd, sd, part[:, :, k, :], ALU.subtract))

            v.wait_ge(edge_in, 48)
            v.wait_ge(iota_set, 2)
            v.wait_ge(const_set, 3)
            ch.do(nc.vector.tensor_single_scalar(first_i, first_i, 7, op=ALU.arith_shift_right))
            ch.step(nc.vector.tensor_copy(iota_f[:, :], iota_i))
            ch.step(nc.vector.tensor_copy(pcol[:, 0:1], pcol_i))
            ch.do(nc.vector.tensor_scalar(nt_f[:, 0:ET], first_i, float(NT - 1), None, ALU.min))
            ch.step(nc.vector.tensor_copy(nt_f[:, ET:VT], iota_f[:, 1:NT]))
            ch.step(nc.vector.tensor_copy(dst_f[:, :], dst_i))
            ch.do(nc.vector.tensor_scalar(pcol[:, 1:2], pcol[:, 0:1], 1.0, None, ALU.add))
            ch.do(nc.vector.tensor_scalar(cmp, nt_f[:, 0:ET], pcol[:, 1:2], None, ALU.is_lt))
            ch.do(nc.vector.reduce_sum(cnt, cmp, mybir.AxisListType.X))
            nc.vector.tensor_scalar(cntd, ident[:, 0:NT - 1], cnt, None, ALU.mult).then_inc(cnt_ready, 1)
            v.wait_ge(cnt_bc, 1)
            ch.do(nc.vector.tensor_scalar(L["never"][:, :], pb[4][:, 0:NT - 1], 0.5, 1.0e7,
                                          ALU.is_lt, ALU.mult))
            ch.do(nc.vector.tensor_scalar(tau_f, pb[4][:, 0:NT - 1], -1.0, 0.0, ALU.add, ALU.max))
            ch.step(nc.vector.tensor_copy(L["tau_i"][0:1, :], tau_f[0:1, :]))
            ch.do(nc.vector.tensor_scalar(nodecol[:, :], nt_f[:, :], float(P), pcol[:, 0:1], ALU.mult, ALU.add))
            ch.do(nc.vector.tensor_tensor(nodecol[:, ET:VT], nodecol[:, ET:VT], L["never"][:, :], ALU.add))
            four = nt_f[0:1, :].rearrange("p (k j) -> p k j", j=4)
            ch.do(nc.vector.tensor_scalar(pack_f[0:1, :], four[:, :, 3], float(NT), None, ALU.mult))
            for j in (2, 1):
                ch.do(nc.vector.tensor_tensor(pack_f[0:1, :], pack_f[0:1, :], four[:, :, j], ALU.add))
                ch.do(nc.vector.tensor_scalar(pack_f[0:1, :], pack_f[0:1, :], float(NT), None, ALU.mult))
            ch.do(nc.vector.tensor_tensor(pack_f[0:1, :], pack_f[0:1, :], four[:, :, 0], ALU.add))
            ch.do(nc.vector.tensor_copy(L["nt_pack"][0:1, :], pack_f[0:1, :]))
            v.wait_ge(squares.sem, NTP)

        @block.scalar
        def _(s):
            s.wait_ge(var_ready, 1)
            nc.scalar.activation(sc[:, 4, :], sc[:, 3, :], ACT.Sqrt).then_inc(std_ready, 1)

            def body(i):
                for u in range(2):
                    t = 2 * i + u
                    s.wait_ge(xn_ready, t + 1)
                    xT_ready.wait_before(s, i, u + 1)
                    squares.wait_before(s, i, u + 1)
                    nc.scalar.activation(xr[:, u, :], xn[:, bass.ds(t, 1), :].rearrange("p o d -> p (o d)"),
                                         ACT.Copy).then_inc(xr_ready.sem, 1)
                for u in range(2):
                    t = 2 * i + u
                    xr_ready.wait(s, i, u + 1)
                    nc.scalar.activation(junk[:, u, :], xr[:, u, :], ACT.Square,
                                         accum_out=sc[:, 0, bass.ds(t, 1)]).then_inc(squares.sem, 1)
                for u in range(2):
                    xT_ready.wait(s, i, u + 1)
                    proj_ready.wait_before(s, i, u + 1)
                    nc.scalar.activation(xnT[:, u, :], pb[u][:, 0:D], ACT.Copy).then_inc(xT_out.sem, 1)
            turns(s, TURNS, body)

        @block.tensor
        def _(pe):
            pe.wait_ge(const_set, 3)
            pe.wait_ge(wa_ready, 1)

            def body(i):
                for u in range(2):
                    xr_ready.wait(pe, i, u + 1)
                    xT_out.wait_before(pe, i, u + 1)
                    for k in range(KD):
                        ins = nc.tensor.transpose(pb[u][:, k * P:(k + 1) * P],
                                                  xr[:, u, k * P:(k + 1) * P], ident[:, :])
                    ins.then_inc(xT_ready.sem, 1)
                for u in range(2):
                    xT_out.wait(pe, i, u + 1)
                    proj_out.wait_before(pe, i, u + 1)
                    for k in range(KD):
                        ins = nc.tensor.matmul(pb[2 + u][:, 0:D + 2 * H], xnT[:, u, k * P:(k + 1) * P], W_sb[:, k, :],
                                               start=k == 0, stop=k == KD - 1)
                    ins.then_inc(proj_ready.sem, 1)
            turns(pe, TURNS, body)
            pe.wait_ge(cnt_ready, 1)
            nc.tensor.matmul(pb[4][:, 0:NT - 1], ones[:, :], cntd, start=True, stop=True).then_inc(cnt_bc, 1)


def row_moments(nc, ch, stats, sc, T=NTP):
    v = nc.vector
    mean, var, d = sc[:, 2, 0:T], sc[:, 3, 0:T], sc[:, 4, 0:T]
    ch.step(v.tensor_tensor(mean, stats[:, :, 1], stats[:, :, 4], ALU.add))
    ch.step(v.tensor_tensor(d, stats[:, :, 1], stats[:, :, 4], ALU.subtract))
    ch.do(v.tensor_tensor(var, stats[:, :, 2], stats[:, :, 5], ALU.add))
    ch.step(v.tensor_scalar(mean, mean, 0.5, None, ALU.mult))
    ch.step(v.tensor_scalar(var, var, 1.0 / D, None, ALU.mult))
    ch.do(v.tensor_tensor(d, d, d, ALU.mult))
    ch.do(v.scalar_tensor_tensor(var, d, 0.25, var, ALU.mult, ALU.add))


class Mix:

    def __init__(self, nc, sem, L):
        self.nc, self.L = nc, L
        self.pb, self.sc, self.xn = L["pb"], L["sc"], L["xn"]
        self.ident, self.ones = L["ident"][:, :], L["ones"][:, :]
        area = L["Area"](L["r3"])
        self.wq = area.take(KD, NQ)
        self.pwbd = area.take(QC, P)
        self.wres = area.take(4, D)
        self.blk = area.take(P)
        self.brow = area.take(D)
        self.bn = area.take(8, QC)
        self.col = area.take(8, BLK)
        self.hrow = area.take(BLK, D)
        start = area.at
        self.x_dst = L["r3"][:, start:start + 2 * EG * P].bitcast(I32)
        self.hT = area.take(KD, 512)
        self.work = area.take(512)
        big = area.take(14 * 512)
        chunks = big.rearrange("p (c n) -> p c n", n=512)
        self.hp = chunks[:, 0:QC, :]
        self.ob = chunks[:, QC:QC + 4, :]
        self.vb = chunks[:, QC + 4:QC + 8, :]
        self.sq = L["Area"](L["r4"][:, 3600:4624]).take(2, 512)
        area.at = start + 2 * EG * P
        self.mu = area.take(D)
        self.cov = area.take(KD, D)
        self.prod = area.take(KD, NQ)
        self.mucol, self.mask = area.take(KD), area.take(1)
        c = lambda name, per, by=1: Count(sem(name), per, by)
        self.w_in = sem("mix_w_in")
        self.pw_zero, self.pw_set = sem("pw_zero"), sem("pw_set")
        self.pw_in = sem("pw_in")
        self.norm_root, self.ratio, self.logged = sem("norm_root"), sem("ratio"), sem("logged")
        self.h_ready, self.h_used = c("h_ready", BLK), c("h_used", BLK)
        self.hc_ready, self.hc_used = c("hc_ready", BLK), c("hc_used", BLK)
        self.mu_ready, self.muT, self.mucol_ready = sem("mu_ready"), sem("muT"), sem("mucol_ready")
        self.cov_ready, self.cw, self.prod_ready, self.bn_sums = sem("cov_ready"), sem("cw"), sem("prod_ready"), sem("bn_sums")
        self.var_set, self.std_set, self.bn_set = sem("var_set"), sem("std_set"), sem("bn_set")
        self.hrow_ready = c("hrow_ready", 1)
        self.hT_ready, self.hT_out = c("hT_ready", 2), c("hT_out", 2)
        self.mm_ready, self.mm_out = c("mm_ready", 12), c("mm_out", 12)
        self.sqa, self.sqa_used = c("sqa", 6), c("sqa_used", 6)
        self.sqb, self.sqb_used = c("sqb", 6), c("sqb_used", 6)
        self.sqo, self.sqo_used = c("sqo", 4), c("sqo_used", 4)
        self.ksum, self.o1 = c("ksum", 4), c("o1", 4)
        self.sums_read, self.root, self.diag, self.spread = c("sums_read", 1), c("root", 2), c("diag", 1), c("spread", 1)
        self.o_ready = c("o_ready", 4)
        self.res, self.res_out = c("res", 4), c("res_out", 4)
        self.fx_sq, self.fx_stored = c("fx_sq", 4), c("fx_stored", 1, 16)
        self.order = (2, 3, 0, 1, 4, 5)

    def loads(self, sp):
        A = self.L["A"]
        sp.dma_start(self.wq, A["w_qkv"].rearrange("(k p) c -> p k c", p=P)).then_inc(self.w_in, 16)
        sp.dma_start(self.wres, A["w_res"].rearrange("(k p) c -> p k c", p=P)).then_inc(self.w_in, 16)
        sp.dma_start(self.brow, A["b_res"].to_broadcast([P, D])).then_inc(self.w_in, 16)
        for j, name in enumerate(("bn_gamma", "bn_beta", "w_dw")):
            sp.dma_start(self.bn[:, j, :], A[name]).then_inc(self.w_in, 16)
        sp.wait_ge(self.pw_zero, 2)
        for b in range(4):
            sp.dma_start(self.pwbd[32 * b:32 * b + 32, :, 32 * b:32 * b + 32],
                         A["w_pw"][32 * b:32 * b + 32]).then_inc(self.pw_in, 16)

    def pool_start(self):
        self.nc.gpsimd.memset(self.pwbd, 0.0).then_inc(self.pw_zero, 1)
        self.nc.gpsimd.memset(self.blk, 0.0).then_inc(self.pw_zero, 1)

    def dve_start(self, ch, between, extra):
        nc, sc, v, pb = self.nc, self.sc, self.nc.vector, self.pb
        v.wait_ge(self.pw_zero, 2)
        for b in range(4):
            ch.step(v.memset(self.blk[32 * b:32 * b + 32, 32 * b:32 * b + 32], 1.0))
        v.wait_ge(self.norm_root, 1)
        n, p, a, b, c, d = (sc[:, j, :] for j in (5, 6, 7, 8, 10, 11))
        ch.do(v.tensor_scalar(n, n, MINN, None, ALU.max))
        ch.do(v.tensor_scalar(p, n, MAXN, None, ALU.min))
        ch.step(v.tensor_scalar(a, p, -1.0, 1.0, ALU.mult, ALU.add))
        ch.do(v.tensor_scalar(b, p, 1.0, None, ALU.add))
        ch.do(v.reciprocal(a, a))
        v.tensor_tensor(a, a, b, ALU.mult).then_inc(self.ratio, 1)
        ch.do(v.tensor_tensor(c, p, p, ALU.mult))
        ch.do(v.tensor_scalar(d, c, 1.0 / 9.0, 1.0 / 7.0, ALU.mult, ALU.add))
        for k in (5.0, 3.0, 1.0):
            ch.do(v.tensor_tensor(d, d, c, ALU.mult))
            ch.do(v.tensor_scalar(d, d, 1.0 / k, None, ALU.add))
        ch.do(v.tensor_tensor(d, d, p, ALU.mult))
        v.wait_ge(self.logged, 1)
        ch.do(v.tensor_scalar(b, b, 0.5, None, ALU.mult))
        ch.do(v.tensor_tensor(d, d, b, ALU.subtract))
        ch.do(v.tensor_scalar(p, p, 0.2, None, ALU.is_lt))
        ch.do(v.tensor_tensor(d, d, p, ALU.mult))
        ch.do(v.tensor_tensor(b, b, d, ALU.add))
        ch.do(v.reciprocal(n, n))
        ch.do(v.tensor_tensor(sc[:, 1, :], b, n, ALU.mult))
        ch.do(v.tensor_scalar(self.mask, self.L["pcol"][:, 0:1], float(N - (NT - 1) * P), None, ALU.is_lt))

        def tile(t):
            return self.xn[:, bass.ds(t, 1), :].rearrange("p o d -> p (o d)")

        def h(i, us=range(BLK)):
            for u in us:
                t = BLK * i + u
                self.h_used.wait_before(v, i, u + 1)
                v.tensor_scalar(self.hrow[:, u, :], tile(t), sc[:, 1, bass.ds(t, 1)], None, ALU.mult)\
                    .then_inc(self.h_ready.sem, 1)
        turns(v, NT // BLK, h)
        h(NT // BLK, (0,))
        v.wait_ge(self.h_used.sem, NT)
        v.tensor_scalar(self.mu, pb[0][:, 0:D], 1.0 / N, None, ALU.mult).then_inc(self.mu_ready, 1)
        v.wait_ge(self.mu_ready, 1)

        def hc(i, us=range(BLK)):
            for u in us:
                t = BLK * i + u
                if len(us) > 1:
                    if not u:
                        ch.turn(i, BLK)
                    extra(t)
                self.hc_used.wait_before(v, i, u + 1)
                ins = v.scalar_tensor_tensor(self.hrow[:, u, :], tile(t), sc[:, 1, bass.ds(t, 1)], self.mu, ALU.mult,
                                             ALU.subtract)
                if len(us) == 1:
                    ch.do(ins)
                    ins = v.tensor_scalar(self.hrow[:, u, :], self.hrow[:, u, :], self.mask, None, ALU.mult)
                ins.then_inc(self.hc_ready.sem, 1)
        between()
        ch.loop()
        hc(0)
        with v.Fori(1, NT // BLK) as i:
            hc(i)
        ch.end(NT // BLK, BLK)
        hc(NT // BLK, (0,))
        v.wait_ge(self.muT, 1)
        for k in range(KD):
            v.tensor_copy(self.mucol[:, k:k + 1], pb[5][:, k * P:k * P + 1]).then_inc(self.mucol_ready, 1)
        v.wait_ge(self.hc_used.sem, NT)
        for k in range(KD):
            v.tensor_scalar(self.cov[:, k, :], pb[1 + k][:, 0:D], 1.0 / N, None, ALU.mult).then_inc(self.cov_ready, 1)
        v.wait_ge(self.w_in, 6 * 16)
        for k in range(KD):
            v.wait_ge(self.cw, 2 * k + 2)
            for j in range(2):
                c = slice(j * NQ // 2, (j + 1) * NQ // 2)
                v.tensor_tensor(self.prod[:, k, c], pb[3 + j][:, 0:NQ // 2], self.wq[:, k, c], ALU.mult)\
                    .then_inc(self.prod_ready, 1)
        v.wait_ge(self.bn_sums, 1)
        bn = self.bn
        v.tensor_scalar(bn[:, 4, :], pb[5][:, 0:QC], 1e-5, None, ALU.add).then_inc(self.var_set, 1)
        v.wait_ge(self.std_set, 1)
        ch.do(v.reciprocal(bn[:, 4, :], bn[:, 4, :]))
        ch.do(v.tensor_tensor(bn[:, 5, :], bn[:, 0, :], bn[:, 4, :], ALU.mult))
        ch.do(v.tensor_tensor(bn[:, 6, :], pb[5][:, 8:8 + QC], bn[:, 5, :], ALU.mult))
        ch.do(v.tensor_tensor(bn[:, 6, :], bn[:, 1, :], bn[:, 6, :], ALU.subtract))
        v.wait_ge(self.pw_in, 64)
        for c in range(QC):
            ch.step(v.tensor_scalar(self.pwbd[:, c, :], self.pwbd[:, c, :], bn[:, 2, c:c + 1], None, ALU.mult))
        ch.done()
        v.sem_inc(self.bn_set, 1)

    def act_start(self, s, between):
        sc, act = self.sc, self.nc.scalar
        act.activation(sc[:, 5, :], sc[:, 0, :], ACT.Sqrt).then_inc(self.norm_root, 1)
        s.wait_ge(self.ratio, 1)
        act.activation(sc[:, 8, :], sc[:, 7, :], ACT.Ln).then_inc(self.logged, 1)
        between()
        s.wait_ge(self.var_set, 1)
        act.activation(self.bn[:, 4, :], self.bn[:, 4, :], ACT.Sqrt).then_inc(self.std_set, 1)
        s.wait_ge(self.bn_set, 1)

    def pe_start(self, pe, between):
        mm, pb, ones = self.nc.tensor.matmul, self.pb, self.ones

        def colsum(i, us=range(BLK)):
            for u in us:
                self.h_ready.wait(pe, i, u + 1)
                first = isinstance(i, int) and i == 0 and u == 0
                mm(pb[0][:, 0:D], ones, self.hrow[:, u, :], start=first, stop=len(us) == 1)\
                    .then_inc(self.h_used.sem, 1)
        turns(pe, NT // BLK, colsum)
        colsum(NT // BLK, (0,))
        pe.wait_ge(self.mu_ready, 1)
        for k in range(KD):
            ins = self.nc.tensor.transpose(pb[5][:, k * P:(k + 1) * P], self.mu[:, k * P:(k + 1) * P], self.ident)
        ins.then_inc(self.muT, 1)

        def gram(i, us=range(BLK)):
            for u in us:
                self.hc_ready.wait(pe, i, u + 1)
                first = isinstance(i, int) and i == 0 and u == 0
                for k in range(KD):
                    ins = mm(pb[1 + k][:, 0:D], self.hrow[:, u, k * P:(k + 1) * P], self.hrow[:, u, :], start=first,
                             stop=len(us) == 1)
                ins.then_inc(self.hc_used.sem, 1)
        between()
        turns(pe, NT // BLK, gram)
        gram(NT // BLK, (0,))
        pe.wait_ge(self.cov_ready, 2)
        pe.wait_ge(self.w_in, 6 * 16)
        for m in range(KD):
            for j in range(2):
                if m:
                    pe.wait_ge(self.prod_ready, j + 1)
                for k in range(KD):
                    ins = mm(pb[3 + j][:, 0:NQ // 2], self.cov[:, k, m * P:(m + 1) * P],
                             self.wq[:, k, j * NQ // 2:(j + 1) * NQ // 2], start=k == 0, stop=k == KD - 1)
                ins.then_inc(self.cw, 1)
        pe.wait_ge(self.prod_ready, 4)
        pe.wait_ge(self.mucol_ready, 2)
        for c in range(QC):
            for k in range(KD):
                mm(pb[5][:, c:c + 1], self.prod[:, k, c * P:(c + 1) * P], ones[:, 0:1], start=k == 0, stop=k == KD - 1)
            for k in range(KD):
                ins = mm(pb[5][:, 8 + c:9 + c], self.wq[:, k, c * P:(c + 1) * P], self.mucol[:, k:k + 1], start=k == 0,
                         stop=k == KD - 1)
        ins.then_inc(self.bn_sums, 1)
        pe.wait_ge(self.bn_set, 1)

    def bank(self, n):
        return self.pb[2 + n % 2][:, :]

    def slot(self, stage, eng, i, q, amid=lambda: None):
        self.amid = amid
        more = not isinstance(i, int) or i < NB - 1
        if q < 2:
            if more:
                stage("a", eng, i + 1, q)
            stage("c", eng, i, q)
        elif q == 2:
            stage("f", eng, i, more)
        elif more:
            stage("b", eng, i + 1, 0)

    def squares_sum(self, pe, bank, at, k, first, last):
        for j in range(BLK):
            ins = self.nc.tensor.matmul(self.pb[bank][:, at + j:at + j + 1], self.sq[:, k % 2, j * P:(j + 1) * P],
                                        self.ones[:, 0:1], start=first and j == 0,
                                        stop=last and j == BLK - 1)
        return ins

    def pe(self, st, pe, b, q):
        mm, tr, pb = self.nc.tensor.matmul, self.nc.tensor.transpose, self.pb

        def square_a(k):
            self.sqa.wait(pe, b, k + 1)
            if k == 0:
                self.sums_read.wait_before(pe, b, 1)
            self.squares_sum(pe, 4, 0, k, k == 0, k == 5).then_inc(self.sqa_used.sem, 1)

        def square_b(k):
            self.sqb.wait(pe, b, k + 1)
            self.squares_sum(pe, 5, 0, k, k == 0, k == 5).then_inc(self.sqb_used.sem, 1)

        if st == "a":
            if q == 0:
                self.hrow_ready.wait(pe, b, 1)
                self.o1.wait_before(pe, b, 4)
                for k in range(KD):
                    for j in range(BLK):
                        ins = tr(pb[k][:, j * P:(j + 1) * P], self.hrow[:, j, k * P:(k + 1) * P], self.ident)
                    ins.then_inc(self.hT_ready.sem, 1)
                if not (isinstance(b, int) and b == 0):
                    self.spread_scale(pe, b - 1)
                self.hT_out.wait(pe, b, 2)
            for n in range(3 * q, 3 * q + 3):
                if n >= 2:
                    self.mm_out.wait(pe, b, n - 1)
                else:
                    self.mm_out.wait_before(pe, b, 11 + n)
                c = self.order[n]
                for k in range(KD):
                    ins = mm(self.bank(n), self.wq[:, k, c * P:(c + 1) * P], self.hT[:, k, :], start=k == 0, stop=k == 1)
                ins.then_inc(self.mm_ready.sem, 1)
                if n:
                    square_a(n - 1)
            if q:
                square_a(5)
        if st == "c" and q == 0 and isinstance(b, int) and b == NB - 1:
            self.spread_scale(pe, b)
        if st == "f":
            if q:
                self.mm_out.wait(pe, b + 1, 6)
            else:
                self.mm_out.wait(pe, b, 12)
            self.o_ready.wait(pe, b, 4)
            for j in range(BLK):
                if j == 1:
                    for k in range(4):
                        self.sqo.wait(pe, b, k + 1)
                        self.squares_sum(pe, 4, 4, k, k == 0, k == 3).then_inc(self.sqo_used.sem, 1)
                for m in range(4):
                    ins = mm(pb[2 + j // 2][:, (j % 2) * D:(j % 2 + 1) * D], self.ob[:, m, j * P:(j + 1) * P],
                             self.wres[:, m, :], start=m == 0, stop=m == 3)
                ins.then_inc(self.res.sem, 1)
        if st == "b":
            def key_sum(j, count):
                self.mm_out.wait(pe, b, count)
                if j >= 2:
                    self.o1.wait(pe, b, j - 1)
                mm(pb[j % 2][:, :], self.blk, self.hp[:, 2 + j % 2, :], start=True, stop=True).then_inc(self.ksum.sem, 1)
            key_sum(0, 2)
            key_sum(1, 2)
            for n in range(QC, 2 * QC):
                self.mm_out.wait(pe, b, n - 1)
                if n == QC:
                    self.res_out.wait_before(pe, b, 4)
                c = self.order[n - QC]
                mm(self.bank(n), self.pwbd[:, c, :], self.hp[:, c, :], start=True, stop=True).then_inc(self.mm_ready.sem, 1)
                if n > QC:
                    square_b(n - 1 - QC)
                if n - QC == 3:
                    key_sum(2, QC + 1)
                    key_sum(3, QC + 2)
            square_b(5)

    def spread_scale(self, pe, b):
        self.diag.wait(pe, b, 1)
        self.nc.tensor.matmul(self.pb[5][:, :], self.ones, self.work, start=True, stop=True).then_inc(self.spread.sem, 1)

    def act(self, st, s, b, q):
        act, pb = self.nc.scalar.activation, self.pb
        if st == "a":
            if q == 0:
                if not (isinstance(b, int) and b == 0):
                    self.roots(s, b - 1)
                self.mm_ready.wait_before(s, b, 6)
                for k in range(KD):
                    self.hT_ready.wait(s, b, k + 1)
                    act(self.hT[:, k, :], pb[k][:, :], ACT.Copy).then_inc(self.hT_out.sem, 1)
                self.mm_ready.wait_before(s, b, 12)
                self.o1.wait_before(s, b, 4)
            for n in range(3 * q, 3 * q + 3):
                c = self.order[n]
                self.mm_ready.wait(s, b, n + 1)
                act(self.hp[:, c, :], self.bank(n), ACT.Relu, bias=self.bn[:, 6, c:c + 1], scale=self.bn[:, 5, c:c + 1])\
                    .then_inc(self.mm_out.sem, 1)
                if n >= 2:
                    self.sqa_used.wait(s, b, n - 1)
                else:
                    self.sqb_used.wait_before(s, b, 5 + n)
                self.mm_out.wait(s, b, n + 1)
                act(self.sq[:, n % 2, :], self.hp[:, c, :], ACT.Square).then_inc(self.sqa.sem, 1)
                if n % 3 == 0:
                    self.amid()
        if st == "c" and q == 0 and isinstance(b, int) and b == NB - 1:
            self.roots(s, b)
        if st == "f":
            for m in range(4):
                if m >= 2:
                    self.sqo_used.wait(s, b, m - 1)
                elif q:
                    self.sqa_used.wait(s, b + 1, 5 + m)
                else:
                    self.sqb_used.wait(s, b, 5 + m)
                self.o_ready.wait(s, b, m + 1)
                act(self.sq[:, m % 2, :], self.ob[:, m, :], ACT.Square).then_inc(self.sqo.sem, 1)
            self.amid()
            self.sqo_used.wait(s, b, 4)
            act(self.col[:, 2, :], pb[4][:, 4:8], ACT.Sqrt).then_inc(self.root.sem, 1)
            for j in range(BLK):
                self.res_out.wait(s, b, j + 1)
                if j:
                    self.fx_sq.wait(s, b, j)
                act(self.sq[:, 0, 0:D], self.xn[:, bass.ds(4 * b + j, 1), :].rearrange("p o d -> p (o d)"), ACT.Square,
                    accum_out=self.sc[:, 9, bass.ds(4 * b + j, 1)]).then_inc(self.fx_sq.sem, 1)
            s.dma_start(self.L["fx_d"][bass.ds(4 * b, BLK), :, :].rearrange("t p d -> p t d"),
                        self.xn[:, bass.ds(4 * b, BLK), :]).then_inc(self.fx_stored.sem, 16)
        if st == "b":
            self.o_ready.wait_before(s, b, 4)
            self.res.wait_before(s, b, 4)
            self.fx_sq.wait_before(s, b, 4)
            for n in range(QC, 2 * QC):
                k, c = n - QC, self.order[n - QC]
                if k == 1:
                    self.amid()
                if k == 4:
                    for j in range(2):
                        act(self.vb[:, j, :], self.hp[:, 4 + j, :], ACT.Copy)
                self.mm_ready.wait(s, b, n + 1)
                if k >= 2:
                    self.sqb_used.wait(s, b, k - 1)
                elif isinstance(b, int) and b == 0:
                    self.sqa_used.wait(s, b, 5 + k)
                else:
                    self.sqo_used.wait_before(s, b, 3 + k)
                act(self.sq[:, k % 2, :], self.bank(n), ACT.Square).then_inc(self.sqb.sem, 1)
                dst = {0: self.ob[:, 2, :], 1: self.ob[:, 3, :], 2: self.hp[:, 2, :], 3: self.hp[:, 3, :],
                       4: self.vb[:, 2, :], 5: self.vb[:, 3, :]}[c]
                act(dst, self.bank(n), ACT.Copy if c >= 4 else ACT.Relu).then_inc(self.mm_out.sem, 1)

    def roots(self, s, b):
        self.sums_read.wait(s, b, 1)
        self.nc.scalar.activation(self.col[:, 0:2, :], self.col[:, 4:6, :], ACT.Sqrt).then_inc(self.root.sem, 1)

    def dve(self, ch):
        return lambda st, v, b, q: self.dve_stage(ch, st, b, q)

    def dve_stage(self, ch, st, b, q):
        v, pb = self.nc.vector, self.pb
        n1, n2, n3, scale, s1, s2, t, r = (self.col[:, j, :] for j in range(8))
        if st == "a" and q == 0:
            if not (isinstance(b, int) and b == 0):
                self.read_sums(ch, b - 1)
            self.hT_ready.wait_before(v, b, 2)
            v.tensor_tensor(self.hrow, self.xn[:, bass.ds(4 * b, BLK), :],
                            self.sc[:, 1, bass.ds(4 * b, BLK)].unsqueeze(2).to_broadcast([P, BLK, D]), ALU.mult)\
                .then_inc(self.hrow_ready.sem, 1)
        if st == "b":
            self.res.wait_before(v, b, 4)
            for j in range(4):
                x = self.hp[:, j, :] if j < 2 else self.ob[:, j, :]
                self.ksum.wait(v, b, j + 1)
                if j >= 2:
                    self.mm_out.wait(v, b, 7 + j)
                v.tensor_tensor(self.ob[:, j, :], x, pb[j % 2][:, :], ALU.mult).then_inc(self.o1.sem, 1)
        if st == "c":
            if q == 0:
                if isinstance(b, int) and b == NB - 1:
                    self.read_sums(ch, b)
                self.root.wait(v, b, 1)
                ch.do(v.tensor_scalar(n1, n1, MINN, None, ALU.max))
                ch.step(v.tensor_scalar(t, n1, CAP, None, ALU.min))
                ch.do(v.reciprocal(n1, n1))
                ch.do(v.tensor_tensor(scale, t, n1, ALU.mult))
                ch.do(v.tensor_tensor(n2, n2, scale, ALU.mult))
                ch.do(v.tensor_scalar(n2, n2, MINN, None, ALU.max))
                ch.step(v.tensor_scalar(t, n2, CAP, None, ALU.min))
                ch.do(v.reciprocal(n2, n2))
                ch.do(v.tensor_tensor(t, t, n2, ALU.mult))
                ch.do(v.tensor_tensor(scale, scale, t, ALU.mult))
                v.tensor_tensor(self.work.rearrange("p (j n) -> p j n", n=P), self.ident.unsqueeze(1).to_broadcast([P, BLK, P]),
                                scale.unsqueeze(2).to_broadcast([P, BLK, P]), ALU.mult).then_inc(self.diag.sem, 1)
                ch.do(v.tensor_tensor(r, scale, scale, ALU.mult))
                self.amid()
                self.spread.wait(v, b, 1)
                self.mm_out.wait(v, b, 12)
            for m in (2 * q, 2 * q + 1):
                val, w = self.vb[:, m, :], self.work
                ch.do(v.tensor_tensor(val, val, pb[5][:, :], ALU.mult))
                ch.do(v.tensor_scalar(w, val, MINN, None, ALU.add))
                ch.do(v.reciprocal(w, w))
                ch.do(v.tensor_tensor(val, val, w, ALU.mult))
                v.tensor_tensor(self.ob[:, m, :], self.ob[:, m, :], val, ALU.mult).then_inc(self.o_ready.sem, 1)
        if st == "f":
            self.root.wait(v, b, 2)
            ch.do(v.tensor_tensor(n3, n3, r, ALU.mult))
            ch.do(v.tensor_scalar(n3, n3, MINN, None, ALU.max))
            ch.step(v.tensor_scalar(t, n3, CAP, None, ALU.min))
            ch.do(v.reciprocal(n3, n3))
            ch.do(v.tensor_tensor(t, t, n3, ALU.mult))
            ch.do(v.tensor_tensor(t, t, r, ALU.mult))
            for j in range(BLK):
                self.res.wait(v, b, 2 * (j // 2) + 2)
                v.scalar_tensor_tensor(self.xn[:, bass.ds(4 * b + j, 1), :].rearrange("p o d -> p (o d)"),
                                       pb[2 + j // 2][:, (j % 2) * D:(j % 2 + 1) * D],
                                       t[:, j:j + 1], self.brow, ALU.mult, ALU.add).then_inc(self.res_out.sem, 1)

    def read_sums(self, ch, b):
        v, s1, s2 = self.nc.vector, self.col[:, 4, :], self.col[:, 5, :]
        self.sqa_used.wait(v, b, 6)
        self.sqb_used.wait(v, b, 6)
        ch.do(v.tensor_copy(s1, self.pb[4][:, 0:4]))
        v.tensor_tensor(s2, s1, self.pb[5][:, 0:4], ALU.add).then_inc(self.sums_read.sem, 1)

    def rest(self, fn, eng, i, groups):
        for q in range(len(groups), 4):
            self.slot(fn, eng, i, q)

    def first(self, fn, eng):
        self.amid = lambda: None
        for st, q in (("a", 0), ("a", 1), ("b", 0)):
            fn(st, eng, 0, q)


def edges_and_mix(nc, ctx, sem, L):
    A, pb, ident, ones, xn, sc = L["A"], L["pb"], L["ident"], L["ones"], L["xn"], L["sc"]
    iota_f, dst_f, nt_f, nodecol, E_all = (L[k] for k in ("iota_f", "dst_f", "nt_f", "nodecol", "E_all"))
    src_sb, idx, grab, sde, r1, r2, r3 = (L[k] for k in ("src_sb", "idx", "grab", "sde", "r1", "r2", "r3"))
    sat_d, et_d, tau_i = L["sat_d"], L["et_d"], L["tau_i"]
    assert NG - 1 == NT - 1
    TA = NB
    NX = NT - 1

    small = L["Area"](L["r4"])
    dstb = small.take(EG * P, dt=I32)
    st = small.take(EG * P // 2, dt=BF16).rearrange("p (t e) -> p t e", e=P)
    st_end = small.at
    edge_pre = small.take(2, EG * H)
    satb = small.take(2, EG * H)
    cols = small.take(16)
    assert small.at <= 3600

    same = r1[:, 0:CH + 1]
    tmp = r1[:, CH + 8:2 * CH + 8]
    dstx = r2[:, 0:CH + 2].bitcast(I32)
    pre = r2[:, 0:CH]
    score = r3[:, 0:CH]
    PR = 4
    TB = VT // (4 * PR)
    rows = r3[:, CH:CH + 4 * PR * TAB].rearrange("p (q e d) -> p q e d", q=4, e=PR)
    acc = r1[:, 0:NT * TAB].rearrange("p (t d) -> p t d", d=TAB)
    S = L["r4"][:, 0:2 * PR * P].rearrange("p (u e n) -> p u e n", u=2, e=PR)
    msg = L["r4"][:, 2 * PR * P:2 * PR * (P + TAB)].rearrange("p (u e d) -> p u e d", u=2, e=PR)
    etb = L["r4"][:, 0:1024].rearrange("p (u t e) -> p u t e", u=2, t=4)
    carry = L["r4"][:, 1024:2048].rearrange("p (j e) -> p j e", e=P)

    idx_in = [Count(sem(f"idx_in{q}"), 1, 16) for q in range(4)]
    grabbed = [Count(sem(f"grabbed{q}"), EG, 16) for q in range(4)]
    copied = [Count(sem(f"copied{q}"), 1, 16) for q in range(4)]
    gate = sem("gate")
    dst_in = Count(sem("dst_in"), 4, 16)
    st_built = Count(sem("st_built"), 4)
    sde_ready = Count(sem("sde_ready"), 4)
    sde_used = Count(sem("sde_used"), 4)
    score_ready = Count(sem("score_ready"), 4)
    scT_ready = Count(sem("scT_ready"), 4)
    scT_out = Count(sem("scT_out"), 4)
    sat_stored = [Count(sem(f"sat_stored{u}"), 2, 16) for u in range(2)]
    x_dst_in, x_cols_in = [sem(f"x_dst_in{j}") for j in range(3)], sem("x_cols_in")
    x_built, x_sde, x_used = sem("x_built"), sem("x_sde"), sem("x_used")
    dve2 = sem("dve2")
    dst_chunks_in, sat_in = sem("dst_chunks_in"), sem("sat_in")
    r2_free = sem("r2_free")
    diag_ready, diag_sum = sem("diag_ready"), sem("diag_sum")
    shifted, weighed, et_out = sem("shifted"), sem("weighed"), sem("et_out")
    et_in = [Count(sem(f"et_in{u}"), 1, 64) for u in range(2)]
    etT_ready, etT_out = Count(sem("etT_ready"), 2), Count(sem("etT_out"), 2)
    e_extra = sem("e_extra")
    bidx_in = [Count(sem(f"bidx_in{q}"), 1, 16) for q in range(4)]
    row_in = [Count(sem(f"row_in{q}"), PR, 16) for q in range(4)]
    msg_ready = Count(sem("msg_ready"), 4)
    summed = Count(sem("summed"), 4)
    added = Count(sem("added"), 4 * PR)
    acc_zero = sem("acc_zero")
    mixed = sem("mixed")

    MIX = Mix(nc, sem, L)
    x_dst = (dstb, MIX.x_dst[:, 0:EG * P], MIX.x_dst[:, EG * P:2 * EG * P])
    xsum = L["r4"][:, st_end:st_end + NX * H].rearrange("p (n h) -> p n h", h=H)

    def groups(i):
        return range(4) if not isinstance(i, int) or i < TA - 1 else range(NG - 4 * (TA - 1))

    def all_turns(eng, body):
        body(0)
        with eng.Fori(1, TA - 1) as i:
            body(i)
        body(TA - 1)

    with nc.Block() as block:
        @block.sync
        def _(sp):
            for q in range(4):
                sp.dma_start(idx[:, q, :], src_sb[:, q * EG:(q + 1) * EG]).then_inc(idx_in[q].sem, 16)
            MIX.loads(sp)

            def body(i):
                for q in groups(i):
                    g = 4 * i + q
                    grabbed[q].wait(sp, i, EG)
                    sp.dma_start(E_all[:, bass.ds(g * EG, EG), :], grab[:, q, :, :]).then_inc(copied[q].sem, 16)
                    copied[q].wait(sp, i, 1)
                    if not (isinstance(g, int) and g + 4 >= NG):
                        sp.dma_start(idx[:, q, :], src_sb[:, bass.ds((g + 4) * EG, EG)]).then_inc(idx_in[q].sem, 16)
                    if not (isinstance(g, int) and g == NG - 1):
                        t = sp.value_load(tau_i[0:1, bass.ds(g, 1)], min_val=0, max_val=ET - 1)
                        sp.dma_start(src_sb[:, bass.ds(ET + g, 1)], src_sb[:, bass.ds(t, 1)]).then_inc(x_cols_in, 16)
                        sp.dma_start(dst_f[:, bass.ds(ET + g, 1)], dst_f[:, bass.ds(t, 1)]).then_inc(x_cols_in, 16)
            body(0)
            with sp.Fori(1, TA - 2) as i:
                body(i)
            body(TA - 2)
            body(TA - 1)
            for q in range(4):
                idx_in[q].wait(sp, TA - 1 if q < 1 else TA - 2, 1)
            for q in range(4):
                sp.dma_start(idx[:, q, 0:PR], src_sb[:, q * PR:(q + 1) * PR]).then_inc(bidx_in[q].sem, 16)
            sp.wait_ge(r2_free, 1)
            for h in range(H):
                sp.dma_start(dstx[16 * h:16 * (h + 1), :], A["dst_chunks"]).then_inc(dst_chunks_in, 16)
            for u in range(2):
                sp.wait_ge(sat_stored[u].sem, 16 * (NG + 1) // 2)
            sp.wait_ge(mixed, 1)
            sp.dma_start(score, sat_d.rearrange("h t e -> (h t e)").rearrange("(p f) -> p f", p=P)).then_inc(sat_in, 16)
            W4 = CH // 4
            for k in range(4):
                sp.wait_ge(weighed, k + 1)
                sp.dma_start(et_d.rearrange("h t e -> (h t e)").rearrange("(p f) -> p f", p=P)[:, k * W4:(k + 1) * W4],
                             score[:, k * W4:(k + 1) * W4]).then_inc(et_out, 16)
            sp.wait_ge(et_out, 64)
            for i in range(TA):
                u = i % 2
                if i > 1:
                    sp.wait_ge(etT_ready.sem, i - 1)
                for k in groups(i):
                    g = 4 * i + k
                    sp.dma_start(etb[:, u, k, :], et_d[:, g * EG:(g + 1) * EG, :].rearrange("h t e -> t h e"))\
                        .then_inc(et_in[u].sem, 16)
            sp.wait_ge(x_cols_in, 2 * 16 * NX)
            sp.wait_ge(etT_out.sem, TA)
            for n in range(NX):
                t = sp.value_load(tau_i[0:1, n:n + 1], min_val=0, max_val=ET - 1)
                sp.dma_start(E_all[:, ET + n:ET + n + 1, :], E_all[:, bass.ds(t, 1), :]).then_inc(e_extra, 16)

            def second(i):
                for q in range(4):
                    msg_ready.wait(sp, i, q + 1)
                    if not (isinstance(i, int) and i == TB - 1):
                        sp.dma_start(idx[:, q, 0:PR], src_sb[:, bass.ds(((i + 1) * 4 + q) * PR, PR)])\
                            .then_inc(bidx_in[q].sem, 16)
            second(0)
            with sp.Fori(1, TB - 1) as i:
                second(i)

        @block.gpsimd
        def _(g_):
            MIX.pool_start()

            def body(i):
                for q in groups(i):
                    idx_in[q].wait(g_, i, 1)
                    g_.sem_inc(gate, 1)
                    for e in range(EG):
                        g_.indirect_dma_start(out=grab[:, q, e, :], out_offset=None, in_=L["ssrc_d"],
                                              in_offset=bass.IndirectOffsetOnAxis(ap=idx[:, q, e:e + 1], axis=0))\
                            .then_inc(grabbed[q].sem, 16)
            all_turns(g_, body)
            g_.wait_ge(mixed, 1)

            def second(i):
                for q in range(4):
                    bidx_in[q].wait(g_, i, 1)
                    g_.sem_inc(gate, 1)
                    for e in range(PR):
                        g_.indirect_dma_start(out=rows[:, q, e, :], out_offset=None, in_=L["table_d"],
                                              in_offset=bass.IndirectOffsetOnAxis(ap=idx[:, q, e:e + 1], axis=0))\
                            .then_inc(row_in[q].sem, 16)
            turns(g_, TB, second)

        @block.vector
        def _(v):
            ch = Chain(v, dve2)
            ch.do(nc.vector.memset(r2[:, :], 0.0))

            def extra_rows():
                for j in range(3):
                    v.wait_ge(x_dst_in[j], 16 * EG)
                    nc.vector.tensor_tensor(st[:, :, :], x_dst[j].rearrange("p (t e) -> p t e", e=P),
                                            nodecol[:, ET + j * EG:ET + (j + 1) * EG].unsqueeze(2).to_broadcast([P, EG, P]),
                                            ALU.is_equal).then_inc(x_built, 1)
                    v.wait_ge(x_sde, j + 1)
                    parts = pb[6][:, 0:3 * EG * H].rearrange("p (t k h) -> p t k h", k=3, h=H)
                    x = xsum[:, j * EG:(j + 1) * EG, :]
                    ch.do(nc.vector.tensor_copy(x, parts[:, :, 2, :]))
                    ch.do(nc.vector.tensor_tensor(x, x, parts[:, :, 1, :], ALU.add))
                    ch.do(nc.vector.tensor_tensor(x, x, parts[:, :, 0, :], ALU.add))
                    v.sem_inc(x_used, 1)

            def extra(n):
                t = v.value_load(tau_i[0:1, bass.ds(n, 1)], min_val=0, max_val=ET - 1)
                ch.do(nc.vector.tensor_tensor(sde[:, bass.ds(t, 1), :], sde[:, bass.ds(t, 1), :],
                                              xsum[:, bass.ds(n, 1), :], ALU.add))
            MIX.dve_start(ch, extra_rows, extra)
            MIX.first(MIX.dve(ch), v)

            def one_hot(i, q):
                dst_in.wait(v, i, q + 1)
                nc.vector.tensor_tensor(st[:, :, :], dstb.rearrange("p (t e) -> p t e", e=P),
                                        nodecol[:, bass.ds((4 * i + q) * EG, EG)].unsqueeze(2).to_broadcast([P, EG, P]),
                                        ALU.is_equal).then_inc(st_built.sem, 1)
            one_hot(0, 0)
            ch.loop()

            def body(i, per):
                ch.turn(i, per)
                for q in groups(i):
                    u, g = q % 2, 4 * i + q
                    sde_ready.wait(v, i, q + 1)
                    copied[q].wait(v, i, 1)
                    if q >= 2:
                        scT_ready.wait(v, i, q - 1)
                    else:
                        scT_ready.wait_before(v, i, q + 3)
                    ep = edge_pre[:, u, :]
                    ep3 = ep.rearrange("p (t h) -> p t h", h=H)
                    parts = pb[6][:, 0:3 * EG * H].rearrange("p (t k h) -> p t k h", k=3, h=H)
                    ch.do(nc.vector.tensor_tensor(ep3, E_all[:, bass.ds(g * EG, EG), :], parts[:, :, 2, :], ALU.add))
                    ch.do(nc.vector.tensor_tensor(ep3, ep3, parts[:, :, 1, :], ALU.add))
                    nc.vector.tensor_tensor(ep3, ep3, parts[:, :, 0, :], ALU.add).then_inc(sde_used.sem, 1)
                    sde_used.wait(v, i, q + 1)
                    ch.do(nc.vector.tensor_tensor(ep, ep, sde[:, bass.ds(g * EG, EG), :].rearrange("p t h -> p (t h)"),
                                                  ALU.add))
                    nc.vector.scalar_tensor_tensor(ep, ep, 0.2, ep, ALU.mult, ALU.max).then_inc(score_ready.sem, 1)
                    def next_rows():
                        if not (isinstance(g, int) and g == NG - 1):
                            one_hot(i, q + 1)
                    if q:
                        next_rows()
                    MIX.slot(MIX.dve(ch), v, i, q, next_rows)
            body(0, 0)
            per = ch.k
            with v.Fori(1, TA - 1) as i:
                body(i, per)
                assert ch.k == per, (ch.k, per)
            body(TA - 1, per)
            v.wait_ge(score_ready.sem, NG)
            v.wait_ge(dst_in.sem, 16 * (NG + 1))
            v.sem_inc(r2_free, 1)
            MIX.rest(MIX.dve(ch), v, TA - 1, groups(TA - 1))
            v.wait_ge(mixed, 1)
            v.wait_ge(dst_chunks_in, 16 * H)
            ch.do(nc.vector.tensor_tensor(same, dstx[:, 1:CH + 2], dstx[:, 0:CH + 1], ALU.not_equal))
            ch.do(nc.vector.tensor_scalar(same, same, -BIG, None, ALU.mult))
            col = lambda j: cols[:, j:j + 1]
            ch.step(nc.vector.tensor_tensor(col(0), dstx[:, CH:CH + 1], dstx[:, 0:1], ALU.not_equal))
            ch.do(nc.vector.tensor_tensor(col(1), dstx[:, CH + 1:CH + 2], dstx[:, 1:2], ALU.not_equal))
            ch.do(nc.vector.tensor_scalar(cols[:, 0:2], cols[:, 0:2], -BIG, None, ALU.mult))
            v.wait_ge(sat_in, 16)
            fwd_neg, bwd_neg = same[:, 0:CH], same[:, 1:CH + 1]

            def across(k, own, chain, edge, back):
                for j, c in enumerate((own, chain, edge)):
                    ch.step(nc.vector.tensor_scalar(carry[:, j, :], ident[:, :], c, None, ALU.mult))
                ch.done()
                v.sem_inc(diag_ready, 1)
                v.wait_ge(diag_sum, k + 1)
                ch.do(nc.vector.tensor_copy(carry[:, 0:3, :], pb[5][:, 0:3 * P].rearrange("p (j e) -> p j e", e=P)))
                o, c, d, w, r = (carry[:, j, :] for j in range(5))
                ch.do(nc.vector.memset(r, -BIG))
                if back:
                    ch.do(nc.vector.tensor_tensor_scan(w[:, ::-1], c[:, ::-1], o[:, ::-1], -BIG, ALU.add, ALU.max))
                    ch.do(nc.vector.tensor_tensor(r[:, 0:P - 1], w[:, 1:P], d[:, 0:P - 1], ALU.add))
                else:
                    ch.do(nc.vector.tensor_tensor_scan(w, c, o, -BIG, ALU.add, ALU.max))
                    ch.do(nc.vector.tensor_tensor(r[:, 1:P], w[:, 0:P - 1], d[:, 1:P], ALU.add))
                ch.do(nc.vector.tensor_tensor(r, r, ident[:, :], ALU.mult))
                ch.do(nc.vector.reduce_sum(col(4 + k), r, mybir.AxisListType.X))
                ch.do(nc.vector.tensor_scalar(col(4 + k), col(4 + k), -BIG, None, ALU.max))

            ch.do(nc.vector.tensor_tensor_scan(pre, fwd_neg, score, -BIG, ALU.add, ALU.max))
            across(0, pre[:, CH - 1:CH], col(0), same[:, 0:1], False)
            ch.do(nc.vector.tensor_tensor_scan(pre, fwd_neg, score, col(4), ALU.add, ALU.max))
            ch.do(nc.vector.tensor_tensor_scan(tmp[:, ::-1], bwd_neg[:, ::-1], pre[:, ::-1], -BIG, ALU.add, ALU.max))
            across(1, tmp[:, 0:1], col(1), same[:, CH:CH + 1], True)
            ch.do(nc.vector.tensor_tensor_scan(tmp[:, ::-1], bwd_neg[:, ::-1], pre[:, ::-1], col(5), ALU.add, ALU.max))
            W4 = CH // 4
            for k in range(4):
                c = slice(k * W4, (k + 1) * W4)
                nc.vector.tensor_tensor(score[:, c], score[:, c], tmp[:, c], ALU.subtract).then_inc(shifted, 1)
            v.wait_ge(shifted, 4)
            nc.vector.memset(r1[:, 0:T2 * TAB], 0.0).then_inc(acc_zero, 1)
            for i in range(TA):
                u = i % 2
                v.wait_ge(etT_ready.sem, i + 1)
                w = 512 if i < TA - 1 else P * len(groups(i))
                nc.vector.tensor_copy(E_all[:, i * 64:i * 64 + w // H, :].rearrange("p t h -> p (t h)"),
                                      pb[6 + u][:, 0:w]).then_inc(etT_out.sem, 1)
            v.wait_ge(etT_out.sem, TA)
            v.wait_ge(x_cols_in, 2 * 16 * NX)
            ch.do(nc.vector.scalar_tensor_tensor(dst_f[:, :], nt_f[:, :], -float(P), dst_f[:, :], ALU.mult, ALU.add))
            ch.do(nc.vector.tensor_tensor(dst_f[:, ET:VT], dst_f[:, ET:VT], L["never"][:, :], ALU.subtract))
            v.wait_ge(acc_zero, 1)
            v.wait_ge(e_extra, 16 * NX)

            def add(i, q):
                nt4 = v.value_load(L["nt_pack"][0:1, bass.ds(i * 4 + q, 1)], min_val=0, max_val=NT ** 4 - 1)
                summed.wait(v, i, q + 1)
                for e in range(PR):
                    c = q * PR + e
                    nt = v.snap(nt4 % NT)
                    if e < PR - 1:
                        nt4 = v.snap(nt4 // NT)
                    if c:
                        added.wait(v, i, c)
                    else:
                        added.wait_before(v, i, 4 * PR)
                    a = acc[:, bass.ds(nt, 1), :]
                    nc.vector.tensor_tensor(a, a, pb[PR * (q % 2) + e][:, 0:TAB].rearrange("p (o d) -> p o d", o=1),
                                            ALU.add).then_inc(added.sem, 1)

            def second(i):
                for q in range(4):
                    u, t = q % 2, bass.ds((i * 4 + q) * PR, PR)
                    row_in[q].wait(v, i, PR)
                    if q >= 2:
                        summed.wait(v, i, q - 1)
                    else:
                        summed.wait_before(v, i, q + 3)
                    nc.vector.tensor_tensor(S[:, u, :, :], iota_f[:, :].unsqueeze(1).to_broadcast([P, PR, P]),
                                            dst_f[:, t].unsqueeze(2).to_broadcast([P, PR, P]), ALU.is_equal)
                    nc.vector.tensor_tensor(msg[:, u, :, :].rearrange("p e (h r) -> p (e h) r", r=ROW),
                                            rows[:, q, :, :].rearrange("p e (h r) -> p (e h) r", r=ROW),
                                            E_all[:, t, :].rearrange("p t h -> p (t h)").unsqueeze(2)
                                            .to_broadcast([P, PR * H, ROW]), ALU.mult).then_inc(msg_ready.sem, 1)
                    if q:
                        add(i, q - 1)
                    elif not (isinstance(i, int) and i == 0):
                        add(i - 1, 3)
            turns(v, TB, second)
            add(TB - 1, 3)

        @block.scalar
        def _(s):
            def extra_dst():
                for n in range(NX):
                    t = s.value_load(tau_i[0:1, n:n + 1], min_val=0, max_val=ET - 1)
                    s.dma_start(x_dst[n // EG][:, (n % EG) * P:(n % EG + 1) * P],
                                A["dst_flat"][:, bass.ds(t * P, P)].to_broadcast([P, P])).then_inc(x_dst_in[n // EG], 16)
                s.wait_ge(x_built, 1)
                s.dma_start(dstb, A["dst_flat"][:, 0:EG * P].to_broadcast([P, EG * P])).then_inc(dst_in.sem, 16)
            MIX.act_start(s, extra_dst)
            MIX.first(MIX.act, s)
            s.wait_ge(st_built.sem, 1)
            s.dma_start(dstb, A["dst_flat"][:, EG * P:2 * EG * P].to_broadcast([P, EG * P])).then_inc(dst_in.sem, 16)

            def body(i):
                for q in groups(i):
                    u, g = q % 2, 4 * i + q
                    def next_dst():
                        if not (isinstance(g, int) and g == NG - 1):
                            st_built.wait(s, i, q + 2)
                            s.dma_start(dstb, A["dst_flat"][:, bass.ds((g + 2) * EG * P, EG * P)]
                                        .to_broadcast([P, EG * P])).then_inc(dst_in.sem, 16)
                    MIX.slot(MIX.act, s, i, q, next_dst)
                    scT_ready.wait(s, i, q + 1)
                    if q < 2:
                        sat_stored[u].wait_before(s, i, 2)
                    else:
                        sat_stored[u].wait(s, i, 1)
                    nc.scalar.activation(satb[:, u, :], pb[7][:, u * P:(u + 1) * P], ACT.Copy).then_inc(scT_out.sem, 1)
                    scT_out.wait(s, i, q + 1)
                    s.dma_start(sat_d[:, bass.ds(g * EG, EG), :].rearrange("h t e -> t h e"),
                                satb[:, u, :]).then_inc(sat_stored[u].sem, 16)
            all_turns(s, body)
            s.dma_start(sat_d[:, ET:VT, :], A["zeros"]).then_inc(sat_stored[1].sem, 16)
            MIX.rest(MIX.act, s, TA - 1, groups(TA - 1))
            s.wait_ge(MIX.fx_stored.sem, 16 * NB)
            s.wait_ge(MIX.fx_sq.sem, 4 * NB)
            s.sem_inc(mixed, 1)
            for k in range(4):
                W4 = CH // 4
                s.wait_ge(shifted, k + 1)
                nc.scalar.activation(score[:, k * W4:(k + 1) * W4], score[:, k * W4:(k + 1) * W4], ACT.Exp)\
                    .then_inc(weighed, 1)

        @block.tensor
        def _(pe):
            def extra_rows():
                for j in range(3):
                    pe.wait_ge(x_built, j + 1)
                    if j:
                        pe.wait_ge(x_used, j)
                    for e in range(EG):
                        ins = nc.tensor.matmul(pb[6][:, e * 3 * H:(e + 1) * 3 * H], st[:, e, :],
                                               L["sd_nodes"][:, j * EG + e + 1, :], start=True, stop=True)
                    ins.then_inc(x_sde, 1)
                pe.wait_ge(x_used, 3)
            MIX.pe_start(pe, extra_rows)
            MIX.first(MIX.pe, pe)

            def body(i):
                for q in groups(i):
                    u, g = q % 2, 4 * i + q
                    nts = []
                    for k in range(4):
                        t4 = pe.value_load(L["nt_pack"][0:1, bass.ds(g * 4 + k, 1)], min_val=0, max_val=NT ** 4 - 1)
                        for e in range(4):
                            nts.append(pe.snap(t4 % NT))
                            if e < 3:
                                t4 = pe.snap(t4 // NT)
                    st_built.wait(pe, i, q + 1)
                    if q:
                        sde_used.wait(pe, i, q)
                    else:
                        sde_used.wait_before(pe, i, 4)
                    for e in range(EG):
                        ins = nc.tensor.matmul(pb[6][:, e * 3 * H:(e + 1) * 3 * H], st[:, e, :],
                                               L["sd_nodes"][:, bass.ds(nts[e], 1), :], start=True, stop=True)
                    ins.then_inc(sde_ready.sem, 1)
                    MIX.slot(MIX.pe, pe, i, q)
                    score_ready.wait(pe, i, q + 1)
                    if q:
                        scT_out.wait(pe, i, q)
                    else:
                        scT_out.wait_before(pe, i, 4)
                    nc.tensor.transpose(pb[7][:, u * P:(u + 1) * P], edge_pre[:, u, :], ident[:, :])\
                        .then_inc(scT_ready.sem, 1)
            all_turns(pe, body)
            MIX.rest(MIX.pe, pe, TA - 1, groups(TA - 1))
            for k in range(2):
                pe.wait_ge(diag_ready, k + 1)
                for j in range(3):
                    ins = nc.tensor.matmul(pb[5][:, j * P:(j + 1) * P], ones[:, :], carry[:, j, :], start=True, stop=True)
                ins.then_inc(diag_sum, 1)
            for i in range(TA):
                u = i % 2
                pe.wait_ge(et_in[u].sem, 64 * (i // 2) + 16 * len(groups(i)))
                if i > 1:
                    pe.wait_ge(etT_out.sem, i - 1)
                for k in groups(i):
                    ins = nc.tensor.transpose(pb[6 + u][:, k * P:(k + 1) * P], etb[:, u, k, :], ident[:, :])
                ins.then_inc(etT_ready.sem, 1)

            def second(i):
                for q in range(4):
                    u = q % 2
                    msg_ready.wait(pe, i, q + 1)
                    if q >= 2:
                        added.wait(pe, i, (q - 1) * PR)
                    else:
                        added.wait_before(pe, i, (q + 3) * PR)
                    for e in range(PR):
                        ins = nc.tensor.matmul(pb[PR * u + e][:, 0:TAB], S[:, u, e, :], msg[:, u, e, :], start=True,
                                               stop=True)
                    ins.then_inc(summed.sem, 1)
            turns(pe, TB, second)


T2 = NT + 1
PAIRS = T2 // 2
FT = PAIRS // 2
CTRL_TIES = 6


def combine_and_ffn(nc, ctx, sem, L, out):
    A, pb, ident, ones, sc = L["A"], L["pb"], L["ident"], L["ones"], L["sc"]
    acc = L["r1"][:, 0:T2 * TAB].rearrange("p (t d) -> p t d", d=TAB)
    area = L["Area"](L["r2"])
    h1 = area.take(HC, 512)
    xT = area.take(KD, 512)
    tri = area.take(P)
    xs = area.take(BLK, D)
    area = L["Area"](L["r3"])
    xn2 = area.take(NTP, D)
    area = L["Area"](L["r4"])
    cmp = L["r4"][:, 0:15 * T2].rearrange("p (c t) -> p c t", c=15)
    xb, fb = area.take(2, 2 * D), area.take(2, 2 * D)
    wk, ek = area.take(2, 2 * D), area.take(2, 2 * D)
    digits = area.take(15)
    area = L["Area"](L["E_all"][:, :, :].rearrange("p t h -> p (t h)"))
    w1 = area.take(KD, HF)
    w2 = area.take(HC, D)
    grow, brow, wrow, b2row = (area.take(D) for _ in range(4))
    b1 = area.take(HC)
    br = area.take(1)
    rec = area.take(T2, H)
    stats = area.take(T2, 6)
    wts, key_hi, key_lo, sel, wsel, t0, t1 = (area.take(T2) for _ in range(7))
    ki, km = area.take(T2, dt=I32), area.take(T2, dt=I32)
    cand, cnt, tot = area.take(15), area.take(15), area.take(15)
    base, need, top = area.take(1), area.take(1), area.take(1)

    c = lambda name, per, by=1: Count(sem(name), per, by)
    w_in = sem("ffn_w_in")
    dve3 = sem("dve3")
    tri_set = sem("tri_set")
    xn_in = [c(f"xn_in{u}", 1, 16) for u in range(2)]
    xf_in = [c(f"xf_in{u}", 2, 16) for u in range(2)]
    c1_used, c2_min, c2_exp, c2_used = c("c1_used", 2), c("c2_min", 2), c("c2_exp", 2), c("c2_used", 2)
    fx_root, fx_tanh, fx_n = sem("fx_root"), sem("fx_tanh"), sem("fx_n")
    var1, std1, var2, std2 = sem("var1"), sem("std1"), sem("var2"), sem("std2")
    x2_ready = sem("x2_ready")
    xT2_ready, xT2_out = c("xT2_ready", 2), c("xT2_out", 2)
    xs_ready, c3_done = c("xs_ready", 1), c("c3_done", 2)
    h_mm, h_gelu = c("h_mm", HC), c("h_gelu", HC)
    y_mm, y_out = c("y_mm", BLK), c("y_out", BLK)
    counted, count_all = sem("counted"), sem("count_all")
    ties_ready, ties = sem("ties_ready"), sem("ties")
    final, out_stored = c("final", BLK), sem("out_stored")
    NFB = (T2 + BLK - 1) // BLK

    def pairs(i):
        return (0, 1) if not isinstance(i, int) or i < FT else (0,)

    def all_pairs(eng, body):
        body(0)
        with eng.Fori(1, FT) as i:
            body(i)
        body(FT)

    def tiles(i):
        return range(BLK) if not isinstance(i, int) or i < NFB - 1 else range(T2 - BLK * (NFB - 1))

    def all_blocks(eng, body, between=None):
        body(0)
        if between:
            with eng.Fori(1, CTRL_TIES) as i:
                body(i)
            between()
            with eng.Fori(CTRL_TIES, NFB - 1) as i:
                body(i)
        else:
            with eng.Fori(1, NFB - 1) as i:
                body(i)
        body(NFB - 1)

    with nc.Block() as block:
        @block.sync
        def _(sp):
            def c1(i):
                for u in pairs(i):
                    c1_used.wait_before(sp, i, u + 1)
                    sp.dma_start(xb[:, u, :], L["xn_d"][bass.ds(4 * i + 2 * u, 2), :, :].rearrange("t p d -> p t d"))\
                        .then_inc(xn_in[u].sem, 16)
            all_pairs(sp, c1)
            sp.dma_start(w1, A["w1"].rearrange("(k p) n -> p k n", p=P)).then_inc(w_in, 16)
            sp.dma_start(w2, A["w2"].rearrange("(k p) n -> p k n", p=P)).then_inc(w_in, 16)
            for dst, name, n in ((grow, "gamma", D), (brow, "beta", D), (wrow, "wr", D), (b2row, "b2", D), (br, "br", 1)):
                sp.dma_start(dst, A[name].to_broadcast([P, n])).then_inc(w_in, 16)
            sp.dma_start(b1, A["b1"]).then_inc(w_in, 16)
            sp.wait_ge(c1_used.sem, PAIRS)

            def c2(i):
                for u in pairs(i):
                    c2_used.wait_before(sp, i, u + 1)
                    sp.dma_start(xb[:, u, :], A["x"].rearrange("(t p) d -> p t d", p=P)[:, bass.ds(4 * i + 2 * u, 2), :])\
                        .then_inc(xf_in[u].sem, 16)
                    sp.dma_start(fb[:, u, :], L["fx_d"][bass.ds(4 * i + 2 * u, 2), :, :].rearrange("t p d -> p t d"))\
                        .then_inc(xf_in[u].sem, 16)
            all_pairs(sp, c2)

            def store(i):
                n = len(tiles(i))
                final.wait(sp, i, n)
                sp.dma_start(out.rearrange("(t p) d -> p t d", p=P)[:, bass.ds(BLK * i, n), :],
                             acc[:, bass.ds(BLK * i, n), 0:D]).then_inc(out_stored, 16)
            all_blocks(sp, store)
            sp.wait_ge(out_stored, 16 * NFB)

        @block.gpsimd
        def _(g):
            g.memset(tri, 1.0).then_inc(tri_set, 1)
            g.wait_ge(tri_set, 1)
            g.affine_select(out=tri, in_=tri, compare_op=ALU.is_gt, fill=0.0, base=0, pattern=[[1, P]],
                            channel_multiplier=-1).then_inc(tri_set, 1)
            for k in range(9):
                g.wait_ge(counted, k + 1)
                g.partition_all_reduce(tot, cnt, P, bass.bass_isa.ReduceOp.add).then_inc(count_all, 1)

        @block.vector
        def _(v_):
            v = nc.vector
            ch = Chain(v_, dve3)
            n, f = sc[:, 5, :], sc[:, 6, :]
            v.wait_ge(fx_root, 1)
            v.tensor_scalar(n, n, MINN, None, ALU.max).then_inc(fx_n, 1)
            ch.do(v.tensor_scalar(rec, acc[:, :, HD::ROW], 1e-30, None, ALU.max))
            ch.do(v.reciprocal(rec, rec))
            v.wait_ge(fx_tanh, 1)
            ch.do(v.tensor_scalar(f, f, MAXN, None, ALU.min))
            ch.do(v.reciprocal(n, n))
            ch.do(v.tensor_tensor(f, f, n, ALU.mult))

            def t4(i, u):
                return bass.ds(4 * i + 2 * u, 2)

            def two(ap):
                return ap.rearrange("p (t d) -> p t d", d=D)

            def c1(i):
                ch.turn(i, 4)
                for u in pairs(i):
                    a = acc[:, t4(i, u), :]
                    ch.do(v.tensor_tensor(wk[:, u, :].rearrange("p (t h d) -> p t h d", h=H, d=HD),
                                          a.rearrange("p t (h r) -> p t h r", r=ROW)[:, :, :, 0:HD],
                                          rec[:, t4(i, u), :].unsqueeze(3).to_broadcast([P, 2, H, HD]), ALU.mult))
                    xn_in[u].wait(v_, i, 1)
                    ch.do(v.tensor_tensor(a[:, :, 0:D], two(wk[:, u, :]), two(xb[:, u, :]), ALU.add))
                    for k in range(2):
                        t = bass.ds(4 * i + 2 * u + k, 1)
                        ins = v.bn_stats(stats[:, t, :], acc[:, t, 0:D])
                        if k:
                            ins.then_inc(c1_used.sem, 1)
            ch.loop()
            all_pairs(v_, c1)
            v_.wait_ge(c1_used.sem, PAIRS)
            row_moments(nc, ch, stats, sc, T2)
            v.tensor_scalar(sc[:, 3, 0:T2], sc[:, 3, 0:T2], 1e-5, None, ALU.add).then_inc(var1, 1)
            v_.wait_ge(std1, 1)
            ch.do(v.reciprocal(sc[:, 3, 0:T2], sc[:, 4, 0:T2]))
            v_.wait_ge(w_in, 8 * 16)

            def c2(i):
                ch.turn(i, 16)
                for u in pairs(i):
                    for k in range(2):
                        t = bass.ds(4 * i + 2 * u + k, 1)
                        ch.step(v.tensor_scalar(wk[:, u, k * D:(k + 1) * D], acc[:, t, 0:D].rearrange("p o d -> p (o d)"),
                                                sc[:, 2, t], sc[:, 3, t], ALU.subtract, ALU.mult))
                    ch.done()
                    w = two(wk[:, u, :])
                    ch.do(v.tensor_tensor(w, w, grow.unsqueeze(1).to_broadcast([P, 2, D]), ALU.mult))
                    ch.do(v.tensor_tensor(w, w, brow.unsqueeze(1).to_broadcast([P, 2, D]), ALU.add))
                    v.tensor_scalar(ek[:, u, :], wk[:, u, :], 0.0, None, ALU.min).then_inc(c2_min.sem, 1)
                for u in pairs(i):
                    w = wk[:, u, :]
                    c2_exp.wait(v_, i, u + 1)
                    ch.do(v.scalar_tensor_tensor(w, w, 0.0, ek[:, u, :], ALU.max, ALU.add))
                    xf_in[u].wait(v_, i, 2)
                    ch.do(v.scalar_tensor_tensor(w, w, -1.0, xb[:, u, :], ALU.add, ALU.add))
                    for k in range(2):
                        t = bass.ds(4 * i + 2 * u + k, 1)
                        cs = slice(k * D, (k + 1) * D)
                        ch.step(v.scalar_tensor_tensor(acc[:, t, 0:D].rearrange("p o d -> p (o d)"), fb[:, u, cs],
                                                       sc[:, 6, t], wk[:, u, cs], ALU.mult, ALU.add))
                    ch.done()
                    for k in range(2):
                        t = bass.ds(4 * i + 2 * u + k, 1)
                        ins = v.bn_stats(stats[:, t, :], acc[:, t, 0:D])
                        if k:
                            ins.then_inc(c2_used.sem, 1)
            ch.loop()
            all_pairs(v_, c2)
            v_.wait_ge(c2_used.sem, PAIRS)
            row_moments(nc, ch, stats, sc, T2)
            v.tensor_scalar(sc[:, 3, 0:T2], sc[:, 3, 0:T2], 1e-5, None, ALU.add).then_inc(var2, 1)
            v_.wait_ge(std2, 1)
            ch.do(v.reciprocal(sc[:, 3, 0:T2], sc[:, 4, 0:T2]))

            def c3(i):
                ch.turn(i, 4)
                for u in pairs(i):
                    for k in range(2):
                        t = bass.ds(4 * i + 2 * u + k, 1)
                        v.tensor_scalar(xn2[:, t, :], acc[:, t, 0:D], sc[:, 2, t], sc[:, 3, t], ALU.subtract, ALU.mult)\
                            .then_inc(x2_ready, 1)
                    v_.wait_ge(x2_ready, 4 * i + 2 * u + 2)
                    tt = t4(i, u)
                    ch.do(v.tensor_tensor(two(wk[:, u, :]), xn2[:, tt, :], wrow.unsqueeze(1).to_broadcast([P, 2, D]), ALU.mult))
                    ch.step(v.reduce_sum(wts[:, tt], two(wk[:, u, :]), mybir.AxisListType.X))
                    v.tensor_tensor(acc[:, tt, 0:D], acc[:, tt, 0:D], xn2[:, tt, :], ALU.add).then_inc(c3_done.sem, 1)
            ch.do(v.memset(xn2[:, T2:NTP, :], 0.0))
            ch.loop()
            all_pairs(v_, c3)
            ch.done()
            v_.wait_ge(c3_done.sem, PAIRS)
            v_.sem_inc(c3_done.sem, 1)
            ch.do(v.tensor_scalar(wts, wts, br, None, ALU.add))
            wbits = wts.bitcast(I32)
            ch.do(v.tensor_single_scalar(km, wbits, 31, op=ALU.arith_shift_right))
            ch.do(v.tensor_single_scalar(km, km, 0x7FFFFFFF, op=ALU.bitwise_and))
            ch.do(v.tensor_tensor(ki, wbits, km, ALU.bitwise_xor))
            ch.do(v.tensor_single_scalar(km, ki, 16, op=ALU.arith_shift_right))
            ch.do(v.tensor_copy(key_hi, km))
            ch.do(v.tensor_single_scalar(km, ki, 0xFFFF, op=ALU.bitwise_and))
            ch.do(v.tensor_copy(key_lo, km))
            ch.do(v.tensor_scalar(key_hi, key_hi, 32768.0, None, ALU.add))
            ch.do(v.memset(key_hi[:, NT:T2], -1.0))
            last = key_hi[:, NT - 1:NT]
            ch.do(v.tensor_scalar(t0[:, 0:1], L["pcol"][:, 0:1], float(N - (NT - 1) * P), None, ALU.is_lt))
            ch.do(v.tensor_scalar(last, last, 1.0, t0[:, 0:1], ALU.add, ALU.mult))
            ch.do(v.tensor_scalar(last, last, -1.0, None, ALU.add))
            ch.do(v.tensor_scalar(digits, L["iota_f"][:, 1:16], 1.0, None, ALU.mult))
            rounds = [0]

            def count(k):
                ch.done()
                v_.sem_inc(counted, 1)
                v_.wait_ge(count_all, k + 1)

            def search(keys, half):
                ch.do(v.memset(base, 0.0))
                for r in range(4):
                    step = float(16 ** (3 - r))
                    ch.do(v.tensor_scalar(cand, digits, step, base, ALU.mult, ALU.add))
                    ch.do(v.tensor_tensor(cmp, keys.unsqueeze(1).to_broadcast([P, 15, T2]),
                                          cand.unsqueeze(2).to_broadcast([P, 15, T2]), ALU.is_ge))
                    ch.do(v.reduce_sum(cnt, cmp, mybir.AxisListType.X))
                    count(4 * half + r)
                    ch.do(v.tensor_scalar(cand, tot, float(KSEL), None, ALU.is_ge))
                    ch.do(v.reduce_sum(need, cand, mybir.AxisListType.X))
                    ch.do(v.scalar_tensor_tensor(base, need, step, base, ALU.mult, ALU.add))
            search(key_hi, 0)
            ch.step(v.tensor_scalar(t0, key_hi, base, None, ALU.is_equal))
            ch.do(v.tensor_scalar(t1, key_hi, base, 1.0e6, ALU.is_gt, ALU.mult))
            ch.do(v.tensor_scalar(key_lo, key_lo, 1.0, None, ALU.add))
            ch.do(v.tensor_tensor(key_lo, key_lo, t0, ALU.mult))
            ch.do(v.tensor_tensor(key_lo, key_lo, t1, ALU.add))
            ch.do(v.tensor_scalar(key_lo, key_lo, -1.0, None, ALU.add))
            search(key_lo, 1)
            ch.step(v.tensor_scalar(sel, key_lo, base, None, ALU.is_gt))
            ch.step(v.tensor_scalar(t0, key_lo, base, None, ALU.is_equal))
            ch.step(v.memset(cnt, 0.0))
            ch.done()
            ch.do(v.reduce_sum(cnt[:, 0:1], sel, mybir.AxisListType.X))
            count(8)
            ch.do(v.tensor_scalar(need, tot[:, 0:1], -1.0, float(KSEL), ALU.mult, ALU.add))
            v_.sem_inc(ties_ready, 1)
            v_.wait_ge(ties, 1)
            ch.do(v.tensor_copy(t1, pb[7][:, 0:T2]))
            ch.do(v.tensor_tensor_scan(key_hi, t1, t1, 0.0, ALU.add, ALU.max))
            ch.do(v.tensor_tensor(key_hi, key_hi, t1, ALU.subtract))
            ch.do(v.tensor_tensor(key_hi, key_hi, pb[6][:, 0:T2], ALU.add))
            ch.do(v.tensor_scalar(key_hi, key_hi, need, None, ALU.is_lt))
            ch.do(v.tensor_tensor(key_hi, key_hi, t0, ALU.mult))
            ch.do(v.tensor_tensor(sel, sel, key_hi, ALU.add))
            ch.do(v.tensor_tensor(wsel, sel, wts, ALU.mult))

            def last_sum(i):
                for j in tiles(i):
                    t = bass.ds(BLK * i + j, 1)
                    a = acc[:, t, 0:D].rearrange("p o d -> p (o d)")
                    ch.turn(i, BLK)
                    ch.k = j
                    ch.do(v.scalar_tensor_tensor(a, b2row, wsel[:, t], a, ALU.mult, ALU.add))
                    y_out.wait(v_, i, j + 1)
                    v.scalar_tensor_tensor(a, xn2[:, t, :].rearrange("p o d -> p (o d)"), wsel[:, t], a, ALU.mult, ALU.add)\
                        .then_inc(final.sem, 1)
            ch.loop()
            all_blocks(v_, last_sum)

        @block.scalar
        def _(s):
            act = nc.scalar.activation
            act(sc[:, 5, :], sc[:, 9, :], ACT.Sqrt).then_inc(fx_root, 1)
            s.wait_ge(fx_n, 1)
            act(sc[:, 6, :], sc[:, 5, :], ACT.Tanh).then_inc(fx_tanh, 1)
            s.wait_ge(var1, 1)
            act(sc[:, 4, 0:T2], sc[:, 3, 0:T2], ACT.Sqrt).then_inc(std1, 1)

            def c2(i):
                for u in pairs(i):
                    c2_min.wait(s, i, u + 1)
                    act(ek[:, u, :], ek[:, u, :], ACT.Exp).then_inc(c2_exp.sem, 1)
            all_pairs(s, c2)
            s.wait_ge(var2, 1)
            act(sc[:, 4, 0:T2], sc[:, 3, 0:T2], ACT.Sqrt).then_inc(std2, 1)
            s.wait_ge(w_in, 8 * 16)

            def fetch(b):
                c3_done.wait(s, b, 2)
                act(xs, xn2[:, bass.ds(BLK * b, BLK), :], ACT.Copy).then_inc(xs_ready.sem, 1)

            def transposed(b):
                for k in range(KD):
                    xT2_ready.wait(s, b, k + 1)
                    act(xT[:, k, :], pb[k][:, :], ACT.Copy).then_inc(xT2_out.sem, 1)

            def ffn(i):
                w = P * len(tiles(i))
                y_mm.wait_before(s, i, BLK)
                for m in range(HC):
                    h_mm.wait(s, i, m + 1)
                    act(h1[:, m, 0:w], pb[2 + m % 2][:, 0:w], ACT.Gelu_apprx_tanh, bias=b1[:, m:m + 1])\
                        .then_inc(h_gelu.sem, 1)
                if not (isinstance(i, int) and i == NFB - 1):
                    xT2_ready.wait(s, i, KD)
                    fetch(i + 1)
                    transposed(i + 1)
                for j in tiles(i):
                    y_mm.wait(s, i, j + 1)
                    act(xn2[:, bass.ds(BLK * i + j, 1), :].rearrange("p o d -> p (o d)"), pb[4 + j % 2][:, 0:D], ACT.Copy)\
                        .then_inc(y_out.sem, 1)
            fetch(0)
            transposed(0)
            all_blocks(s, ffn)

        @block.tensor
        def _(pe):
            mm = nc.tensor.matmul
            pe.wait_ge(w_in, 8 * 16)

            def transposes(b):
                xs_ready.wait(pe, b, 1)
                for k in range(KD):
                    for j in range(BLK):
                        ins = nc.tensor.transpose(pb[k][:, j * P:(j + 1) * P], xs[:, j, k * P:(k + 1) * P], ident[:, :])
                    ins.then_inc(xT2_ready.sem, 1)

            def ffn(i):
                w = P * len(tiles(i))
                for m in range(HC):
                    xT2_out.wait(pe, i, 2)
                    if m >= 2:
                        h_gelu.wait(pe, i, m - 1)
                    else:
                        h_gelu.wait_before(pe, i, HC + m - 1)
                    for k in range(KD):
                        ins = mm(pb[2 + m % 2][:, 0:w], w1[:, k, m * P:(m + 1) * P], xT[:, k, 0:w], start=k == 0, stop=k == 1)
                    ins.then_inc(h_mm.sem, 1)
                if not (isinstance(i, int) and i == NFB - 1):
                    transposes(i + 1)
                h_gelu.wait(pe, i, HC)
                for j in tiles(i):
                    if j >= 2:
                        y_out.wait(pe, i, j - 1)
                    else:
                        y_out.wait_before(pe, i, BLK + j - 1)
                    for m in range(HC):
                        ins = mm(pb[4 + j % 2][:, 0:D], h1[:, m, j * P:(j + 1) * P], w2[:, m, :], start=m == 0,
                                 stop=m == HC - 1)
                    ins.then_inc(y_mm.sem, 1)

            def count_ties():
                pe.wait_ge(tri_set, 2)
                pe.wait_ge(ties_ready, 1)
                mm(pb[6][:, 0:T2], tri, t0, start=True, stop=True)
                mm(pb[7][:, 0:T2], ones[:, :], t0, start=True, stop=True).then_inc(ties, 1)
            transposes(0)
            all_blocks(pe, ffn, count_ties)


def kernel(x, src, dst, L0_gnn_W, L0_gnn_a_src, L0_gnn_a_dst, L0_gnn_gamma, L0_gnn_beta, L0_mix_w_qkv,
           L0_mix_bn_gamma, L0_mix_bn_beta, L0_mix_w_dw, L0_mix_w_pw, L0_mix_w_res, L0_mix_b_res,
           L0_ffn_attention_mask, L0_ffn_wr, L0_ffn_br, L0_ffn_w1, L0_ffn_b1, L0_ffn_w2, L0_ffn_b2):
    import concourse.bacc as bacc
    from concourse.bass_utils import run_bass_kernel_spmd

    def arr(a):
        return np.ascontiguousarray(a)

    x_pad = np.zeros((NTP * P, D), np.float32)
    x_pad[:N] = x
    src_pad = np.zeros((VT + 2 * EG) * P, np.int32)
    src_pad[:E] = src
    dst_pad = np.full(VT * P + 2, PAD_DST, np.int32)
    dst_pad[0] = -1
    dst_pad[-1] = -2
    dst_pad[1:E + 1] = dst
    dst_main = dst_pad[1:-1]
    chunks = np.lib.stride_tricks.as_strided(dst_pad, (16, CH + 2), (CH * 4, 4))

    def by_role(w):
        return arr(np.asarray(w).reshape((8, 3, 32) + w.shape[1:]).swapaxes(0, 1).reshape((NQ,) + w.shape[1:]))

    pw = by_role(np.asarray(L0_mix_w_pw)[:, :, 0]).reshape(QC, 4, 32, 32)
    arrays = {
        "x": x_pad,
        "src_cols": arr(src_pad.reshape(-1, P).T),
        "dst_cols": arr(dst_main.reshape(VT, P).T),
        "dst_flat": arr(dst_main.reshape(1, VT * P)),
        "dst_chunks": arr(chunks),
        "first": arr(dst_main.reshape(VT, P)[:ET, 0].reshape(1, ET)),
        "W": arr(L0_gnn_W),
        "a_src": arr(L0_gnn_a_src).reshape(1, D),
        "a_dst": arr(L0_gnn_a_dst).reshape(1, D),
        "gamma": arr(L0_gnn_gamma).reshape(1, D),
        "beta": arr(L0_gnn_beta).reshape(1, D),
        "w_qkv": arr(by_role(np.asarray(L0_mix_w_qkv)[:, :, 2]).T),
        "bn_gamma": arr(by_role(L0_mix_bn_gamma).reshape(QC, P).T),
        "bn_beta": arr(by_role(L0_mix_bn_beta).reshape(QC, P).T),
        "w_dw": arr(by_role(np.asarray(L0_mix_w_dw)[:, 0, 2]).reshape(QC, P).T),
        "w_pw": arr(pw.transpose(1, 3, 0, 2).reshape(P, QC, 32)),
        "w_res": arr(np.asarray(L0_mix_w_res)[:, :, 0].T),
        "b_res": arr(L0_mix_b_res).reshape(1, D),
        "wr": arr(L0_ffn_wr).reshape(1, D),
        "br": arr(L0_ffn_br).reshape(1, 1),
        "w1": arr(L0_ffn_w1),
        "b1": arr(np.asarray(L0_ffn_b1).reshape(HC, P).T),
        "w2": arr(L0_ffn_w2),
        "b2": arr(L0_ffn_b2).reshape(1, D),
        "zeros": np.zeros((H, VT - ET, P), np.float32),
    }
    nc = bacc.Bacc("TRN2", target_bir_lowering=False, num_devices=1)
    A = {}
    for name, a in arrays.items():
        A[name] = nc.dram_tensor(name, a.shape, mybir.dt.from_np(a.dtype), kind="ExternalInput").ap()
    out = nc.dram_tensor("out", [T2 * P, D], F32, kind="ExternalOutput").ap()
    build(nc, A, out)
    r = run_bass_kernel_spmd(nc, [arrays], core_ids=[0])
    return np.asarray(r.results[0]["out"])[:N]
```

```python
from contextlib import ExitStack

import numpy as np

import concourse.bass as bass
from concourse import mybir

F32 = mybir.dt.float32
I32 = mybir.dt.int32
BF16 = mybir.dt.bfloat16
ALU = mybir.AluOpType
ACT = mybir.ActivationFunctionType

P = 128
N = 6250
D = 256
KD = D // P
E = 100000
H = 8
HD = D // H
ROW = HD + 1
TAB = H * ROW
NT = -(-N // P)
BLK = 4
NB = -(-NT // BLK)
NTP = NB * BLK
ET = -(-E // (16 * P)) * 16
EG = 16
NG = ET // EG
VT = ET + NT - 1
CH = VT * P // 16
NQ = 3 * D
QC = NQ // P
HF = 4 * D
HC = HF // P
PAD_DST = 1000000
BIG = 1.0e30
MAXN = float(np.float32(1.0 - 1e-5))
CAP = float(np.arctanh(np.float64(MAXN)))
MINN = 1e-15
KSEL = N // 2 - 1

assert VT % EG == 0 and VT == 832 and NTP * P == 512 * NB


class Count:

    def __init__(self, sem, per, by=1, before=0):
        self.sem, self.per, self.by, self.before = sem, per, by, before

    def wait(self, eng, i, c):
        eng.wait_ge(self.sem, (i * self.per + (self.before + c)) * self.by)

    def wait_before(self, eng, i, c):
        if not (isinstance(i, int) and i == 0):
            eng.wait_ge(self.sem, ((i - 1) * self.per + (self.before + c)) * self.by)


class Chain:

    def __init__(self, eng, sem):
        self.eng, self.sem, self.base, self.k = eng, sem, 0, 0

    def turn(self, i, per):
        self.base, self.k = self.start + i * per, 0

    def loop(self):
        self.start, self.base, self.k = self.base + self.k, self.base + self.k, 0

    def end(self, turns, per):
        assert self.k == per, (self.k, per)
        self.base, self.k = self.start + turns * per, 0

    def step(self, ins):
        ins.then_inc(self.sem, 1)
        self.k += 1

    def done(self):
        self.eng.wait_ge(self.sem, self.base + self.k)

    def do(self, ins):
        self.step(ins)
        self.done()


def turns(eng, n, body):
    body(0)
    if n > 1:
        with eng.Fori(1, n) as i:
            body(i)


def build(nc, A, out):
    with ExitStack() as ctx:
        def sb(name, shape, dt=F32):
            return ctx.enter_context(nc.sbuf_tensor(name, shape, dt))

        def sem(name):
            return ctx.enter_context(nc.semaphore(name))

        def dram(name, shape, dt=F32):
            return nc.dram_tensor(name, shape, dt).ap()

        table_d = dram("table_d", [NTP * P, TAB])
        ssrc_d = dram("ssrc_d", [NTP * P, H])
        xn_d = dram("xn_d", [NTP, P, D])
        fx_d = dram("fx_d", [NTP, P, D])
        sat_d = dram("sat_d", [H, VT, P])
        et_d = dram("et_d", [VT, H, P])

        pb = [ctx.enter_context(nc.psum_tensor(f"bank{i}", [P, 512], F32)) for i in range(8)]

        ident = sb("ident", [P, P])
        ones = sb("ones", [P, P])
        iota_f = sb("iota_f", [P, P])
        pcol = sb("pcol", [P, 2])
        src_sb = sb("src_sb", [P, VT + 2 * EG], I32)
        dst_f = sb("dst_f", [P, VT])
        nt_f = sb("nt_f", [P, VT])
        nodecol = sb("nodecol", [P, VT])
        nt_pack = sb("nt_pack", [1, VT // 4], I32)
        tau_i = sb("tau_i", [1, NT - 1], I32)
        never = sb("never", [P, NT - 1])
        sc = sb("sc", [P, 12, NTP])
        sd_nodes = sb("sd_nodes", [P, NTP, 3 * H], BF16)
        E_all = sb("E_all", [P, VT, H])
        idx = sb("idx", [P, 4, EG], I32)
        grab = sb("grab", [P, 4, EG, H])

        r1 = sb("r1", [P, NTP * D + 8])
        r2 = sb("r2", [P, CH + 8])
        r3 = sb("r3", [P, CH + 8 * 4 * TAB + 8])
        r4 = sb("r4", [P, 4640])
        xn = r1[:, 0:NTP * D].rearrange("p (t d) -> p t d", d=D)
        sde = r2[:, 0:CH].rearrange("p (t h) -> p t h", h=H)

        class Area:
            def __init__(self, region):
                self.region, self.at = region, 0

            def take(self, *shape, dt=F32):
                n = int(np.prod(shape))
                v = self.region[:, self.at:self.at + n]
                self.at += n
                if dt != F32:
                    v = v.bitcast(dt)
                if len(shape) == 2:
                    v = v.rearrange("p (a b) -> p a b", b=shape[1])
                elif len(shape) == 3:
                    v = v.rearrange("p (a b c) -> p a b c", b=shape[1], c=shape[2])
                return v

        prologue(nc, ctx, sem, locals())
        edges_and_mix(nc, ctx, sem, locals())
        combine_and_ffn(nc, ctx, sem, locals(), out)


def prologue(nc, ctx, sem, L):
    A, pb, ident, ones, xn, sc = L["A"], L["pb"], L["ident"], L["ones"], L["xn"], L["sc"]
    iota_f, pcol, dst_f, nt_f, nodecol = (L[k] for k in ("iota_f", "pcol", "dst_f", "nt_f", "nodecol"))
    U = BLK
    area = L["Area"](L["r3"])
    W_sb = area.take(KD, D + 2 * H)
    a_sb = area.take(2, D)
    wa_tmp = area.take(D)
    xr = area.take(U, D)
    xnT = area.take(U, D)
    trow = area.take(U, TAB)
    srow = area.take(U, H)
    sd = area.take(NTP, H)
    stats = area.take(NTP, 6)
    first_i = area.take(ET, dt=I32)
    cmp = area.take(ET)
    dst_i = area.take(VT, dt=I32)
    iota_i = area.take(P, dt=I32)
    pcol_i = area.take(1, dt=I32)
    cnt = area.take(1)
    cntd = area.take(NT - 1)
    pack_f = area.take(VT // 4)
    tau_f = area.take(NT - 1)

    x_in = [sem(f"x_in{j}") for j in range(4)]
    r2_zero = sem("r2_zero")
    w_in, edge_in, src_in = sem("w_in"), sem("edge_in"), sem("src_in")
    const_set, iota_set = sem("const_set"), sem("iota_set")
    dve_pro = sem("dve_pro")
    var_ready, std_ready = sem("var_ready"), sem("std_ready")
    xn_ready = sem("xn_ready")
    wa_ready = sem("wa_ready")
    xT_ready, xT_out = Count(sem("xT_ready"), U), Count(sem("xT_out"), U)
    proj_ready, proj_out = Count(sem("proj_ready"), U), Count(sem("proj_out"), U)
    stored = Count(sem("rows_stored"), 2, 16)
    xn_stored = sem("xn_stored")
    xr_ready = Count(sem("xr_ready"), U)
    cnt_ready, cnt_bc = sem("cnt_ready"), sem("cnt_bc")
    TURNS = NTP // U
    LOADS = ((0, 12), (12, 24), (24, 36), (36, NTP))

    T_bank, proj_bank = pb[0:4], pb[4:8]

    with nc.Block() as block:
        @block.sync
        def _(sp):
            sp.dma_start(first_i, A["first"].to_broadcast([P, ET])).then_inc(edge_in, 16)
            sp.dma_start(dst_i, A["dst_cols"]).then_inc(edge_in, 16)
            for j, (t0, t1) in enumerate(LOADS):
                sp.dma_start(xn[:, t0:t1, :], A["x"].rearrange("(t p) d -> p t d", p=P)[:, t0:t1, :]).then_inc(x_in[j], 16)
            sp.dma_start(W_sb[:, :, 0:D], A["W"].rearrange("(k p) n -> p k n", p=P)).then_inc(w_in, 16)
            for j, name in enumerate(("a_src", "a_dst")):
                sp.dma_start(a_sb[:, j, :], A[name].to_broadcast([P, D])).then_inc(w_in, 16)
            sp.dma_start(L["src_sb"][:, :], A["src_cols"]).then_inc(src_in, 16)

            def body(i):
                proj_out.wait(sp, i, U)
                rows = bass.ds(i * (U * P), U * P)
                sp.dma_start(L["table_d"][rows, :].rearrange("(u p) d -> p u d", p=P), trow).then_inc(stored.sem, 16)
                sp.dma_start(L["ssrc_d"][rows, :].rearrange("(u p) d -> p u d", p=P), srow).then_inc(stored.sem, 16)
            turns(sp, TURNS, body)
            sp.wait_ge(xn_ready, NTP)
            sp.dma_start(L["xn_d"].rearrange("t p d -> p t d"), xn).then_inc(xn_stored, 16)
            sp.wait_ge(xn_stored, 16)
            sp.wait_ge(src_in, 16)
            sp.wait_ge(stored.sem, TURNS * 32)

        @block.gpsimd
        def _(g):
            nc.gpsimd.memset(ones[:, :], 1.0).then_inc(const_set, 1)
            nc.gpsimd.memset(ident[:, :], 0.0).then_inc(const_set, 1)
            g.wait_ge(const_set, 2)
            nc.gpsimd.affine_select(out=ident[:, :], in_=ident[:, :], compare_op=ALU.not_equal, fill=1.0, base=0,
                                    pattern=[[-1, P]], channel_multiplier=1).then_inc(const_set, 1)
            nc.gpsimd.iota(iota_i, pattern=[[1, P]], base=0, channel_multiplier=0).then_inc(iota_set, 1)
            nc.gpsimd.iota(pcol_i, pattern=[[0, 1]], base=0, channel_multiplier=1).then_inc(iota_set, 1)
            nc.gpsimd.memset(L["r2"][:, :], 0.0).then_inc(r2_zero, 1)
            g.wait_ge(r2_zero, 1)

        @block.vector
        def _(v):
            ch = Chain(v, dve_pro)
            v.wait_ge(edge_in, 32)
            v.wait_ge(iota_set, 2)
            v.wait_ge(const_set, 3)
            ch.do(nc.vector.tensor_single_scalar(first_i, first_i, 7, op=ALU.arith_shift_right))
            ch.step(nc.vector.tensor_copy(iota_f[:, :], iota_i))
            ch.step(nc.vector.tensor_copy(pcol[:, 0:1], pcol_i))
            ch.do(nc.vector.tensor_scalar(nt_f[:, 0:ET], first_i, float(NT - 1), None, ALU.min))
            ch.step(nc.vector.tensor_copy(nt_f[:, ET:VT], iota_f[:, 1:NT]))
            ch.step(nc.vector.tensor_copy(dst_f[:, :], dst_i))
            ch.do(nc.vector.tensor_scalar(pcol[:, 1:2], pcol[:, 0:1], 1.0, None, ALU.add))
            ch.do(nc.vector.tensor_scalar(cmp, nt_f[:, 0:ET], pcol[:, 1:2], None, ALU.is_lt))
            ch.do(nc.vector.reduce_sum(cnt, cmp, mybir.AxisListType.X))
            nc.vector.tensor_scalar(cntd, ident[:, 0:NT - 1], cnt, None, ALU.mult).then_inc(cnt_ready, 1)
            v.wait_ge(cnt_bc, 1)
            ch.do(nc.vector.tensor_scalar(L["never"][:, :], pb[4][:, 0:NT - 1], 0.5, 1.0e7,
                                          ALU.is_lt, ALU.mult))
            ch.do(nc.vector.tensor_scalar(tau_f, pb[4][:, 0:NT - 1], -1.0, 0.0, ALU.add, ALU.max))
            ch.step(nc.vector.tensor_copy(L["tau_i"][0:1, :], tau_f[0:1, :]))
            ch.do(nc.vector.tensor_scalar(nodecol[:, :], nt_f[:, :], float(P), pcol[:, 0:1], ALU.mult, ALU.add))
            ch.do(nc.vector.tensor_tensor(nodecol[:, ET:VT], nodecol[:, ET:VT], L["never"][:, :], ALU.add))
            four = nt_f[0:1, :].rearrange("p (k j) -> p k j", j=4)
            ch.do(nc.vector.tensor_scalar(pack_f[0:1, :], four[:, :, 3], float(NT), None, ALU.mult))
            for j in (2, 1):
                ch.do(nc.vector.tensor_tensor(pack_f[0:1, :], pack_f[0:1, :], four[:, :, j], ALU.add))
                ch.do(nc.vector.tensor_scalar(pack_f[0:1, :], pack_f[0:1, :], float(NT), None, ALU.mult))
            ch.do(nc.vector.tensor_tensor(pack_f[0:1, :], pack_f[0:1, :], four[:, :, 0], ALU.add))
            ch.do(nc.vector.tensor_copy(L["nt_pack"][0:1, :], pack_f[0:1, :]))
            ch.loop()
            for j, (t0, t1) in enumerate(LOADS):
                v.wait_ge(x_in[j], 16)
                with v.Fori(t0 // 4, t1 // 4) as i:
                    ch.turn(i, 4)
                    for u in range(4):
                        t = bass.ds(4 * i + u, 1)
                        ch.step(nc.vector.bn_stats(stats[:, t, :], xn[:, t, :]))
            ch.end(NTP // 4, 4)
            ch.done()
            row_moments(nc, ch, stats, sc)
            ch.do(nc.vector.tensor_scalar(sc[:, 5, :], sc[:, 3, :], 1e-5, None, ALU.add))
            ch.do(nc.vector.reciprocal(sc[:, 5, :], sc[:, 5, :]))
            ch.do(nc.vector.scalar_tensor_tensor(sc[:, 0, :], sc[:, 3, :], float(D), sc[:, 5, :], ALU.mult, ALU.mult))
            nc.vector.tensor_scalar(sc[:, 3, :], sc[:, 3, :], 1e-5, None, ALU.add).then_inc(var_ready, 1)
            v.wait_ge(w_in, 48)
            for k in range(KD):
                for j in range(2):
                    ch.do(nc.vector.tensor_tensor(wa_tmp, W_sb[:, k, 0:D], a_sb[:, j, :], ALU.mult))
                    ins = nc.vector.reduce_sum(W_sb[:, k, D + H * j:D + H * (j + 1)],
                                               wa_tmp.rearrange("p (h d) -> p h d", h=H), mybir.AxisListType.X)
                    ch.do(ins)
            nc.vector.memset(trow[:, :, :], 1.0).then_inc(wa_ready, 1)
            v.wait_ge(std_ready, 1)
            ch.do(nc.vector.reciprocal(sc[:, 3, :], sc[:, 4, :]))

            def normalise(i):
                for u in range(U):
                    t = bass.ds(U * i + u, 1)
                    nc.vector.tensor_scalar(xn[:, t, :], xn[:, t, :], sc[:, 2, t], sc[:, 3, t],
                                            ALU.subtract, ALU.mult).then_inc(xn_ready, 1)

            def body(i, more=True):
                if more:
                    normalise(i + 2)
                for u in range(U):
                    t = U * i + u
                    proj_ready.wait(v, i, u + 1)
                    if u == 0:
                        stored.wait_before(v, i, 2)
                    q = proj_bank[u]
                    nc.vector.tensor_copy(trow[:, u, :].rearrange("p (h r) -> p h r", r=ROW)[:, :, 0:HD],
                                          q[:, 0:D].rearrange("p (h d) -> p h d", h=H))
                    nc.vector.tensor_copy(sd[:, bass.ds(t, 1), :],
                                          q[:, D + H:D + 2 * H].rearrange("p (o h) -> p o h", o=1))
                    nc.vector.tensor_copy(srow[:, u, :], q[:, D:D + H]).then_inc(proj_out.sem, 1)
            normalise(0)
            normalise(1)
            turns(v, TURNS - 2, body)
            body(TURNS - 2, False)
            body(TURNS - 1, False)

            part = L["sd_nodes"][:, :, :].rearrange("p t (k h) -> p t k h", k=3)
            v.wait_ge(proj_out.sem, NTP)
            for k in range(3):
                ch.do(nc.vector.tensor_copy(part[:, :, k, :], sd))
                if k < 2:
                    ch.do(nc.vector.tensor_tensor(sd, sd, part[:, :, k, :], ALU.subtract))

        @block.scalar
        def _(s):
            s.wait_ge(var_ready, 1)
            nc.scalar.activation(sc[:, 4, :], sc[:, 3, :], ACT.Sqrt).then_inc(std_ready, 1)

            def rows(i):
                for u in range(U):
                    t = U * i + u
                    s.wait_ge(xn_ready, t + 1)
                    xT_ready.wait_before(s, i, u + 1)
                    nc.scalar.activation(xr[:, u, :], xn[:, bass.ds(t, 1), :].rearrange("p o d -> p (o d)"),
                                         ACT.Copy).then_inc(xr_ready.sem, 1)

            def body(i, last=False):
                if not last:
                    rows(i + 1)
                for u in range(U):
                    xT_ready.wait(s, i, u + 1)
                    proj_ready.wait_before(s, i, u + 1)
                    nc.scalar.activation(xnT[:, u, :], T_bank[u][:, 0:D], ACT.Copy).then_inc(xT_out.sem, 1)
            rows(0)
            turns(s, TURNS - 1, body)
            body(TURNS - 1, True)

        @block.tensor
        def _(pe):
            pe.wait_ge(const_set, 3)
            pe.wait_ge(cnt_ready, 1)
            nc.tensor.matmul(pb[4][:, 0:NT - 1], ones[:, :], cntd, start=True, stop=True).then_inc(cnt_bc, 1)
            pe.wait_ge(wa_ready, 1)

            def transposes(i):
                for u in range(U):
                    xr_ready.wait(pe, i, u + 1)
                    xT_out.wait_before(pe, i, u + 1)
                    for k in range(KD):
                        ins = nc.tensor.transpose(T_bank[u][:, k * P:(k + 1) * P],
                                                  xr[:, u, k * P:(k + 1) * P], ident[:, :])
                    ins.then_inc(xT_ready.sem, 1)

            def body(i, last=False):
                for u in range(U):
                    xT_out.wait(pe, i, u + 1)
                    proj_out.wait_before(pe, i, u + 1)
                    for k in range(KD):
                        ins = nc.tensor.matmul(proj_bank[u][:, 0:D + 2 * H], xnT[:, u, k * P:(k + 1) * P], W_sb[:, k, :],
                                               start=k == 0, stop=k == KD - 1)
                    ins.then_inc(proj_ready.sem, 1)
                if not last:
                    transposes(i + 1)
            transposes(0)
            turns(pe, TURNS - 1, body)
            body(TURNS - 1, True)


def row_moments(nc, ch, stats, sc, T=NTP):
    v = nc.vector
    mean, var, d = sc[:, 2, 0:T], sc[:, 3, 0:T], sc[:, 4, 0:T]
    ch.step(v.tensor_tensor(mean, stats[:, :, 1], stats[:, :, 4], ALU.add))
    ch.step(v.tensor_tensor(d, stats[:, :, 1], stats[:, :, 4], ALU.subtract))
    ch.do(v.tensor_tensor(var, stats[:, :, 2], stats[:, :, 5], ALU.add))
    ch.step(v.tensor_scalar(mean, mean, 0.5, None, ALU.mult))
    ch.step(v.tensor_scalar(var, var, 1.0 / D, None, ALU.mult))
    ch.do(v.tensor_tensor(d, d, d, ALU.mult))
    ch.do(v.scalar_tensor_tensor(var, d, 0.25, var, ALU.mult, ALU.add))


class Mix:

    def __init__(self, nc, sem, L):
        self.nc, self.L = nc, L
        self.pb, self.sc, self.xn = L["pb"], L["sc"], L["xn"]
        self.ident, self.ones = L["ident"][:, :], L["ones"][:, :]
        area = L["Area"](L["r3"])
        self.wq = area.take(KD, NQ)
        self.pwbd = area.take(QC, P)
        self.wres = area.take(4, D)
        self.blk = area.take(P)
        self.brow = area.take(D)
        self.bn = area.take(8, QC)
        self.col = area.take(8, BLK)
        self.hrow = area.take(BLK, D)
        start = area.at
        self.x_dst = L["r3"][:, start:start + 2 * EG * P].bitcast(I32)
        self.hT = area.take(KD, 512)
        self.scale_diag = area.take(512)
        big = area.take(14 * 512)
        chunks = big.rearrange("p (c n) -> p c n", n=512)
        self.hp = chunks[:, 0:QC, :]
        self.ob = chunks[:, QC:QC + 4, :]
        self.vb = chunks[:, QC + 4:QC + 8, :]
        self.sq = L["Area"](L["r4"][:, 3600:4624]).take(2, 512)
        area.at = start + 2 * EG * P
        self.mu = area.take(D)
        self.cov = area.take(KD, D)
        self.prod = area.take(KD, NQ)
        self.mucol, self.mask = area.take(KD), area.take(1)
        c = lambda name, per, by=1: Count(sem(name), per, by)
        self.w_in = sem("mix_w_in")
        self.pw_zero, self.pw_set = sem("pw_zero"), sem("pw_set")
        self.pw_in = sem("pw_in")
        self.norm_root, self.ratio, self.logged = sem("norm_root"), sem("ratio"), sem("logged")
        self.h_ready, self.h_used = c("h_ready", BLK), c("h_used", BLK)
        self.hc_ready, self.hc_used = c("hc_ready", BLK), c("hc_used", BLK)
        self.mu_ready, self.muT, self.mucol_ready = sem("mu_ready"), sem("muT"), sem("mucol_ready")
        assert KD == 2
        self.covT = sem("covT")
        self.cov_ready, self.cw, self.prod_ready, self.bn_sums = sem("cov_ready"), sem("cw"), sem("prod_ready"), sem("bn_sums")
        self.var_set, self.std_set, self.bn_set = sem("var_set"), sem("std_set"), sem("bn_set")
        self.hrow_ready = c("hrow_ready", 1)
        self.hT_ready, self.hT_out = c("hT_ready", 2), c("hT_out", 2)
        self.mm_ready, self.mm_out = c("mm_ready", 12), c("mm_out", 12)
        self.sqa, self.sqa_used = c("sqa", 6), c("sqa_used", 6)
        self.sqb, self.sqb_used = c("sqb", 6), c("sqb_used", 6)
        self.sqo, self.sqo_used = c("sqo", 4), c("sqo_used", 4)
        self.ksum, self.o1 = c("ksum", 4), c("o1", 4)
        self.sums_read, self.root, self.diag, self.spread = c("sums_read", 1), c("root", 2), c("diag", 1), c("spread", 1)
        self.o_ready, self.o_read = c("o_ready", 4), c("o_read", 1)
        self.res, self.res_out = c("res", 4), c("res_out", 4)
        self.fx_sq, self.fx_stored = c("fx_sq", 4), c("fx_stored", 1, 16)
        self.order = (2, 3, 0, 1, 4, 5)

    def loads(self, sp):
        A = self.L["A"]
        sp.dma_start(self.wq, A["w_qkv"].rearrange("(k p) c -> p k c", p=P)).then_inc(self.w_in, 16)
        sp.dma_start(self.wres, A["w_res"].rearrange("(k p) c -> p k c", p=P)).then_inc(self.w_in, 16)
        sp.dma_start(self.brow, A["b_res"].to_broadcast([P, D])).then_inc(self.w_in, 16)
        for j, name in enumerate(("bn_gamma", "bn_beta", "w_dw")):
            sp.dma_start(self.bn[:, j, :], A[name]).then_inc(self.w_in, 16)
        sp.wait_ge(self.pw_zero, 2)
        for b in range(4):
            sp.dma_start(self.pwbd[32 * b:32 * b + 32, :, 32 * b:32 * b + 32],
                         A["w_pw"][32 * b:32 * b + 32]).then_inc(self.pw_in, 16)

    def pool_start(self):
        self.nc.gpsimd.memset(self.pwbd, 0.0).then_inc(self.pw_zero, 1)
        self.nc.gpsimd.memset(self.blk, 0.0).then_inc(self.pw_zero, 1)

    def dve_start(self, ch, between):
        sc, v, pb = self.sc, self.nc.vector, self.pb
        v.wait_ge(self.pw_zero, 2)
        for b in range(4):
            ch.step(v.memset(self.blk[32 * b:32 * b + 32, 32 * b:32 * b + 32], 1.0))
        v.wait_ge(self.norm_root, 1)
        n, p, a, b, c, d = (sc[:, j, :] for j in (5, 6, 7, 8, 10, 11))
        ch.do(v.tensor_scalar(n, n, MINN, None, ALU.max))
        ch.do(v.tensor_scalar(p, n, MAXN, None, ALU.min))
        ch.step(v.tensor_scalar(a, p, -1.0, 1.0, ALU.mult, ALU.add))
        ch.do(v.tensor_scalar(b, p, 1.0, None, ALU.add))
        ch.do(v.reciprocal(a, a))
        v.tensor_tensor(a, a, b, ALU.mult).then_inc(self.ratio, 1)
        ch.do(v.tensor_tensor(c, p, p, ALU.mult))
        ch.do(v.tensor_scalar(d, c, 1.0 / 9.0, 1.0 / 7.0, ALU.mult, ALU.add))
        for k in (5.0, 3.0, 1.0):
            ch.do(v.tensor_tensor(d, d, c, ALU.mult))
            ch.do(v.tensor_scalar(d, d, 1.0 / k, None, ALU.add))
        ch.do(v.tensor_tensor(d, d, p, ALU.mult))
        v.wait_ge(self.logged, 1)
        ch.do(v.tensor_scalar(b, b, 0.5, None, ALU.mult))
        ch.do(v.tensor_tensor(d, d, b, ALU.subtract))
        ch.do(v.tensor_scalar(p, p, 0.2, None, ALU.is_lt))
        ch.do(v.tensor_tensor(d, d, p, ALU.mult))
        ch.do(v.tensor_tensor(b, b, d, ALU.add))
        ch.do(v.reciprocal(n, n))
        ch.do(v.tensor_tensor(sc[:, 1, :], b, n, ALU.mult))
        ch.do(v.tensor_scalar(self.mask, self.L["pcol"][:, 0:1], float(N - (NT - 1) * P), None, ALU.is_lt))

        def tile(t):
            return self.xn[:, bass.ds(t, 1), :].rearrange("p o d -> p (o d)")

        def h(i, us=range(BLK)):
            for u in us:
                t = BLK * i + u
                self.h_used.wait_before(v, i, u + 1)
                v.tensor_scalar(self.hrow[:, u, :], tile(t), sc[:, 1, bass.ds(t, 1)], None, ALU.mult)\
                    .then_inc(self.h_ready.sem, 1)
        turns(v, NT // BLK, h)
        h(NT // BLK, (0,))
        v.wait_ge(self.h_used.sem, NT)
        v.tensor_scalar(self.mu, pb[0][:, 0:D], 1.0 / N, None, ALU.mult).then_inc(self.mu_ready, 1)
        v.wait_ge(self.mu_ready, 1)

        def hc(i, us=range(BLK)):
            for u in us:
                t = BLK * i + u
                self.hc_used.wait_before(v, i, u + 1)
                ins = v.scalar_tensor_tensor(self.hrow[:, u, :], tile(t), sc[:, 1, bass.ds(t, 1)], self.mu, ALU.mult,
                                             ALU.subtract)
                if len(us) == 1:
                    ch.do(ins)
                    ins = v.tensor_scalar(self.hrow[:, u, :], self.hrow[:, u, :], self.mask, None, ALU.mult)
                ins.then_inc(self.hc_ready.sem, 1)
        turns(v, NT // BLK, hc)
        hc(NT // BLK, (0,))
        between()
        v.wait_ge(self.muT, 1)
        for k in range(KD):
            v.tensor_copy(self.mucol[:, k:k + 1], pb[5][:, k * P:k * P + 1]).then_inc(self.mucol_ready, 1)
        v.wait_ge(self.hc_used.sem, NT)
        for k in range(KD):
            v.tensor_scalar(self.cov[:, k, k * P:D], pb[1 + k][:, k * P:D], 1.0 / N, None, ALU.mult)\
                .then_inc(self.cov_ready, 1)
        v.wait_ge(self.covT, 1)
        v.tensor_copy(self.cov[:, 1, 0:P], pb[5][:, 0:P]).then_inc(self.cov_ready, 1)
        v.wait_ge(self.w_in, 6 * 16)
        for k in range(KD):
            v.wait_ge(self.cw, 2 * k + 2)
            for j in range(2):
                c = slice(j * NQ // 2, (j + 1) * NQ // 2)
                v.tensor_tensor(self.prod[:, k, c], pb[3 + j][:, 0:NQ // 2], self.wq[:, k, c], ALU.mult)\
                    .then_inc(self.prod_ready, 1)
        v.wait_ge(self.bn_sums, 1)
        bn = self.bn
        v.tensor_scalar(bn[:, 4, :], pb[5][:, 0:QC], 1e-5, None, ALU.add).then_inc(self.var_set, 1)
        v.wait_ge(self.std_set, 1)
        ch.do(v.reciprocal(bn[:, 4, :], bn[:, 4, :]))
        ch.do(v.tensor_tensor(bn[:, 5, :], bn[:, 0, :], bn[:, 4, :], ALU.mult))
        ch.do(v.tensor_tensor(bn[:, 6, :], pb[5][:, 8:8 + QC], bn[:, 5, :], ALU.mult))
        ch.do(v.tensor_tensor(bn[:, 6, :], bn[:, 1, :], bn[:, 6, :], ALU.subtract))
        v.wait_ge(self.pw_in, 64)
        for c in range(QC):
            ch.step(v.tensor_scalar(self.pwbd[:, c, :], self.pwbd[:, c, :], bn[:, 2, c:c + 1], None, ALU.mult))
        ch.done()
        v.sem_inc(self.bn_set, 1)

    def act_start(self, s, between):
        sc, act = self.sc, self.nc.scalar
        act.activation(sc[:, 5, :], sc[:, 0, :], ACT.Sqrt).then_inc(self.norm_root, 1)
        s.wait_ge(self.ratio, 1)
        act.activation(sc[:, 8, :], sc[:, 7, :], ACT.Ln).then_inc(self.logged, 1)
        between()
        s.wait_ge(self.var_set, 1)
        act.activation(self.bn[:, 4, :], self.bn[:, 4, :], ACT.Sqrt).then_inc(self.std_set, 1)
        s.wait_ge(self.bn_set, 1)

    def pe_start(self, pe, between):
        mm, pb, ones = self.nc.tensor.matmul, self.pb, self.ones

        def colsum(i, us=range(BLK)):
            for u in us:
                self.h_ready.wait(pe, i, u + 1)
                first = isinstance(i, int) and i == 0 and u == 0
                mm(pb[0][:, 0:D], ones, self.hrow[:, u, :], start=first, stop=len(us) == 1)\
                    .then_inc(self.h_used.sem, 1)
        turns(pe, NT // BLK, colsum)
        colsum(NT // BLK, (0,))
        pe.wait_ge(self.mu_ready, 1)
        for k in range(KD):
            ins = self.nc.tensor.transpose(pb[5][:, k * P:(k + 1) * P], self.mu[:, k * P:(k + 1) * P], self.ident)
        ins.then_inc(self.muT, 1)

        def gram(i, us=range(BLK)):
            for u in us:
                self.hc_ready.wait(pe, i, u + 1)
                first = isinstance(i, int) and i == 0 and u == 0
                for k in range(KD):
                    ins = mm(pb[1 + k][:, k * P:D], self.hrow[:, u, k * P:(k + 1) * P], self.hrow[:, u, k * P:D],
                             start=first, stop=len(us) == 1)
                ins.then_inc(self.hc_used.sem, 1)
        turns(pe, NT // BLK, gram)
        gram(NT // BLK, (0,))
        between()
        pe.wait_ge(self.cov_ready, 2)
        pe.wait_ge(self.mucol_ready, 2)
        self.nc.tensor.transpose(pb[5][:, 0:P], self.cov[:, 0, P:D], self.ident).then_inc(self.covT, 1)
        pe.wait_ge(self.cov_ready, 3)
        pe.wait_ge(self.w_in, 6 * 16)
        for m in range(KD):
            for j in range(2):
                if m:
                    pe.wait_ge(self.prod_ready, j + 1)
                for k in range(KD):
                    ins = mm(pb[3 + j][:, 0:NQ // 2], self.cov[:, k, m * P:(m + 1) * P],
                             self.wq[:, k, j * NQ // 2:(j + 1) * NQ // 2], start=k == 0, stop=k == KD - 1)
                ins.then_inc(self.cw, 1)
        pe.wait_ge(self.prod_ready, 4)
        pe.wait_ge(self.mucol_ready, 2)
        for c in range(QC):
            for k in range(KD):
                mm(pb[5][:, c:c + 1], self.prod[:, k, c * P:(c + 1) * P], ones[:, 0:1], start=k == 0, stop=k == KD - 1)
            for k in range(KD):
                ins = mm(pb[5][:, 8 + c:9 + c], self.wq[:, k, c * P:(c + 1) * P], self.mucol[:, k:k + 1], start=k == 0,
                         stop=k == KD - 1)
        ins.then_inc(self.bn_sums, 1)
        pe.wait_ge(self.bn_set, 1)

    def bank(self, n):
        return self.pb[2 + n % 2][:, :]

    def slot(self, stage, eng, i, q, amid=lambda: None):
        self.amid = amid
        more = not isinstance(i, int) or i < NB - 1
        if q < 2:
            if more:
                stage("a", eng, i + 1, q)
            stage("c", eng, i, q)
        elif q == 2:
            stage("f", eng, i, more)
        elif more:
            stage("b", eng, i + 1, 0)

    def squares_sum(self, bank, k, first, last):
        return self.nc.tensor.matmul(self.pb[bank][:, :], self.ones, self.sq[:, k % 2, :], start=first, stop=last)

    def by_row(self, ch, bank, out):
        v, d = self.nc.vector, self.scale_diag.rearrange("p (j n) -> p j n", n=P)
        ch.do(v.tensor_tensor(d, self.pb[bank][:, :].rearrange("p (j n) -> p j n", n=P),
                              self.ident.unsqueeze(1).to_broadcast([P, BLK, P]), ALU.mult))
        return v.reduce_sum(out, d, mybir.AxisListType.X)

    def pe(self, st, pe, b, q):
        mm, tr, pb = self.nc.tensor.matmul, self.nc.tensor.transpose, self.pb

        def square_a(k):
            self.sqa.wait(pe, b, k + 1)
            if k == 0:
                self.sums_read.wait_before(pe, b, 1)
            self.squares_sum(4, k, k == 0, k == 5).then_inc(self.sqa_used.sem, 1)

        def square_b(k):
            self.sqb.wait(pe, b, k + 1)
            self.squares_sum(5, k, k == 0, k == 5).then_inc(self.sqb_used.sem, 1)

        if st == "a":
            if q == 0:
                self.hrow_ready.wait(pe, b, 1)
                self.o1.wait_before(pe, b, 4)
                for k in range(KD):
                    for j in range(BLK):
                        ins = tr(pb[k][:, j * P:(j + 1) * P], self.hrow[:, j, k * P:(k + 1) * P], self.ident)
                    ins.then_inc(self.hT_ready.sem, 1)
                if not (isinstance(b, int) and b == 0):
                    self.spread_scale(pe, b - 1)
                self.hT_out.wait(pe, b, 2)
            for n in range(3 * q, 3 * q + 3):
                if n >= 2:
                    self.mm_out.wait(pe, b, n - 1)
                else:
                    self.mm_out.wait_before(pe, b, 11 + n)
                c = self.order[n]
                for k in range(KD):
                    ins = mm(self.bank(n), self.wq[:, k, c * P:(c + 1) * P], self.hT[:, k, :], start=k == 0, stop=k == 1)
                ins.then_inc(self.mm_ready.sem, 1)
                if n == 3 * q + 2:
                    self.amid()
                if n:
                    square_a(n - 1)
            if q:
                square_a(5)
        if st == "c" and q == 0 and isinstance(b, int) and b == NB - 1:
            self.spread_scale(pe, b)
        if st == "f":
            def square_o(k):
                self.sqo.wait(pe, b, k + 1)
                self.squares_sum(0, k, k == 0, k == 3).then_inc(self.sqo_used.sem, 1)
            if q:
                self.mm_out.wait(pe, b + 1, 6)
            else:
                self.mm_out.wait(pe, b, 12)

            def last_map(ms):
                self.o_ready.wait(pe, b, ms[-1] + 1)
                for j in range(BLK):
                    for m in ms:
                        ins = mm(pb[2 + j // 2][:, (j % 2) * D:(j % 2 + 1) * D], self.ob[:, m, j * P:(j + 1) * P],
                                 self.wres[:, m, :], start=m == 0 and j % 2 == 0, stop=m == 3 and j % 2 == 1)
                    if ms[-1] == 3:
                        ins.then_inc(self.res.sem, 1)
            last_map((0, 1))
            square_o(0)
            square_o(1)
            square_o(2)
            square_o(3)
            last_map((2, 3))
            self.amid()
        if st == "b":
            def key_sum(j, count):
                self.mm_out.wait(pe, b, count)
                if j >= 2:
                    self.o1.wait(pe, b, j - 1)
                mm(pb[j % 2][:, :], self.blk, self.hp[:, 2 + j % 2, :], start=True, stop=True).then_inc(self.ksum.sem, 1)
            self.o_read.wait_before(pe, b, 1)
            key_sum(0, 2)
            key_sum(1, 2)
            for n in range(QC, 2 * QC):
                self.mm_out.wait(pe, b, n - 1)
                if n == QC:
                    self.res_out.wait_before(pe, b, 4)
                c = self.order[n - QC]
                mm(self.bank(n), self.pwbd[:, c, :], self.hp[:, c, :], start=True, stop=True).then_inc(self.mm_ready.sem, 1)
                if n > QC:
                    square_b(n - 1 - QC)
                if n - QC == 3:
                    key_sum(2, QC + 1)
                    key_sum(3, QC + 2)
            square_b(5)

    def spread_scale(self, pe, b):
        self.diag.wait(pe, b, 1)
        self.nc.tensor.matmul(self.pb[5][:, :], self.ones, self.scale_diag, start=True, stop=True).then_inc(self.spread.sem, 1)

    def act(self, st, s, b, q):
        act, pb = self.nc.scalar.activation, self.pb
        if st == "a":
            if q == 0:
                if not (isinstance(b, int) and b == 0):
                    self.roots(s, b - 1)
                self.mm_ready.wait_before(s, b, 6)
                for k in range(KD):
                    self.hT_ready.wait(s, b, k + 1)
                    act(self.hT[:, k, :], pb[k][:, :], ACT.Copy).then_inc(self.hT_out.sem, 1)
                self.mm_ready.wait_before(s, b, 12)
                self.o1.wait_before(s, b, 4)
            for n in range(3 * q, 3 * q + 3):
                c = self.order[n]
                self.mm_ready.wait(s, b, n + 1)
                act(self.hp[:, c, :], self.bank(n), ACT.Relu, bias=self.bn[:, 6, c:c + 1], scale=self.bn[:, 5, c:c + 1])\
                    .then_inc(self.mm_out.sem, 1)
                if n >= 2:
                    self.sqa_used.wait(s, b, n - 1)
                else:
                    self.sqb_used.wait_before(s, b, 5 + n)
                self.mm_out.wait(s, b, n + 1)
                act(self.sq[:, n % 2, :], self.hp[:, c, :], ACT.Square).then_inc(self.sqa.sem, 1)
                if n % 3 == 0:
                    self.amid()
        if st == "c" and q == 0 and isinstance(b, int) and b == NB - 1:
            self.roots(s, b)
        if st == "f":
            for m in range(4):
                if m >= 2:
                    self.sqo_used.wait(s, b, m - 1)
                elif q:
                    self.sqa_used.wait(s, b + 1, 5 + m)
                else:
                    self.sqb_used.wait(s, b, 5 + m)
                self.o_ready.wait(s, b, m + 1)
                act(self.sq[:, m % 2, :], self.ob[:, m, :], ACT.Square).then_inc(self.sqo.sem, 1)
            self.amid()
            self.o_read.wait(s, b, 1)
            act(self.col[:, 2, :], self.col[:, 2, :], ACT.Sqrt).then_inc(self.root.sem, 1)
            for j in range(BLK):
                self.res_out.wait(s, b, j + 1)
                if j:
                    self.fx_sq.wait(s, b, j)
                act(self.sq[:, 0, 0:D], self.xn[:, bass.ds(4 * b + j, 1), :].rearrange("p o d -> p (o d)"), ACT.Square,
                    accum_out=self.sc[:, 9, bass.ds(4 * b + j, 1)]).then_inc(self.fx_sq.sem, 1)
            s.dma_start(self.L["fx_d"][bass.ds(4 * b, BLK), :, :].rearrange("t p d -> p t d"),
                        self.xn[:, bass.ds(4 * b, BLK), :]).then_inc(self.fx_stored.sem, 16)
        if st == "b":
            self.o_ready.wait_before(s, b, 4)
            self.res.wait_before(s, b, 4)
            self.fx_sq.wait_before(s, b, 4)
            for n in range(QC, 2 * QC):
                k, c = n - QC, self.order[n - QC]
                if k == 1:
                    self.amid()
                if k == 4:
                    for j in range(2):
                        act(self.vb[:, j, :], self.hp[:, 4 + j, :], ACT.Copy)
                self.mm_ready.wait(s, b, n + 1)
                if k >= 2:
                    self.sqb_used.wait(s, b, k - 1)
                elif isinstance(b, int) and b == 0:
                    self.sqa_used.wait(s, b, 5 + k)
                else:
                    self.sqo_used.wait_before(s, b, 3 + k)
                act(self.sq[:, k % 2, :], self.bank(n), ACT.Square).then_inc(self.sqb.sem, 1)
                dst = {0: self.ob[:, 2, :], 1: self.ob[:, 3, :], 2: self.hp[:, 2, :], 3: self.hp[:, 3, :],
                       4: self.vb[:, 2, :], 5: self.vb[:, 3, :]}[c]
                act(dst, self.bank(n), ACT.Copy if c >= 4 else ACT.Relu).then_inc(self.mm_out.sem, 1)

    def roots(self, s, b):
        self.sums_read.wait(s, b, 1)
        self.nc.scalar.activation(self.col[:, 0:2, :], self.col[:, 4:6, :], ACT.Sqrt).then_inc(self.root.sem, 1)

    def dve(self, ch):
        return lambda st, v, b, q: self.dve_stage(ch, st, b, q)

    def dve_stage(self, ch, st, b, q):
        v, pb = self.nc.vector, self.pb
        n1, n2, n3, scale, t, r = (self.col[:, j, :] for j in (0, 1, 2, 3, 6, 7))
        if st == "a" and q == 0:
            if not (isinstance(b, int) and b == 0):
                self.read_sums(ch, b - 1)
            self.hT_ready.wait_before(v, b, 2)
            v.tensor_tensor(self.hrow, self.xn[:, bass.ds(4 * b, BLK), :],
                            self.sc[:, 1, bass.ds(4 * b, BLK)].unsqueeze(2).to_broadcast([P, BLK, D]), ALU.mult)\
                .then_inc(self.hrow_ready.sem, 1)
        if st == "b":
            self.res.wait_before(v, b, 4)
            for j in range(4):
                if j == 2:
                    self.sqa_used.wait(v, b, 6)
                    ch.do(self.by_row(ch, 4, self.col[:, 4, :]))
                x = self.hp[:, j, :] if j < 2 else self.ob[:, j, :]
                self.ksum.wait(v, b, j + 1)
                if j >= 2:
                    self.mm_out.wait(v, b, 7 + j)
                v.tensor_tensor(self.ob[:, j, :], x, pb[j % 2][:, :], ALU.mult).then_inc(self.o1.sem, 1)
        if st == "c":
            if q == 0:
                if isinstance(b, int) and b == NB - 1:
                    self.read_sums(ch, b)
                self.root.wait(v, b, 1)
                ch.do(v.tensor_scalar(n1, n1, MINN, None, ALU.max))
                ch.step(v.tensor_scalar(t, n1, CAP, None, ALU.min))
                ch.do(v.reciprocal(n1, n1))
                ch.do(v.tensor_tensor(scale, t, n1, ALU.mult))
                ch.do(v.tensor_tensor(n2, n2, scale, ALU.mult))
                ch.do(v.tensor_scalar(n2, n2, MINN, None, ALU.max))
                ch.step(v.tensor_scalar(t, n2, CAP, None, ALU.min))
                ch.do(v.reciprocal(n2, n2))
                ch.do(v.tensor_tensor(t, t, n2, ALU.mult))
                ch.do(v.tensor_tensor(scale, scale, t, ALU.mult))
                v.tensor_tensor(self.scale_diag.rearrange("p (j n) -> p j n", n=P),
                                self.ident.unsqueeze(1).to_broadcast([P, BLK, P]),
                                scale.unsqueeze(2).to_broadcast([P, BLK, P]), ALU.mult).then_inc(self.diag.sem, 1)
                ch.do(v.tensor_tensor(r, scale, scale, ALU.mult))
                self.amid()
                self.spread.wait(v, b, 1)
                self.mm_out.wait(v, b, 12)
            pair = slice(2 * q, 2 * q + 2)
            val, o = self.vb[:, pair, :], self.ob[:, pair, :]
            ch.do(v.tensor_tensor(val, val, pb[5][:, :].unsqueeze(1).to_broadcast([P, 2, 512]), ALU.mult))
            ch.step(v.tensor_tensor(o, o, val, ALU.mult))
            ch.do(v.tensor_scalar(val, val, MINN, None, ALU.add))
            ch.do(v.reciprocal(val, val))
            for m in range(2):
                v.tensor_tensor(o[:, m, :], o[:, m, :], val[:, m, :], ALU.mult).then_inc(self.o_ready.sem, 1)
        if st == "f":
            self.sqo_used.wait(v, b, 4)
            self.by_row(ch, 0, n3).then_inc(self.o_read.sem, 1)
            self.root.wait(v, b, 2)
            ch.do(v.tensor_tensor(n3, n3, r, ALU.mult))
            ch.do(v.tensor_scalar(n3, n3, MINN, None, ALU.max))
            ch.step(v.tensor_scalar(t, n3, CAP, None, ALU.min))
            ch.do(v.reciprocal(n3, n3))
            ch.do(v.tensor_tensor(t, t, n3, ALU.mult))
            ch.do(v.tensor_tensor(t, t, r, ALU.mult))
            for j in range(BLK):
                self.res.wait(v, b, 2 * (j // 2) + 2)
                v.scalar_tensor_tensor(self.xn[:, bass.ds(4 * b + j, 1), :].rearrange("p o d -> p (o d)"),
                                       pb[2 + j // 2][:, (j % 2) * D:(j % 2 + 1) * D],
                                       t[:, j:j + 1], self.brow, ALU.mult, ALU.add).then_inc(self.res_out.sem, 1)

    def read_sums(self, ch, b):
        v, s1, s2 = self.nc.vector, self.col[:, 4, :], self.col[:, 5, :]
        self.sqb_used.wait(v, b, 6)
        ch.do(self.by_row(ch, 5, s2))
        v.tensor_tensor(s2, s1, s2, ALU.add).then_inc(self.sums_read.sem, 1)

    def rest(self, fn, eng, i, groups):
        for q in range(len(groups), 4):
            self.slot(fn, eng, i, q)

    def first(self, fn, eng):
        self.amid = lambda: None
        for st, q in (("a", 0), ("a", 1), ("b", 0)):
            fn(st, eng, 0, q)


def edges_and_mix(nc, ctx, sem, L):
    A, pb, ident, ones, xn, sc = L["A"], L["pb"], L["ident"], L["ones"], L["xn"], L["sc"]
    iota_f, dst_f, nt_f, nodecol, E_all = (L[k] for k in ("iota_f", "dst_f", "nt_f", "nodecol", "E_all"))
    src_sb, idx, grab, sde, r1, r2, r3 = (L[k] for k in ("src_sb", "idx", "grab", "sde", "r1", "r2", "r3"))
    sat_d, et_d, tau_i = L["sat_d"], L["et_d"], L["tau_i"]
    assert NG - 1 == NT - 1
    TA = NB
    NX = NT - 1

    small = L["Area"](L["r4"])
    dstb = small.take(EG * P, dt=I32)
    st = small.take(EG * P // 2, dt=BF16).rearrange("p (t e) -> p t e", e=P)
    st_end = small.at
    edge_pre = small.take(2, EG * H)
    satb = small.take(2, EG * H)
    cols = small.take(16)
    assert small.at <= 3600

    same = r1[:, 0:CH + 1]
    tmp = r1[:, CH + 8:2 * CH + 8]
    dstx = r2[:, 0:CH + 2].bitcast(I32)
    pre = r2[:, 0:CH]
    score = r3[:, 0:CH]
    PR = 4
    RP = 8
    TB = VT // (RP * PR)
    XB = ET // (RP * PR)
    rows = r3[:, CH:CH + RP * PR * TAB].rearrange("p (q e d) -> p q e d", q=RP, e=PR)
    ring_idx = idx[:, :, :].rearrange("p q e -> p (q e)")[:, 0:RP * PR].rearrange("p (q e) -> p q e", e=PR)
    acc = r1[:, 0:NT * TAB].rearrange("p (t d) -> p t d", d=TAB)
    S = L["r4"][:, 0:2 * PR * P].rearrange("p (u e n) -> p u e n", u=2, e=PR)
    msg = L["r4"][:, 2 * PR * P:2 * PR * (P + TAB)].rearrange("p (u e d) -> p u e d", u=2, e=PR)
    etb = L["r4"][:, 0:1024].rearrange("p (u t e) -> p u t e", u=2, t=4)
    carry = L["r4"][:, 1024:2048].rearrange("p (j e) -> p j e", e=P)

    idx_in = [Count(sem(f"idx_in{q}"), 1, 16) for q in range(4)]
    grabbed = [Count(sem(f"grabbed{q}"), EG, 16) for q in range(4)]
    copied = [Count(sem(f"copied{q}"), 1, 16) for q in range(4)]
    gate = sem("gate")
    dst_in = Count(sem("dst_in"), 4, 16)
    st_built = Count(sem("st_built"), 4)
    sde_ready = Count(sem("sde_ready"), 4)
    sde_used = Count(sem("sde_used"), 4)
    score_ready = Count(sem("score_ready"), 4)
    scT_ready = Count(sem("scT_ready"), 4)
    scT_out = Count(sem("scT_out"), 4)
    sat_stored = [Count(sem(f"sat_stored{u}"), 2, 16) for u in range(2)]
    x_dst_in, x_cols_in = [sem(f"x_dst_in{j}") for j in range(3)], sem("x_cols_in")
    x_added = sem("x_added")
    x_built, x_sde, x_used = sem("x_built"), sem("x_sde"), sem("x_used")
    dve2 = sem("dve2")
    dst_chunks_in, sat_in = sem("dst_chunks_in"), sem("sat_in")
    r2_free = sem("r2_free")
    diag_ready, diag_sum = sem("diag_ready"), sem("diag_sum")
    shifted, weighed, et_out = sem("shifted"), sem("weighed"), sem("et_out")
    et_in = [Count(sem(f"et_in{u}"), 1, 16) for u in range(2)]
    etT_ready, etT_out = Count(sem("etT_ready"), 2), Count(sem("etT_out"), 2)
    e_extra = sem("e_extra")
    first_groups = [len(range(q, NG, 4)) for q in range(4)]
    bidx_in = [Count(idx_in[q].sem, 1, 16, before=first_groups[q]) for q in range(4)] \
        + [Count(sem(f"bidx_in{q}"), 1, 16) for q in range(4, RP)]
    row_in = [Count(grabbed[q].sem, PR, 16, before=EG * first_groups[q]) for q in range(4)] \
        + [Count(sem(f"row_in{q}"), PR, 16) for q in range(4, RP)]
    msg_ready = Count(sem("msg_ready"), RP)
    summed = Count(sem("summed"), RP)
    added = Count(sem("added"), RP * PR)
    acc_zero = sem("acc_zero")
    mixed = sem("mixed")

    MIX = Mix(nc, sem, L)
    x_dst = (dstb, MIX.x_dst[:, 0:EG * P], MIX.x_dst[:, EG * P:2 * EG * P])
    xsum = L["r4"][:, st_end:st_end + NX * H].rearrange("p (n h) -> p n h", h=H)

    def groups(i):
        return range(4) if not isinstance(i, int) or i < TA - 1 else range(NG - 4 * (TA - 1))

    def all_turns(eng, body):
        body(0)
        with eng.Fori(1, TA - 1) as i:
            body(i)
        body(TA - 1)

    def weight_rows(eng, u):
        for i in range(u, TA, 2):
            if i > 1:
                eng.wait_ge(etT_ready.sem, i - 1)
            n = len(groups(i))
            eng.dma_start(etb[:, u, 0:n, :], et_d[4 * i * EG:(4 * i + n) * EG].rearrange("(k t) h e -> (t h) k e", t=EG))\
                .then_inc(et_in[u].sem, 16)

    with nc.Block() as block:
        @block.sync
        def _(sp):
            for q in range(4):
                sp.dma_start(idx[:, q, :], src_sb[:, q * EG:(q + 1) * EG]).then_inc(idx_in[q].sem, 16)
            MIX.loads(sp)

            def body(i):
                for q in groups(i):
                    g = 4 * i + q
                    grabbed[q].wait(sp, i, EG)
                    sp.dma_start(E_all[:, bass.ds(g * EG, EG), :], grab[:, q, :, :]).then_inc(copied[q].sem, 16)
                    copied[q].wait(sp, i, 1)
                    if not (isinstance(g, int) and g + 4 >= NG):
                        sp.dma_start(idx[:, q, :], src_sb[:, bass.ds((g + 4) * EG, EG)]).then_inc(idx_in[q].sem, 16)
                    if not (isinstance(g, int) and g == NG - 1):
                        t = sp.value_load(tau_i[0:1, bass.ds(g, 1)], min_val=0, max_val=ET - 1)
                        sp.dma_start(src_sb[:, bass.ds(ET + g, 1)], src_sb[:, bass.ds(t, 1)]).then_inc(x_cols_in, 16)
                        sp.dma_start(dst_f[:, bass.ds(ET + g, 1)], dst_f[:, bass.ds(t, 1)]).then_inc(x_cols_in, 16)
            body(0)
            with sp.Fori(1, TA - 2) as i:
                body(i)
            body(TA - 2)
            body(TA - 1)
            for q in range(4):
                idx_in[q].wait(sp, TA - 1 if q < 1 else TA - 2, 1)
            for q in range(RP):
                sp.dma_start(ring_idx[:, q, :], src_sb[:, q * PR:(q + 1) * PR]).then_inc(bidx_in[q].sem, 16)
            sp.wait_ge(r2_free, 1)
            for h in range(H):
                sp.dma_start(dstx[16 * h:16 * (h + 1), :], A["dst_chunks"]).then_inc(dst_chunks_in, 16)
            for u in range(2):
                sp.wait_ge(sat_stored[u].sem, 16 * (NG + 1) // 2)
            sp.wait_ge(mixed, 1)
            sp.dma_start(score, sat_d.rearrange("h t e -> (h t e)").rearrange("(p f) -> p f", p=P)).then_inc(sat_in, 16)
            CT = CH // P
            for half in range(2):
                sp.wait_ge(weighed, 2 * half + 2)
                tiles = slice(half * CT // 2, (half + 1) * CT // 2)
                for h in range(H):
                    sp.dma_start(et_d.rearrange("(c t) h e -> h c t e", c=16)[h, :, tiles, :],
                                 score[16 * h:16 * (h + 1), :].rearrange("c (t e) -> c t e", e=P)[:, tiles, :])\
                        .then_inc(et_out, 16)
            sp.wait_ge(et_out, 256)
            weight_rows(sp, 0)
            sp.wait_ge(x_cols_in, 2 * 16 * NX)

            def second(i):
                for q in range(RP):
                    msg_ready.wait(sp, i, q + 1)
                    if not (isinstance(i, int) and i == TB - 1):
                        sp.dma_start(ring_idx[:, q, :], src_sb[:, bass.ds(((i + 1) * RP + q) * PR, PR)])\
                            .then_inc(bidx_in[q].sem, 16)
            second(0)
            with sp.Fori(1, TB - 1) as i:
                second(i)

        @block.gpsimd
        def _(g_):
            MIX.pool_start()

            def body(i):
                for q in groups(i):
                    idx_in[q].wait(g_, i, 1)
                    g_.sem_inc(gate, 1)
                    for e in range(EG):
                        g_.indirect_dma_start(out=grab[:, q, e, :], out_offset=None, in_=L["ssrc_d"],
                                              in_offset=bass.IndirectOffsetOnAxis(ap=idx[:, q, e:e + 1], axis=0))\
                            .then_inc(grabbed[q].sem, 16)
            body(0)
            g_.wait_ge(x_used, 3)

            def extra(n):
                t = g_.value_load(tau_i[0:1, bass.ds(n, 1)], min_val=0, max_val=ET - 1)
                if not (isinstance(n, int) and n == 0):
                    g_.wait_ge(x_added, n)
                nc.gpsimd.tensor_tensor(sde[:, bass.ds(t, 1), :], sde[:, bass.ds(t, 1), :], xsum[:, bass.ds(n, 1), :],
                                        ALU.add).then_inc(x_added, 1)
            extra(0)
            with g_.Fori(1, NX) as n:
                extra(n)
            with g_.Fori(1, TA - 1) as i:
                body(i)
            body(TA - 1)
            g_.wait_ge(mixed, 1)

            def second(i):
                for q in range(RP):
                    bidx_in[q].wait(g_, i, 1)
                    g_.sem_inc(gate, 1)
                    for e in range(PR):
                        g_.indirect_dma_start(out=rows[:, q, e, :], out_offset=None, in_=L["table_d"],
                                              in_offset=bass.IndirectOffsetOnAxis(ap=ring_idx[:, q, e:e + 1], axis=0))\
                            .then_inc(row_in[q].sem, 16)
            second(0)
            g_.wait_ge(shifted, 4)
            nc.gpsimd.memset(r1[:, 0:T2 * TAB], 0.0).then_inc(acc_zero, 1)
            with g_.Fori(1, TB) as i:
                second(i)

        @block.vector
        def _(v):
            ch = Chain(v, dve2)

            def extra_rows():
                for j in range(3):
                    v.wait_ge(x_dst_in[j], 16 * EG)
                    nc.vector.tensor_tensor(st[:, :, :], x_dst[j].rearrange("p (t e) -> p t e", e=P),
                                            nodecol[:, ET + j * EG:ET + (j + 1) * EG].unsqueeze(2).to_broadcast([P, EG, P]),
                                            ALU.is_equal).then_inc(x_built, 1)
                    v.wait_ge(x_sde, j + 1)
                    parts = pb[6][:, 0:3 * EG * H].rearrange("p (t k h) -> p t k h", k=3, h=H)
                    x = xsum[:, j * EG:(j + 1) * EG, :]
                    ch.do(nc.vector.tensor_copy(x, parts[:, :, 2, :]))
                    ch.do(nc.vector.tensor_tensor(x, x, parts[:, :, 1, :], ALU.add))
                    ch.do(nc.vector.tensor_tensor(x, x, parts[:, :, 0, :], ALU.add))
                    v.sem_inc(x_used, 1)

            MIX.dve_start(ch, extra_rows)
            MIX.first(MIX.dve(ch), v)

            def one_hot(i, q):
                dst_in.wait(v, i, q + 1)
                nc.vector.tensor_tensor(st[:, :, :], dstb.rearrange("p (t e) -> p t e", e=P),
                                        nodecol[:, bass.ds((4 * i + q) * EG, EG)].unsqueeze(2).to_broadcast([P, EG, P]),
                                        ALU.is_equal).then_inc(st_built.sem, 1)
            one_hot(0, 0)
            v.wait_ge(x_added, NX)
            ch.loop()

            def body(i, per):
                ch.turn(i, per)
                for q in groups(i):
                    u, g = q % 2, 4 * i + q

                    def scores():
                        sde_ready.wait(v, i, q + 1)
                        copied[q].wait(v, i, 1)
                        if q >= 2:
                            scT_ready.wait(v, i, q - 1)
                        else:
                            scT_ready.wait_before(v, i, q + 3)
                        ep = edge_pre[:, u, :]
                        ep3 = ep.rearrange("p (t h) -> p t h", h=H)
                        parts = pb[6][:, 0:3 * EG * H].rearrange("p (t k h) -> p t k h", k=3, h=H)
                        ch.do(nc.vector.tensor_tensor(ep3, E_all[:, bass.ds(g * EG, EG), :], parts[:, :, 2, :], ALU.add))
                        ch.do(nc.vector.tensor_tensor(ep3, ep3, parts[:, :, 1, :], ALU.add))
                        nc.vector.tensor_tensor(ep3, ep3, parts[:, :, 0, :], ALU.add).then_inc(sde_used.sem, 1)
                        sde_used.wait(v, i, q + 1)
                        ch.do(nc.vector.tensor_tensor(ep, ep, sde[:, bass.ds(g * EG, EG), :].rearrange("p t h -> p (t h)"),
                                                      ALU.add))
                        nc.vector.scalar_tensor_tensor(ep, ep, 0.2, ep, ALU.mult, ALU.max).then_inc(score_ready.sem, 1)

                    def edge_work():
                        scores()
                        if not (isinstance(g, int) and g == NG - 1):
                            one_hot(i, q + 1)

                    if q:
                        edge_work()
                    MIX.slot(MIX.dve(ch), v, i, q, edge_work)
            body(0, 0)
            per = ch.k
            with v.Fori(1, TA - 1) as i:
                body(i, per)
                assert ch.k == per, (ch.k, per)
            body(TA - 1, per)
            v.wait_ge(score_ready.sem, NG)
            v.wait_ge(dst_in.sem, 16 * (NG + 1))
            v.sem_inc(r2_free, 1)
            MIX.rest(MIX.dve(ch), v, TA - 1, groups(TA - 1))
            v.wait_ge(mixed, 1)
            v.wait_ge(dst_chunks_in, 16 * H)
            ch.do(nc.vector.tensor_tensor(same, dstx[:, 1:CH + 2], dstx[:, 0:CH + 1], ALU.not_equal))
            ch.do(nc.vector.tensor_scalar(same, same, -BIG, None, ALU.mult))
            col = lambda j: cols[:, j:j + 1]
            ch.step(nc.vector.tensor_tensor(col(0), dstx[:, CH:CH + 1], dstx[:, 0:1], ALU.not_equal))
            ch.do(nc.vector.tensor_tensor(col(1), dstx[:, CH + 1:CH + 2], dstx[:, 1:2], ALU.not_equal))
            ch.do(nc.vector.tensor_scalar(cols[:, 0:2], cols[:, 0:2], -BIG, None, ALU.mult))
            v.wait_ge(sat_in, 16)
            fwd_neg, bwd_neg = same[:, 0:CH], same[:, 1:CH + 1]

            def across(k, own, chain, edge, back):
                for j, c in enumerate((own, chain, edge)):
                    ch.step(nc.vector.tensor_scalar(carry[:, j, :], ident[:, :], c, None, ALU.mult))
                ch.done()
                v.sem_inc(diag_ready, 1)
                v.wait_ge(diag_sum, k + 1)
                ch.do(nc.vector.tensor_copy(carry[:, 0:3, :], pb[5][:, 0:3 * P].rearrange("p (j e) -> p j e", e=P)))
                o, c, d, w, r = (carry[:, j, :] for j in range(5))
                ch.do(nc.vector.memset(r, -BIG))
                if back:
                    ch.do(nc.vector.tensor_tensor_scan(w[:, ::-1], c[:, ::-1], o[:, ::-1], -BIG, ALU.add, ALU.max))
                    ch.do(nc.vector.tensor_tensor(r[:, 0:P - 1], w[:, 1:P], d[:, 0:P - 1], ALU.add))
                else:
                    ch.do(nc.vector.tensor_tensor_scan(w, c, o, -BIG, ALU.add, ALU.max))
                    ch.do(nc.vector.tensor_tensor(r[:, 1:P], w[:, 0:P - 1], d[:, 1:P], ALU.add))
                ch.do(nc.vector.tensor_tensor(r, r, ident[:, :], ALU.mult))
                ch.do(nc.vector.reduce_sum(col(4 + k), r, mybir.AxisListType.X))
                ch.do(nc.vector.tensor_scalar(col(4 + k), col(4 + k), -BIG, None, ALU.max))

            ch.do(nc.vector.tensor_tensor_scan(pre, fwd_neg, score, -BIG, ALU.add, ALU.max))
            across(0, pre[:, CH - 1:CH], col(0), same[:, 0:1], False)
            ch.do(nc.vector.tensor_tensor_scan(pre, fwd_neg, score, col(4), ALU.add, ALU.max))
            ch.do(nc.vector.tensor_tensor_scan(tmp[:, ::-1], bwd_neg[:, ::-1], pre[:, ::-1], -BIG, ALU.add, ALU.max))
            across(1, tmp[:, 0:1], col(1), same[:, CH:CH + 1], True)
            ch.do(nc.vector.tensor_tensor_scan(tmp[:, ::-1], bwd_neg[:, ::-1], pre[:, ::-1], col(5), ALU.add, ALU.max))
            W4 = CH // 4
            for k in range(4):
                c = slice(k * W4, (k + 1) * W4)
                nc.vector.tensor_tensor(score[:, c], score[:, c], tmp[:, c], ALU.subtract).then_inc(shifted, 1)
            for i in range(TA):
                u = i % 2
                v.wait_ge(etT_ready.sem, i + 1)
                w = 512 if i < TA - 1 else P * len(groups(i))
                nc.vector.tensor_copy(E_all[:, i * 64:i * 64 + w // H, :].rearrange("p t h -> p (t h)"),
                                      pb[6 + u][:, 0:w]).then_inc(etT_out.sem, 1)
            v.wait_ge(etT_out.sem, TA)
            v.wait_ge(x_cols_in, 2 * 16 * NX)
            ch.do(nc.vector.scalar_tensor_tensor(dst_f[:, :], nt_f[:, :], -float(P), dst_f[:, :], ALU.mult, ALU.add))
            ch.do(nc.vector.tensor_tensor(dst_f[:, ET:VT], dst_f[:, ET:VT], L["never"][:, :], ALU.subtract))
            v.wait_ge(acc_zero, 1)

            def add(i, q):
                nt4 = v.value_load(L["nt_pack"][0:1, bass.ds(i * RP + q, 1)], min_val=0, max_val=NT ** 4 - 1)
                summed.wait(v, i, q + 1)
                for e in range(PR):
                    c = q * PR + e
                    nt = v.snap(nt4 % NT)
                    if e < PR - 1:
                        nt4 = v.snap(nt4 // NT)
                    if c:
                        added.wait(v, i, c)
                    else:
                        added.wait_before(v, i, RP * PR)
                    a = acc[:, bass.ds(nt, 1), :]
                    nc.vector.tensor_tensor(a, a, pb[PR * (q % 2) + e][:, 0:TAB].rearrange("p (o d) -> p o d", o=1),
                                            ALU.add).then_inc(added.sem, 1)

            def second(i):
                for q in range(RP):
                    u, t = q % 2, bass.ds((i * RP + q) * PR, PR)
                    row_in[q].wait(v, i, PR)
                    if q >= 2:
                        summed.wait(v, i, q - 1)
                    else:
                        summed.wait_before(v, i, q + RP - 1)
                    nc.vector.tensor_tensor(S[:, u, :, :], iota_f[:, :].unsqueeze(1).to_broadcast([P, PR, P]),
                                            dst_f[:, t].unsqueeze(2).to_broadcast([P, PR, P]), ALU.is_equal)
                    nc.vector.tensor_tensor(msg[:, u, :, :].rearrange("p e (h r) -> p (e h) r", r=ROW),
                                            rows[:, q, :, :].rearrange("p e (h r) -> p (e h) r", r=ROW),
                                            E_all[:, t, :].rearrange("p t h -> p (t h)").unsqueeze(2)
                                            .to_broadcast([P, PR * H, ROW]), ALU.mult).then_inc(msg_ready.sem, 1)
                    if q:
                        add(i, q - 1)
                    elif not (isinstance(i, int) and i == 0):
                        add(i - 1, RP - 1)
            second(0)
            with v.Fori(1, XB) as i:
                second(i)
            v.wait_ge(e_extra, 16 * NX)
            with v.Fori(XB, TB) as i:
                second(i)
            add(TB - 1, RP - 1)

        @block.scalar
        def _(s):
            def extra_dst():
                for n in range(NX):
                    t = s.value_load(tau_i[0:1, n:n + 1], min_val=0, max_val=ET - 1)
                    s.dma_start(x_dst[n // EG][:, (n % EG) * P:(n % EG + 1) * P],
                                A["dst_flat"][:, bass.ds(t * P, P)].to_broadcast([P, P])).then_inc(x_dst_in[n // EG], 16)
                s.wait_ge(x_built, 1)
                s.dma_start(dstb, A["dst_flat"][:, 0:EG * P].to_broadcast([P, EG * P])).then_inc(dst_in.sem, 16)
            MIX.act_start(s, extra_dst)
            MIX.first(MIX.act, s)
            s.wait_ge(st_built.sem, 1)
            s.dma_start(dstb, A["dst_flat"][:, EG * P:2 * EG * P].to_broadcast([P, EG * P])).then_inc(dst_in.sem, 16)

            def body(i):
                for q in groups(i):
                    u, g = q % 2, 4 * i + q

                    def next_dst():
                        if not (isinstance(g, int) and g == NG - 1):
                            st_built.wait(s, i, q + 2)
                            s.dma_start(dstb, A["dst_flat"][:, bass.ds((g + 2) * EG * P, EG * P)]
                                        .to_broadcast([P, EG * P])).then_inc(dst_in.sem, 16)
                    MIX.slot(MIX.act, s, i, q, next_dst)
                    scT_ready.wait(s, i, q + 1)
                    if q < 2:
                        sat_stored[u].wait_before(s, i, 2)
                    else:
                        sat_stored[u].wait(s, i, 1)
                    nc.scalar.activation(satb[:, u, :], pb[7][:, u * P:(u + 1) * P], ACT.Copy).then_inc(scT_out.sem, 1)
                    scT_out.wait(s, i, q + 1)
                    s.dma_start(sat_d[:, bass.ds(g * EG, EG), :].rearrange("h t e -> t h e"),
                                satb[:, u, :]).then_inc(sat_stored[u].sem, 16)
            all_turns(s, body)
            s.dma_start(sat_d[:, ET:VT, :], A["zeros"]).then_inc(sat_stored[1].sem, 16)
            MIX.rest(MIX.act, s, TA - 1, groups(TA - 1))
            s.wait_ge(MIX.fx_stored.sem, 16 * NB)
            s.wait_ge(MIX.fx_sq.sem, 4 * NB)
            s.sem_inc(mixed, 1)
            for k in range(4):
                W4 = CH // 4
                s.wait_ge(shifted, k + 1)
                nc.scalar.activation(score[:, k * W4:(k + 1) * W4], score[:, k * W4:(k + 1) * W4], ACT.Exp)\
                    .then_inc(weighed, 1)
            s.wait_ge(et_out, 256)
            weight_rows(s, 1)
            s.wait_ge(etT_out.sem, TA)
            for n in range(NX):
                t = s.value_load(tau_i[0:1, n:n + 1], min_val=0, max_val=ET - 1)
                s.dma_start(E_all[:, ET + n:ET + n + 1, :], E_all[:, bass.ds(t, 1), :]).then_inc(e_extra, 16)

        @block.tensor
        def _(pe):
            def extra_rows():
                for j in range(3):
                    pe.wait_ge(x_built, j + 1)
                    if j:
                        pe.wait_ge(x_used, j)
                    for e in range(EG):
                        ins = nc.tensor.matmul(pb[6][:, e * 3 * H:(e + 1) * 3 * H], st[:, e, :],
                                               L["sd_nodes"][:, j * EG + e + 1, :], start=True, stop=True)
                    ins.then_inc(x_sde, 1)
                pe.wait_ge(x_used, 3)
            MIX.pe_start(pe, extra_rows)
            MIX.first(MIX.pe, pe)

            def body(i):
                nts = []

                def node_tiles(q):
                    nts.clear()
                    for k in range(4):
                        t4 = pe.value_load(L["nt_pack"][0:1, bass.ds((4 * i + q) * 4 + k, 1)], min_val=0,
                                           max_val=NT ** 4 - 1)
                        for e in range(4):
                            nts.append(pe.snap(t4 % NT))
                            if e < 3:
                                t4 = pe.snap(t4 // NT)
                node_tiles(0)
                for q in groups(i):
                    u = q % 2
                    st_built.wait(pe, i, q + 1)
                    if q:
                        sde_used.wait(pe, i, q)
                    else:
                        sde_used.wait_before(pe, i, 4)
                    for e in range(EG):
                        ins = nc.tensor.matmul(pb[6][:, e * 3 * H:(e + 1) * 3 * H], st[:, e, :],
                                               L["sd_nodes"][:, bass.ds(nts[e], 1), :], start=True, stop=True)
                    ins.then_inc(sde_ready.sem, 1)
                    MIX.slot(MIX.pe, pe, i, q, (lambda: node_tiles(q + 1)) if q + 1 in groups(i) else (lambda: None))
                    score_ready.wait(pe, i, q + 1)
                    if q:
                        scT_out.wait(pe, i, q)
                    else:
                        scT_out.wait_before(pe, i, 4)
                    nc.tensor.transpose(pb[7][:, u * P:(u + 1) * P], edge_pre[:, u, :], ident[:, :])\
                        .then_inc(scT_ready.sem, 1)
            all_turns(pe, body)
            MIX.rest(MIX.pe, pe, TA - 1, groups(TA - 1))
            for k in range(2):
                pe.wait_ge(diag_ready, k + 1)
                for j in range(3):
                    ins = nc.tensor.matmul(pb[5][:, j * P:(j + 1) * P], ones[:, :], carry[:, j, :], start=True, stop=True)
                ins.then_inc(diag_sum, 1)
            for i in range(TA):
                u = i % 2
                pe.wait_ge(et_in[u].sem, 16 * (i // 2 + 1))
                if i > 1:
                    pe.wait_ge(etT_out.sem, i - 1)
                for k in groups(i):
                    ins = nc.tensor.transpose(pb[6 + u][:, k * P:(k + 1) * P], etb[:, u, k, :], ident[:, :])
                ins.then_inc(etT_ready.sem, 1)

            def second(i):
                for q in range(RP):
                    u = q % 2
                    msg_ready.wait(pe, i, q + 1)
                    if q >= 2:
                        added.wait(pe, i, (q - 1) * PR)
                    else:
                        added.wait_before(pe, i, (q + RP - 1) * PR)
                    for e in range(PR):
                        ins = nc.tensor.matmul(pb[PR * u + e][:, 0:TAB], S[:, u, e, :], msg[:, u, e, :], start=True,
                                               stop=True)
                    ins.then_inc(summed.sem, 1)
            turns(pe, TB, second)


T2 = NT + 1


def combine_and_ffn(nc, ctx, sem, L, out):
    A, pb, ident, ones, sc = L["A"], L["pb"], L["ident"], L["ones"], L["sc"]
    acc = L["r1"][:, 0:T2 * TAB].rearrange("p (t d) -> p t d", d=TAB)
    area = L["Area"](L["r2"])
    h1 = area.take(HC, 512)
    xT = area.take(KD, 512)
    tri = area.take(P)
    xs = area.take(BLK, D)
    y = L["r3"][:, 0:NTP * D].rearrange("p (t d) -> p t d", d=D)
    area = L["Area"](L["r4"])
    cmp = L["r4"][:, 0:15 * T2].rearrange("p (c t) -> p c t", c=15)
    xb = area.take(BLK, D)
    xf, fb, wk = area.take(BLK, D), area.take(BLK, D), area.take(BLK, D)
    digits = area.take(15)
    stats = area.take(BLK, 6)
    mom = area.take(5, BLK)
    area = L["Area"](L["E_all"][:, :, :].rearrange("p t h -> p (t h)"))
    w1 = area.take(KD, HF)
    w2 = area.take(HC, D)
    grow, brow, wrow, b2row = (area.take(D) for _ in range(4))
    b1 = area.take(HC)
    br = area.take(1)
    rec = area.take(T2, H)
    wts, key_hi, key_lo, sel, wsel, t0, t1 = (area.take(T2) for _ in range(7))
    ki, km = area.take(T2, dt=I32), area.take(T2, dt=I32)
    cand, cnt, tot = area.take(15), area.take(15), area.take(15)
    base, need = area.take(1), area.take(1)

    c = lambda name, per, by=1: Count(sem(name), per, by)
    w_in, row_in = sem("ffn_w_in"), sem("ffn_rows_in")
    dve3 = sem("dve3")
    tri_set = sem("tri_set")
    xn_in, xf_in = c("xn_in", 1, 16), c("xf_in", 2, 16)
    xb_used, xf_used = c("xb_used", 1), c("xf_used", 1)
    elu_min, elu_exp = c("elu_min", 1), c("elu_exp", 1)
    var, std = c("var", 2), c("std", 2)
    fx_root, fx_tanh, fx_n = sem("fx_root"), sem("fx_tanh"), sem("fx_n")
    xs_ready = c("xs_ready", 1)
    xT2_ready, xT2_out = c("xT2_ready", 2), c("xT2_out", 2)
    h_mm, h_gelu = c("h_mm", HC), c("h_gelu", HC)
    y_mm, y_out, y_biased = c("y_mm", BLK), c("y_out", BLK), c("y_biased", 1)
    counted, count_all = sem("counted"), sem("count_all")
    ties_ready, ties = sem("ties_ready"), sem("ties")
    final, out_stored = c("final", BLK), sem("out_stored")
    h_bank = (pb[2], pb[3], pb[6], pb[7])
    NFB = (T2 + BLK - 1) // BLK

    def last(i):
        return isinstance(i, int) and i == NFB - 1

    def tiles(i):
        return range(T2 - BLK * (NFB - 1)) if last(i) else range(BLK)

    def all_blocks(eng, body):
        body(0)
        with eng.Fori(1, NFB - 2) as i:
            body(i)
        body(NFB - 2)
        body(NFB - 1)

    with nc.Block() as block:
        @block.sync
        def _(sp):
            def loads(b):
                n = len(tiles(b))
                ts = bass.ds(BLK * b, n)
                xb_used.wait_before(sp, b, 1)
                sp.dma_start(xb[:, 0:n, :], L["xn_d"][ts, :, :].rearrange("t p d -> p t d")).then_inc(xn_in.sem, 16)
                xf_used.wait_before(sp, b, 1)
                sp.dma_start(xf[:, 0:n, :], A["x"].rearrange("(t p) d -> p t d", p=P)[:, ts, :]).then_inc(xf_in.sem, 16)
                sp.dma_start(fb[:, 0:n, :], L["fx_d"][ts, :, :].rearrange("t p d -> p t d")).then_inc(xf_in.sem, 16)
                if isinstance(b, int) and b == 0:
                    for dst, name, k in ((grow, "gamma", D), (brow, "beta", D), (wrow, "wr", D), (b2row, "b2", D), (br, "br", 1)):
                        sp.dma_start(dst, A[name].to_broadcast([P, k])).then_inc(row_in, 16)
                    sp.dma_start(w1, A["w1"].rearrange("(k p) n -> p k n", p=P)).then_inc(w_in, 16)
                    sp.dma_start(w2, A["w2"].rearrange("(k p) n -> p k n", p=P)).then_inc(w_in, 16)
                    sp.dma_start(b1, A["b1"]).then_inc(w_in, 16)
            all_blocks(sp, loads)

            def store(i):
                n = len(tiles(i))
                final.wait(sp, i, n)
                sp.dma_start(out.rearrange("(t p) d -> p t d", p=P)[:, bass.ds(BLK * i, n), :],
                             acc[:, bass.ds(BLK * i, n), 0:D]).then_inc(out_stored, 16)
            all_blocks(sp, store)
            sp.wait_ge(out_stored, 16 * NFB)

        @block.gpsimd
        def _(g):
            g.memset(tri, 1.0).then_inc(tri_set, 1)
            g.wait_ge(tri_set, 1)
            g.affine_select(out=tri, in_=tri, compare_op=ALU.is_gt, fill=0.0, base=0, pattern=[[1, P]],
                            channel_multiplier=-1).then_inc(tri_set, 1)
            g.wait_ge(row_in, 16 * 5)

            def bias(i):
                n = len(tiles(i))
                yt = y[:, bass.ds(BLK * i, n), :]
                y_out.wait(g, i, n)
                g.tensor_tensor(yt, yt, b2row.unsqueeze(1).to_broadcast([P, n, D]), ALU.add).then_inc(y_biased.sem, 1)
            bias(0)
            with g.Fori(1, NFB - 1) as i:
                bias(i)
            for k in range(9):
                g.wait_ge(counted, k + 1)
                g.partition_all_reduce(tot, cnt, P, bass.bass_isa.ReduceOp.add).then_inc(count_all, 1)
            bias(NFB - 1)

        @block.vector
        def _(v_):
            v = nc.vector
            ch = Chain(v_, dve3)
            n, f = sc[:, 5, :], sc[:, 6, :]
            v.wait_ge(fx_root, 1)
            v.tensor_scalar(n, n, MINN, None, ALU.max).then_inc(fx_n, 1)
            ch.do(v.tensor_scalar(rec, acc[:, :, HD::ROW], 1e-30, None, ALU.max))
            ch.do(v.reciprocal(rec, rec))
            v.wait_ge(fx_tanh, 1)
            ch.do(v.tensor_scalar(f, f, MAXN, None, ALU.min))
            ch.do(v.reciprocal(n, n))
            ch.do(v.tensor_tensor(f, f, n, ALU.mult))
            v_.wait_ge(row_in, 16 * 5)

            def moments(b, k):
                m = len(tiles(b))
                ch.step(v.memset(mom[:, 0, :], 0.0))
                for j in range(m):
                    ch.step(v.bn_stats(stats[:, j:j + 1, :], acc[:, bass.ds(BLK * b + j, 1), 0:D]))
                ch.done()
                row_moments(nc, ch, stats[:, 0:m, :], mom, m)
                v.tensor_scalar(mom[:, 3, 0:m], mom[:, 3, 0:m], 1e-5, None, ALU.add).then_inc(var.sem, 1)
                std.wait(v_, b, k)
                ch.do(v.reciprocal(mom[:, 3, 0:m], mom[:, 4, 0:m]))

            def normalise(b, dst):
                ins = None
                for j in tiles(b):
                    ins = v.tensor_scalar(dst[:, j, :], acc[:, bass.ds(BLK * b + j, 1), 0:D].rearrange("p o d -> p (o d)"),
                                          mom[:, 2, j:j + 1], mom[:, 3, j:j + 1], ALU.subtract, ALU.mult)
                    if dst is wk:
                        ch.step(ins)
                return ins

            def block_rows(b, per):
                ch.turn(b, per)
                m = len(tiles(b))
                ts = bass.ds(BLK * b, m)
                a, w, e = acc[:, ts, 0:D], wk[:, 0:m, :], xb[:, 0:m, :]
                ch.do(v.tensor_tensor(w.rearrange("p t (h d) -> p t h d", d=HD),
                                      acc[:, ts, :].rearrange("p t (h r) -> p t h r", r=ROW)[:, :, :, 0:HD],
                                      rec[:, ts, :].unsqueeze(3).to_broadcast([P, m, H, HD]), ALU.mult))
                xn_in.wait(v_, b, 1)
                ch.do(v.tensor_tensor(a, w, e, ALU.add))
                moments(b, 1)
                normalise(b, wk)
                ch.done()
                ch.do(v.tensor_tensor(w, w, grow.unsqueeze(1).to_broadcast([P, m, D]), ALU.mult))
                ch.do(v.tensor_tensor(w, w, brow.unsqueeze(1).to_broadcast([P, m, D]), ALU.add))
                v.tensor_scalar(e, w, 0.0, None, ALU.min).then_inc(elu_min.sem, 1)
                elu_exp.wait(v_, b, 1)
                v.scalar_tensor_tensor(w, w, 0.0, e, ALU.max, ALU.add).then_inc(xb_used.sem, 1)
                xb_used.wait(v_, b, 1)
                xf_in.wait(v_, b, 2)
                ch.do(v.scalar_tensor_tensor(w, w, -1.0, xf[:, 0:m, :], ALU.add, ALU.add))
                for j in tiles(b):
                    t = bass.ds(BLK * b + j, 1)
                    ins = v.scalar_tensor_tensor(acc[:, t, 0:D].rearrange("p o d -> p (o d)"), fb[:, j, :],
                                                 sc[:, 6, t], wk[:, j, :], ALU.mult, ALU.add)
                    if j < m - 1:
                        ch.step(ins)
                ins.then_inc(xf_used.sem, 1)
                ch.done()
                xf_used.wait(v_, b, 1)
                moments(b, 2)
                xT2_ready.wait_before(v_, b, 2)
                normalise(b, xs).then_inc(xs_ready.sem, 1)
                xs_ready.wait(v_, b, 1)
                x = xs[:, 0:m, :]
                ch.do(v.tensor_tensor(w, x, wrow.unsqueeze(1).to_broadcast([P, m, D]), ALU.mult))
                ch.do(v.reduce_sum(wts[:, ts], w, mybir.AxisListType.X))
                ch.do(v.tensor_tensor(a, a, x, ALU.add))
            ch.loop()
            block_rows(0, 0)
            per = ch.k
            with v_.Fori(1, NFB - 1) as i:
                block_rows(i, per)
                assert ch.k == per, (ch.k, per)
            block_rows(NFB - 1, per)
            ch.do(v.tensor_scalar(wts, wts, br, None, ALU.add))
            wbits = wts.bitcast(I32)
            ch.do(v.tensor_single_scalar(km, wbits, 31, op=ALU.arith_shift_right))
            ch.do(v.tensor_single_scalar(km, km, 0x7FFFFFFF, op=ALU.bitwise_and))
            ch.do(v.tensor_tensor(ki, wbits, km, ALU.bitwise_xor))
            ch.do(v.tensor_single_scalar(km, ki, 16, op=ALU.arith_shift_right))
            ch.do(v.tensor_copy(key_hi, km))
            ch.do(v.tensor_single_scalar(km, ki, 0xFFFF, op=ALU.bitwise_and))
            ch.do(v.tensor_copy(key_lo, km))
            ch.do(v.tensor_scalar(key_hi, key_hi, 32768.0, None, ALU.add))
            ch.do(v.memset(key_hi[:, NT:T2], -1.0))
            last = key_hi[:, NT - 1:NT]
            ch.do(v.tensor_scalar(t0[:, 0:1], L["pcol"][:, 0:1], float(N - (NT - 1) * P), None, ALU.is_lt))
            ch.do(v.tensor_scalar(last, last, 1.0, t0[:, 0:1], ALU.add, ALU.mult))
            ch.do(v.tensor_scalar(last, last, -1.0, None, ALU.add))
            ch.do(v.tensor_scalar(digits, L["iota_f"][:, 1:16], 1.0, None, ALU.mult))

            def count(k):
                ch.done()
                v_.sem_inc(counted, 1)
                v_.wait_ge(count_all, k + 1)

            def search(keys, half):
                ch.do(v.memset(base, 0.0))
                for r in range(4):
                    step = float(16 ** (3 - r))
                    ch.do(v.tensor_scalar(cand, digits, step, base, ALU.mult, ALU.add))
                    ch.do(v.tensor_tensor(cmp, keys.unsqueeze(1).to_broadcast([P, 15, T2]),
                                          cand.unsqueeze(2).to_broadcast([P, 15, T2]), ALU.is_ge))
                    ch.do(v.reduce_sum(cnt, cmp, mybir.AxisListType.X))
                    count(4 * half + r)
                    ch.do(v.tensor_scalar(cand, tot, float(KSEL), None, ALU.is_ge))
                    ch.do(v.reduce_sum(need, cand, mybir.AxisListType.X))
                    ch.do(v.scalar_tensor_tensor(base, need, step, base, ALU.mult, ALU.add))
            search(key_hi, 0)
            ch.step(v.tensor_scalar(t0, key_hi, base, None, ALU.is_equal))
            ch.do(v.tensor_scalar(t1, key_hi, base, 1.0e6, ALU.is_gt, ALU.mult))
            ch.do(v.tensor_scalar(key_lo, key_lo, 1.0, None, ALU.add))
            ch.do(v.tensor_tensor(key_lo, key_lo, t0, ALU.mult))
            ch.do(v.tensor_tensor(key_lo, key_lo, t1, ALU.add))
            ch.do(v.tensor_scalar(key_lo, key_lo, -1.0, None, ALU.add))
            search(key_lo, 1)
            ch.step(v.tensor_scalar(sel, key_lo, base, None, ALU.is_gt))
            ch.step(v.tensor_scalar(t0, key_lo, base, None, ALU.is_equal))
            ch.step(v.memset(cnt, 0.0))
            ch.done()
            ch.do(v.reduce_sum(cnt[:, 0:1], sel, mybir.AxisListType.X))
            count(8)
            ch.do(v.tensor_scalar(need, tot[:, 0:1], -1.0, float(KSEL), ALU.mult, ALU.add))
            v_.sem_inc(ties_ready, 1)
            v_.wait_ge(ties, 1)
            ch.do(v.tensor_copy(t1, pb[7][:, 0:T2]))
            ch.do(v.tensor_tensor_scan(key_hi, t1, t1, 0.0, ALU.add, ALU.max))
            ch.do(v.tensor_tensor(key_hi, key_hi, t1, ALU.subtract))
            ch.do(v.tensor_tensor(key_hi, key_hi, pb[6][:, 0:T2], ALU.add))
            ch.do(v.tensor_scalar(key_hi, key_hi, need, None, ALU.is_lt))
            ch.do(v.tensor_tensor(key_hi, key_hi, t0, ALU.mult))
            ch.do(v.tensor_tensor(sel, sel, key_hi, ALU.add))
            ch.do(v.tensor_tensor(wsel, sel, wts, ALU.mult))

            def last_sum(i):
                y_biased.wait(v_, i, 1)
                for j in tiles(i):
                    t = bass.ds(BLK * i + j, 1)
                    at = acc[:, t, 0:D].rearrange("p o d -> p (o d)")
                    v.scalar_tensor_tensor(at, y[:, t, :].rearrange("p o d -> p (o d)"), wsel[:, t], at, ALU.mult, ALU.add)\
                        .then_inc(final.sem, 1)
            all_blocks(v_, last_sum)

        @block.scalar
        def _(s):
            act = nc.scalar.activation
            act(sc[:, 5, :], sc[:, 9, :], ACT.Sqrt).then_inc(fx_root, 1)
            s.wait_ge(fx_n, 1)
            act(sc[:, 6, :], sc[:, 5, :], ACT.Tanh).then_inc(fx_tanh, 1)

            def root(b, k):
                m = len(tiles(b))
                var.wait(s, b, k)
                act(mom[:, 4, 0:m], mom[:, 3, 0:m], ACT.Sqrt).then_inc(std.sem, 1)

            def exp(b):
                e = xb[:, 0:len(tiles(b)), :]
                elu_min.wait(s, b, 1)
                act(e, e, ACT.Exp).then_inc(elu_exp.sem, 1)

            def transposed(b):
                m = len(tiles(b)) * P
                for k in range(KD):
                    xT2_ready.wait(s, b, k + 1)
                    act(xT[:, k, 0:m], pb[k][:, 0:m], ACT.Copy).then_inc(xT2_out.sem, 1)

            def ffn(i):
                w = P * len(tiles(i))
                y_mm.wait_before(s, i, BLK)
                for m in range(HC):
                    h_mm.wait(s, i, m + 1)
                    act(h1[:, m, 0:w], h_bank[m % 4][:, 0:w], ACT.Gelu_apprx_tanh, bias=b1[:, m:m + 1])\
                        .then_inc(h_gelu.sem, 1)
                    if m == 1 and not last(i):
                        root(i + 1, 1)
                    if m == 5 and not last(i):
                        exp(i + 1)
                for j in tiles(i):
                    y_mm.wait(s, i, j + 1)
                    act(y[:, bass.ds(BLK * i + j, 1), :].rearrange("p o d -> p (o d)"), pb[4 + j % 2][:, 0:D], ACT.Copy)\
                        .then_inc(y_out.sem, 1)
                    if j == 0 and not last(i):
                        root(i + 1, 2)
                    if j == 2:
                        transposed(i + 1)
            root(0, 1)
            exp(0)
            root(0, 2)
            s.wait_ge(w_in, 3 * 16)
            transposed(0)
            all_blocks(s, ffn)

        @block.tensor
        def _(pe):
            mm = nc.tensor.matmul
            pe.wait_ge(w_in, 3 * 16)

            def transposes(b):
                xs_ready.wait(pe, b, 1)
                for k in range(KD):
                    for j in tiles(b):
                        ins = nc.tensor.transpose(pb[k][:, j * P:(j + 1) * P], xs[:, j, k * P:(k + 1) * P], ident[:, :])
                    ins.then_inc(xT2_ready.sem, 1)

            def ffn(i):
                w = P * len(tiles(i))
                for m in range(HC):
                    xT2_out.wait(pe, i, 2)
                    if m >= 4:
                        h_gelu.wait(pe, i, m - 3)
                    else:
                        h_gelu.wait_before(pe, i, HC + m - 3)
                    for k in range(KD):
                        ins = mm(h_bank[m % 4][:, 0:w], w1[:, k, m * P:(m + 1) * P], xT[:, k, 0:w], start=k == 0, stop=k == 1)
                    ins.then_inc(h_mm.sem, 1)
                h_gelu.wait(pe, i, HC)
                for j in tiles(i):
                    if j == 2:
                        transposes(i + 1)
                    if j >= 2:
                        y_out.wait(pe, i, j - 1)
                    else:
                        y_out.wait_before(pe, i, BLK + j - 1)
                    for m in range(HC):
                        ins = mm(pb[4 + j % 2][:, 0:D], h1[:, m, j * P:(j + 1) * P], w2[:, m, :], start=m == 0,
                                 stop=m == HC - 1)
                    ins.then_inc(y_mm.sem, 1)
            transposes(0)
            all_blocks(pe, ffn)
            pe.wait_ge(tri_set, 2)
            pe.wait_ge(ties_ready, 1)
            mm(pb[6][:, 0:T2], tri, t0, start=True, stop=True)
            mm(pb[7][:, 0:T2], ones[:, :], t0, start=True, stop=True).then_inc(ties, 1)


def kernel(x, src, dst, L0_gnn_W, L0_gnn_a_src, L0_gnn_a_dst, L0_gnn_gamma, L0_gnn_beta, L0_mix_w_qkv,
           L0_mix_bn_gamma, L0_mix_bn_beta, L0_mix_w_dw, L0_mix_w_pw, L0_mix_w_res, L0_mix_b_res,
           L0_ffn_attention_mask, L0_ffn_wr, L0_ffn_br, L0_ffn_w1, L0_ffn_b1, L0_ffn_w2, L0_ffn_b2):
    import concourse.bacc as bacc
    from concourse.bass_utils import run_bass_kernel_spmd

    def arr(a):
        return np.ascontiguousarray(a)

    x_pad = np.zeros((NTP * P, D), np.float32)
    x_pad[:N] = x
    src_pad = np.zeros((VT + 2 * EG) * P, np.int32)
    src_pad[:E] = src
    dst_pad = np.full(VT * P + 2, PAD_DST, np.int32)
    dst_pad[0] = -1
    dst_pad[-1] = -2
    dst_pad[1:E + 1] = dst
    dst_main = dst_pad[1:-1]
    chunks = np.lib.stride_tricks.as_strided(dst_pad, (16, CH + 2), (CH * 4, 4))

    def by_role(w):
        return arr(np.asarray(w).reshape((8, 3, 32) + w.shape[1:]).swapaxes(0, 1).reshape((NQ,) + w.shape[1:]))

    pw = by_role(np.asarray(L0_mix_w_pw)[:, :, 0]).reshape(QC, 4, 32, 32)
    arrays = {
        "x": x_pad,
        "src_cols": arr(src_pad.reshape(-1, P).T),
        "dst_cols": arr(dst_main.reshape(VT, P).T),
        "dst_flat": arr(dst_main.reshape(1, VT * P)),
        "dst_chunks": arr(chunks),
        "first": arr(dst_main.reshape(VT, P)[:ET, 0].reshape(1, ET)),
        "W": arr(L0_gnn_W),
        "a_src": arr(L0_gnn_a_src).reshape(1, D),
        "a_dst": arr(L0_gnn_a_dst).reshape(1, D),
        "gamma": arr(L0_gnn_gamma).reshape(1, D),
        "beta": arr(L0_gnn_beta).reshape(1, D),
        "w_qkv": arr(by_role(np.asarray(L0_mix_w_qkv)[:, :, 2]).T),
        "bn_gamma": arr(by_role(L0_mix_bn_gamma).reshape(QC, P).T),
        "bn_beta": arr(by_role(L0_mix_bn_beta).reshape(QC, P).T),
        "w_dw": arr(by_role(np.asarray(L0_mix_w_dw)[:, 0, 2]).reshape(QC, P).T),
        "w_pw": arr(pw.transpose(1, 3, 0, 2).reshape(P, QC, 32)),
        "w_res": arr(np.asarray(L0_mix_w_res)[:, :, 0].T),
        "b_res": arr(L0_mix_b_res).reshape(1, D),
        "wr": arr(L0_ffn_wr).reshape(1, D),
        "br": arr(L0_ffn_br).reshape(1, 1),
        "w1": arr(L0_ffn_w1),
        "b1": arr(np.asarray(L0_ffn_b1).reshape(HC, P).T),
        "w2": arr(L0_ffn_w2),
        "b2": arr(L0_ffn_b2).reshape(1, D),
        "zeros": np.zeros((H, VT - ET, P), np.float32),
    }
    nc = bacc.Bacc("TRN2", target_bir_lowering=False, num_devices=1)
    A = {}
    for name, a in arrays.items():
        A[name] = nc.dram_tensor(name, a.shape, mybir.dt.from_np(a.dtype), kind="ExternalInput").ap()
    out = nc.dram_tensor("out", [T2 * P, D], F32, kind="ExternalOutput").ap()
    build(nc, A, out)
    r = run_bass_kernel_spmd(nc, [arrays], core_ids=[0])
    return np.asarray(r.results[0]["out"])[:N]
```
